# Optimizing a Trainium2 kernel written in Bass

```python
import numpy as np
import jax
import jax.numpy as jnp

def _softmax(x, axis=-1):
    return jax.nn.softmax(x, axis=axis)

def _gelu(x):
    return jax.nn.gelu(x, approximate=True)

def _silu(x):
    return jax.nn.silu(x)

def _sigmoid(x):
    return jax.nn.sigmoid(x)

def _layernorm(x, axis=-1, eps=1e-05):
    m = jnp.mean(x, axis=axis, keepdims=True)
    v = jnp.var(x, axis=axis, keepdims=True)
    return (x - m) / jnp.sqrt(v + eps)

def _scatter_add(tgt, idx, src, axis=0):
    return tgt.at[idx].add(src)

def _segment_sum(src, seg, n):
    return jax.ops.segment_sum(src, seg, n)
kernel_name = 'mk_decoder_preln_d1_seqx_r4_b12534'

def setup_inputs(seed: int=0):
    np.random.seed(seed)
    _w = jnp.asarray

    def _rec_inputs():
        import jax
        import jax.numpy as jnp
        _rk = jax.random.key(seed)
        x = 4.136e-05 + 0.9999 * jax.random.normal(jax.random.fold_in(_rk, 1), (16, 256, 256), jnp.float32)
        _lenS = 256 - jax.random.randint(jax.random.fold_in(_rk, 7), (16,), 0, max(1, 256 // 4) + 1, jnp.int32)
        _lenS2 = 256 - jax.random.randint(jax.random.fold_in(_rk, 8), (16,), 0, max(1, 256 // 4) + 1, jnp.int32)
        _ctx_2048P = jax.random.normal(jax.random.fold_in(_rk, 11), (16, 16, 512), jnp.float32)
        _ctx_2048c = jax.random.dirichlet(jax.random.fold_in(_rk, 511), 0.3 * jnp.ones((16,), jnp.float32), (16, 256))
        _ctx_2048t = jnp.einsum('bsk,bkd->bsd', _ctx_2048c, _ctx_2048P)
        _ctx_2048t = _ctx_2048t * jax.lax.rsqrt(jnp.mean(jnp.square(_ctx_2048t)) + 1e-12) * 0.953939
        ctx_2048 = -0.000392918 + 0.999932 * (_ctx_2048t + 0.3 * jax.random.normal(jax.random.fold_in(_rk, 611), (16, 256, 512), jnp.float32))
        itok_Bx1_68_817 = jax.random.randint(jax.random.fold_in(_rk, 12), (16, 1), 68, 818, jnp.int32)
        return (x, ctx_2048, itok_Bx1_68_817)
    x, ctx_2048, itok_Bx1_68_817 = _rec_inputs()

    def _L0_attn_setup():
        import jax, jax.numpy as jnp
        import numpy as np
        B, N, C = (32, 128, 256)
        H = 16
        D = C // H
        MAX_SEQ = 128
        BASE = 10000.0

        def _rope_tables(n, d):
            position = jnp.arange(n, dtype=jnp.float32)[:, None]
            div_term = jnp.exp(jnp.arange(0, d, 2, dtype=jnp.float32) * (-np.log(BASE) / d))
            ang = position * div_term
            return (jnp.sin(ang), jnp.cos(ang))

        def _apply_rope(x, sin, cos):
            x1 = x[..., ::2]
            x2 = x[..., 1::2]
            out = jnp.stack([x1 * cos - x2 * sin, x1 * sin + x2 * cos], axis=-1)
            return out.reshape(*x.shape[:-1], -1)
        key = jax.random.key(seed)
        k1, k2, k3, k4, k5 = jax.random.split(key, 5)
        s = 0.02
        return {'x': jax.random.normal(k1, (B, N, C), dtype=jnp.float32), 'w_qkv': jax.random.normal(k2, (3 * C, C), dtype=jnp.float32) * s, 'b_qkv': jax.random.normal(k3, (3 * C,), dtype=jnp.float32) * s, 'w_lepe': jax.random.normal(k4, (C, 1, 3), dtype=jnp.float32) * s, 'b_lepe': jax.random.normal(k5, (C,), dtype=jnp.float32) * s}
    _L0_attn_all = _L0_attn_setup()
    _L0_attn_in = {k: v for k, v in _L0_attn_all.items() if k in ('w_qkv', 'b_qkv', 'w_lepe', 'b_lepe')}
    del _L0_attn_all

    def _L0_xattn_setup():
        import jax, jax.numpy as jnp
        import numpy as np
        UNITS = 256
        NUM_HEADS = 16
        MASK_VALUE = -1000000000000.0

        def _split_heads(x, n):
            B, S, D = x.shape
            return x.reshape(B, S, n, D // n).transpose(0, 2, 1, 3)
        key = jax.random.key(seed)
        k1, k2, k3, k4 = jax.random.split(key, 4)
        B, S = (8, 256)
        memory = jax.random.normal(k1, (B, S, 2 * UNITS), dtype=jnp.float32)
        query = jax.random.normal(k2, (B, S, UNITS), dtype=jnp.float32)
        b = jax.random.normal(k3, (S,), dtype=jnp.float32)
        seq_len = jax.random.randint(k4, (B, 1), 0, S, dtype=jnp.int32)
        return {'memory': memory, 'query': query, 'b': b, 'seq_len': seq_len}
    _L0_xattn_all = _L0_xattn_setup()
    _L0_xattn_in = {k: v for k, v in _L0_xattn_all.items() if k in ('b',)}
    del _L0_xattn_all

    def _L0_ffn_setup():
        import jax, jax.numpy as jnp
        import numpy as np
        TOPK = 8
        NUM_EXPERTS = 64
        FFN = 768
        CAPACITY = 160

        def _swiglu(x, w1, w2):
            h = x @ w1.T
            x1, x2 = jnp.split(h, 2, axis=-1)
            return x1 * jax.nn.silu(x2) @ w2.T
        key = jax.random.key(seed)
        ks = jax.random.split(key, 6)
        B, S, H = (1, 128, 256)
        scale = 0.02
        return {'hidden_states': jax.random.normal(ks[0], (B, S, H), jnp.float32), 'wg': jax.random.normal(ks[1], (NUM_EXPERTS, H), jnp.float32) * scale, 'shared_w1': jax.random.normal(ks[2], (2 * FFN, H), jnp.float32) * scale, 'shared_w2': jax.random.normal(ks[3], (H, FFN), jnp.float32) * scale, 'expert_w1': jax.random.normal(ks[4], (NUM_EXPERTS, 2 * FFN, H), jnp.float32) * scale, 'expert_w2': jax.random.normal(ks[5], (NUM_EXPERTS, H, FFN), jnp.float32) * scale}
    _L0_ffn_all = _L0_ffn_setup()
    _L0_ffn_in = {k: v for k, v in _L0_ffn_all.items() if k in ('wg', 'shared_w1', 'shared_w2', 'expert_w1', 'expert_w2')}
    del _L0_ffn_all
    return {'x': x, 'ctx_2048': ctx_2048, 'itok_Bx1_68_817': itok_Bx1_68_817, 'L0_attn_w_qkv': _L0_attn_in['w_qkv'], 'L0_attn_b_qkv': _L0_attn_in['b_qkv'], 'L0_attn_w_lepe': _L0_attn_in['w_lepe'], 'L0_attn_b_lepe': _L0_attn_in['b_lepe'], 'L0_xattn_b': _L0_xattn_in['b'], 'L0_ffn_wg': _L0_ffn_in['wg'], 'L0_ffn_shared_w1': _L0_ffn_in['shared_w1'], 'L0_ffn_shared_w2': _L0_ffn_in['shared_w2'], 'L0_ffn_expert_w1': _L0_ffn_in['expert_w1'], 'L0_ffn_expert_w2': _L0_ffn_in['expert_w2']}

def reference(x, ctx_2048, itok_Bx1_68_817, L0_attn_w_qkv, L0_attn_b_qkv, L0_attn_w_lepe, L0_attn_b_lepe, L0_xattn_b, L0_ffn_wg, L0_ffn_shared_w1, L0_ffn_shared_w2, L0_ffn_expert_w1, L0_ffn_expert_w2):
    import jax
    import jax.numpy as jnp

    def _L0_attn_ref(x, w_qkv, b_qkv, w_lepe, b_lepe):
        import jax, jax.numpy as jnp
        import numpy as np
        B, N, C = (32, 128, 256)
        H = 16
        D = C // H
        MAX_SEQ = 128
        BASE = 10000.0

        def _rope_tables(n, d):
            position = jnp.arange(n, dtype=jnp.float32)[:, None]
            div_term = jnp.exp(jnp.arange(0, d, 2, dtype=jnp.float32) * (-np.log(BASE) / d))
            ang = position * div_term
            return (jnp.sin(ang), jnp.cos(ang))

        def _apply_rope(x, sin, cos):
            x1 = x[..., ::2]
            x2 = x[..., 1::2]
            out = jnp.stack([x1 * cos - x2 * sin, x1 * sin + x2 * cos], axis=-1)
            return out.reshape(*x.shape[:-1], -1)
        b, n, c = x.shape
        scale = 1.0 / np.sqrt(D)
        sin, cos = _rope_tables(n, D)
        qkv = (x @ w_qkv.T + b_qkv).reshape(b, n, 3, H, D).transpose(2, 0, 3, 1, 4)
        q, k, v = (qkv[0], qkv[1], qkv[2])
        q = jax.nn.elu(q) + 1.0
        k = jax.nn.elu(k) + 1.0
        q = _apply_rope(q, sin, cos)
        k = _apply_rope(k, sin, cos)
        attn = jnp.einsum('bhnd,bhmd->bhnm', q, k) * scale
        attn = jax.nn.softmax(attn, axis=-1)
        attn_out = jnp.einsum('bhnm,bhmd->bhnd', attn, v)
        attn_out = attn_out.transpose(0, 2, 1, 3).reshape(b, n, c)
        v_conv = v.transpose(0, 2, 1, 3).reshape(b, n, c).transpose(0, 2, 1)
        lepe = jax.lax.conv_general_dilated(v_conv, w_lepe, window_strides=(1,), padding=((1, 1),), dimension_numbers=('NCH', 'OIH', 'NCH'), feature_group_count=c) + b_lepe[None, :, None]
        lepe = lepe.transpose(0, 2, 1)
        return attn_out + lepe

    def _L0_xattn_ref(memory, query, b, seq_len):
        import jax, jax.numpy as jnp
        import numpy as np
        UNITS = 256
        NUM_HEADS = 16
        MASK_VALUE = -1000000000000.0

        def _split_heads(x, n):
            B, S, D = x.shape
            return x.reshape(B, S, n, D // n).transpose(0, 2, 1, 3)
        B, S, _ = query.shape
        dh = UNITS // NUM_HEADS
        k_mem, v_mem = jnp.split(memory, 2, axis=2)
        Q = _split_heads(query, NUM_HEADS) * dh ** (-0.5)
        Kh = _split_heads(k_mem, NUM_HEADS)
        Vh = _split_heads(v_mem, NUM_HEADS)
        logits = jnp.einsum('bhqd,bhkd->bhqk', Q, Kh) + b
        valid = (jnp.arange(S)[None, :] < seq_len[:, 0:1]).astype(jnp.float32)
        logits = logits + MASK_VALUE * (1.0 - valid)[:, None, None, :]
        weights = jax.nn.softmax(logits, axis=-1)
        out = jnp.einsum('bhqk,bhkd->bhqd', weights, Vh)
        return out.transpose(0, 2, 1, 3).reshape(B, S, UNITS)

    def _L0_ffn_ref(hidden_states, wg, shared_w1, shared_w2, expert_w1, expert_w2):
        import jax, jax.numpy as jnp
        import numpy as np
        TOPK = 8
        NUM_EXPERTS = 64
        FFN = 768
        CAPACITY = 160

        def _swiglu(x, w1, w2):
            h = x @ w1.T
            x1, x2 = jnp.split(h, 2, axis=-1)
            return x1 * jax.nn.silu(x2) @ w2.T
        B, S, H = hidden_states.shape
        T = B * S
        x = hidden_states.reshape(T, H)
        shared_out = _swiglu(x, shared_w1, shared_w2)
        logits = x.astype(jnp.float32) @ wg.T
        gates = jax.nn.softmax(logits, axis=-1)
        w_topk, idx_topk = jax.lax.top_k(gates, TOPK)
        denom = jnp.maximum(w_topk.sum(-1, keepdims=True), jnp.finfo(jnp.float32).eps)
        w_topk = w_topk / denom
        A = T * TOPK
        flat_e = idx_topk.reshape(A)
        flat_w = w_topk.reshape(A)
        flat_t = jnp.repeat(jnp.arange(T), TOPK)
        order = jnp.argsort(flat_e)
        se, st, sw = (flat_e[order], flat_t[order], flat_w[order])
        counts = jnp.zeros(NUM_EXPERTS, jnp.int32).at[flat_e].add(1)
        starts = jnp.cumsum(counts) - counts
        rank = jnp.arange(A) - starts[se]
        valid = rank < CAPACITY
        buf = jnp.zeros((NUM_EXPERTS, CAPACITY, H), x.dtype).at[se, rank].set(x[st], mode='drop')
        h = jnp.einsum('ech,efh->ecf', buf, expert_w1)
        x1, x2 = jnp.split(h, 2, axis=-1)
        out = jnp.einsum('ecf,ehf->ech', x1 * jax.nn.silu(x2), expert_w2)
        y = out[se, jnp.clip(rank, 0, CAPACITY - 1)]
        y = jnp.where(valid[:, None], y * sw[:, None].astype(y.dtype), 0.0)
        combined = jnp.zeros((T, H), x.dtype).at[st].add(y)
        return (shared_out + combined).reshape(B, S, H)
    x = x + _L0_attn_ref(_layernorm(x, axis=-1), L0_attn_w_qkv, L0_attn_b_qkv, L0_attn_w_lepe, L0_attn_b_lepe)
    x = x + _L0_xattn_ref(ctx_2048, _layernorm(x, axis=-1), L0_xattn_b, itok_Bx1_68_817)
    x = x + _L0_ffn_ref(_layernorm(x, axis=-1), L0_ffn_wg, L0_ffn_shared_w1, L0_ffn_shared_w2, L0_ffn_expert_w1, L0_ffn_expert_w2)
    return x

_drawn_inputs = setup_inputs


def setup_inputs(seed=0):
    import zlib

    import numpy as np

    out = dict(_drawn_inputs(seed))
    spreads = {}
    factors = {'L0_attn_b_qkv': 2.844,
     'L0_attn_w_lepe': 5.658,
     'L0_attn_b_lepe': 3.224,
     'L0_ffn_wg': 8.0,
     'L0_ffn_expert_w1': 8.0,
     'L0_ffn_expert_w2': 8.0,
     'L0_ffn_shared_w1': 8.0,
     'L0_ffn_shared_w2': 8.0}
    for name, (base, spread) in spreads.items():
        noise = np.random.default_rng([zlib.crc32(name.encode()), seed]).standard_normal(out[name].shape)
        drawn = base * np.exp(spread * noise) if base else spread * noise
        out[name] = jnp.asarray(drawn.astype(out[name].dtype))
    for name, factor in factors.items():
        out[name] = (out[name] * factor).astype(out[name].dtype)
    return out
```

```python
from contextlib import ExitStack

import concourse.bass as bass
import numpy as np
from concourse import mybir

P = 128
B, N, C = 16, 256, 256
H = 16
D = C // H
T = N // P
K2 = C // P
TERMS = 6
DATA = TERMS * D
BIAS = DATA
TOP = DATA + 3
W = DATA + 6
G = 4
NG = H // G
VW = 32
RH = D // 2

E, TOPK, CAP, FF = 64, 8, 160, 768
FT = FF // P
HC = CAP // 2
SLOTS = E * CAP
ROW = C + E
NTOK = B * N
ROWS = NTOK + CAP
FAR = 16384.0
MASK = -1.0e12
EPS_LN = 1.0e-5
EPS = float(np.finfo(np.float32).eps)
CH = 512

F32, BF16, I32, U32 = mybir.dt.float32, mybir.dt.bfloat16, mybir.dt.int32, mybir.dt.uint32
ALU = mybir.AluOpType
ACT = mybir.ActivationFunctionType
AX = mybir.AxisListType.X

Q_HI, Q_MID, Q_LO = (0, 6, 2), (1, 5, 2), (5, 6, 1)
K_HI, K_MID, K_LO = (3, 6, 1), (0, 2, 1), (2, 3, 1)


def reach(eng, sem, value):
    if isinstance(value, int) and value <= 0:
        return
    eng.wait_ge(sem, value)


class Steps:

    def __init__(self, sem, names):
        self.sem, self.names = sem, names.split()

    def done(self, name, b):
        return b * len(self.names) + self.names.index(name) + 1

    def wait(self, eng, name, b):
        reach(eng, self.sem, self.done(name, b))


def decoder_layer(nc, x, ctx_in, itok, w_qkv, b_qkv, w_lepe, b_lepe, xb, wg, sw1, sw2, ew, cos_t,
                  sin_t, y):
    v, a, pl, pe, sp = nc.vector, nc.scalar, nc.gpsimd, nc.tensor, nc.sync
    slot_tok = nc.dram_tensor("slot_tok", (SLOTS, 1), I32, kind="Internal").ap()
    rows = nc.dram_tensor("rows", (ROWS, ROW), F32, kind="Internal").ap()
    xt_dram = nc.dram_tensor("xt_dram", (P, K2, NTOK), F32, kind="Internal").ap()

    stack = ExitStack()
    with stack:
        def sb(name, shape, dt=F32, scope=stack):
            return scope.enter_context(nc.sbuf_tensor(name, shape, dt))

        def sem(name):
            return stack.enter_context(nc.semaphore(name))

        bank = [stack.enter_context(nc.psum_tensor(f"bank{i}", [P, 512], F32)) for i in range(8)]

        X = sb("X", [P, B * T * C])
        ident = sb("ident", [P, P])
        identb = sb("identb", [P, P], BF16)
        ew_sb = [sb(f"ew{i}", [P, 2 * K2 * FF + FT * C]) for i in range(2)]
        loaded_ew = [sem(f"loaded_ew{i}") for i in range(2)]

        def xrow(b):
            return X[:, bass.ds(b * (T * C), T * C)]

        attn = ExitStack()
        asb = lambda name, shape, dt=F32: sb(name, shape, dt, attn)
        wq_sb = asb("wq_sb", [P, K2, 3 * C])
        wg_sb = asb("wg_sb", [P, K2, E])
        bq_sb = asb("bq_sb", [P, 3 * C])
        cos_sb = asb("cos_sb", [P, T, RH])
        sin_sb = asb("sin_sb", [P, T, RH])
        wl_sb = asb("wl_sb", [P, K2, 3])
        bl_sb = asb("bl_sb", [P, K2])
        xb_sb = asb("xb_sb", [P, T])
        seq_i = asb("seq_i", [P, B], I32)
        seq_f = asb("seq_f", [P, B])
        pos_i = asb("pos_i", [P, T], I32)
        pos_f = asb("pos_f", [P, T])
        minus1 = asb("minus1", [P, 1])
        mhalf = asb("mhalf", [P, T])
        bm = asb("bm", [P, B, T])
        bmr = asb("bmr", [P, B, T])
        bms = asb("bms", [P, B, T, 3], BF16)
        lower = asb("lower", [P, P], BF16)
        onesb = asb("onesb", [P, P], BF16)
        onesf = asb("onesf", [P, P])
        init_i = asb("init_i", [E, CAP], I32)
        zrow = asb("zrow", [HC, 2, ROW])
        ebase = asb("ebase", [P, E])
        ebase_i = asb("ebase_i", [P, E], I32)
        tok_f = asb("tok_f", [P, T])
        tok_i = asb("tok_i", [P, T], I32)
        before = asb("before", [P, E], BF16)

        ks = [asb(f"ks{i}", [P, T, H, W], BF16) for i in range(2)]
        qs = [asb(f"qs{i}", [P, T, H, W], BF16) for i in range(2)]
        va = [asb(f"va{i}", [P, T, H, VW]) for i in range(2)]
        kT = asb("kT", [W, H, N], BF16)
        qT = asb("qT", [TOP, H, N], BF16)
        q2 = [asb(f"q2_{i}", [W, 2 * N], BF16) for i in range(2)]
        ex = asb("ex", [P, 2 * G, T * N])
        oT = [asb(f"oT{i}", [P, N]) for i in range(2)]
        nm = asb("nm", [P, T, H])
        nmr = asb("nmr", [P, T, H])
        rden = asb("rden", [P, T * G])
        otmp = asb("otmp", [P, T, G * D])

        stats = asb("stats", [P, T, 6])
        mv = asb("mv", [P, T, 2])
        rstd = asb("rstd", [P, T])
        veps = asb("veps", [P, T])
        xn = asb("xn", [P, T, C])
        xnT = asb("xnT", [P, K2, N])
        z = asb("z", [P, T, 2 * C])
        ez = asb("ez", [P, T, 2 * C])
        rc = asb("rc", [P, 2 * H, 2, RH])
        rs = asb("rs", [P, 2 * H, 2, RH])
        r = asb("r", [P, 2 * H, D])
        rem = asb("rem", [P, H, D])
        lep = asb("lep", [P, K2, N])
        vtok = asb("vtok", [P, T, C])
        vTs = asb("vTs", [P, K2, N])

        cx = [asb(f"cx{i}", [P, T, 2 * C]) for i in range(2)]
        row = [asb(f"row{i}", [P, T, ROW]) for i in range(2)]
        stats3 = asb("stats3", [P, T, 6])
        mv3 = asb("mv3", [P, T, 2])
        rstd3 = asb("rstd3", [P, T])
        veps3 = asb("veps3", [P, T])
        x3T = [asb(f"x3T{i}", [P, K2, N]) for i in range(2)]
        nml = asb("nml", [P, T])
        eg = asb("eg", [P, T, E])
        esum = asb("esum", [P, T])
        ersum = asb("ersum", [P, T])
        gates = asb("gates", [P, T, E])
        top = asb("top", [P, T, TOPK])
        left = asb("left", [P, T, E])
        chosen = asb("chosen", [P, T, E], BF16)
        wsum = asb("wsum", [P, T])
        wsum2 = asb("wsum2", [P, T])
        wr = asb("wr", [P, T])
        vd = asb("vd", [P, T, E])
        sl = asb("sl", [P, T, E])
        val = asb("val", [P, T, E])
        topv = asb("topv", [P, T, TOPK])
        sidx = [asb(f"sidx{i}", [P, T, TOPK], U32) for i in range(2)]
        stok = [asb(f"stok{i}", [P, T], I32) for i in range(2)]

        in_w = sem("in_w")
        in_x = sem("in_x")
        init_st = sem("init_st")
        set_pool = sem("set_pool")
        set_dve = sem("set_dve")

        passed = {}

        def alone(eng):
            name = str(eng.engine).split(".")[-1]
            if name not in passed:
                passed[name] = sem(f"passed_{name}")
            eng.sem_inc(passed[name], 1)

        with nc.Block() as block:
            NW = 10

            @block.sync
            def _(eng):
                for dst, src in (
                    (wq_sb[:], w_qkv.rearrange("(k p) n -> p k n", p=P)),
                    (wg_sb[:], wg.rearrange("(k p) n -> p k n", p=P)),
                    (bq_sb[:], b_qkv.partition_broadcast(P)),
                    (cos_sb[:], cos_t.rearrange("(t p) n -> p t n", p=P)),
                    (sin_sb[:], sin_t.rearrange("(t p) n -> p t n", p=P)),
                    (wl_sb[:], w_lepe.rearrange("(k p) n -> p k n", p=P)),
                    (bl_sb[:], b_lepe),
                    (xb_sb[:], xb),
                    (seq_i[:], itok.rearrange("b o -> (b o)").partition_broadcast(P)),
                ):
                    eng.dma_start(dst, src).then_inc(in_w, 16)
                eng.dma_start(X[:].rearrange("p (b t c) -> p b t c", b=B, t=T),
                              x.rearrange("b (t p) c -> p b t c", p=P)).then_inc(in_x, 16)
                for i in range(2):
                    eng.dma_start(ew_sb[i][:], ew[i]).then_inc(loaded_ew[i], 16)
                eng.wait_ge(set_pool, 12)
                eng.dma_start(slot_tok.rearrange("(e s) o -> e (s o)", e=E), init_i[:]).then_inc(init_st, 16)
                eng.dma_start(rows[NTOK:ROWS, :].rearrange("(p a) n -> p a n", a=2), zrow[:]).then_inc(init_st, 16)
                eng.dma_start(y[NTOK:ROWS, :].rearrange("(p a) n -> p a n", a=2), zrow[:, :, 0:C]).then_inc(init_st, 16)
                eng.wait_ge(init_st, 48)
                eng.wait_ge(in_w, 16 * 9)
                eng.wait_ge(in_x, 16)

            @block.gpsimd
            def _(eng):
                pl.memset(ident[:], 0.0).then_inc(set_pool, 1)
                pl.memset(onesf[:], 1.0).then_inc(set_pool, 1)
                pl.memset(zrow[:], 0.0).then_inc(set_pool, 1)
                pl.memset(before[:], 0.0).then_inc(set_pool, 1)
                pl.memset(minus1[:], -1.0).then_inc(set_pool, 1)
                pl.memset(mhalf[:], -0.5).then_inc(set_pool, 1)
                eng.wait_ge(set_pool, 2)
                pl.affine_select(out=ident[:], in_=ident[:], compare_op=ALU.not_equal, fill=1.0, base=0,
                                 pattern=[[-1, P]], channel_multiplier=1).then_inc(set_pool, 1)
                pl.affine_select(out=onesf[:], in_=onesf[:], compare_op=ALU.is_gt, fill=0.0, base=0,
                                 pattern=[[1, P]], channel_multiplier=-1).then_inc(set_pool, 1)
                pl.iota(pos_i[:], pattern=[[P, T]], base=0, channel_multiplier=1).then_inc(set_pool, 1)
                pl.iota(init_i[:], pattern=[[1, CAP]], base=NTOK, channel_multiplier=0).then_inc(set_pool, 1)
                pl.iota(ebase_i[:], pattern=[[-CAP, E]], base=int(FAR), channel_multiplier=0)\
                    .then_inc(set_pool, 1)
                pl.memset(onesb[:], 1.0).then_inc(set_pool, 1)

            @block.vector
            def _(eng):
                def step(ins):
                    ins.then_inc(set_dve, 1)

                for i in range(2):
                    step(v.memset(qs[i][:, :, :, BIAS:BIAS + 3], 1.0))
                    step(v.memset(ks[i][:, :, :, BIAS:BIAS + 3], 0.0))
                    step(v.memset(ks[i][:, :, :, TOP:TOP + 3], 1.0))
                    step(v.memset(va[i][:], 0.0))
                eng.wait_ge(set_dve, 8)
                for i in range(2):
                    step(v.memset(va[i][:, :, :, D:D + 1], 1.0))
                eng.wait_ge(set_pool, 12)
                step(v.tensor_copy(identb[:], ident[:]))
                step(v.tensor_copy(lower[:], onesf[:]))
                step(v.tensor_copy(pos_f[:], pos_i[:]))
                step(v.tensor_copy(tok_f[:], pos_i[:]))
                step(v.tensor_copy(ebase[:], ebase_i[:]))
                eng.wait_ge(in_w, 16 * 9)
                step(v.tensor_scalar(bq_sb[:, 0:2 * C], bq_sb[:, 0:2 * C], 1.0, None, ALU.add))
                step(v.tensor_copy(seq_f[:], seq_i[:]))
                eng.wait_ge(set_dve, 17)
                for t in range(T):
                    step(v.tensor_scalar(bm[:, :, t], seq_f[:], pos_f[:, t:t + 1], None, ALU.is_gt))
                eng.wait_ge(set_dve, 19)
                for t in range(T):
                    step(v.tensor_scalar(bmr[:, :, t], bm[:, :, t], -MASK, MASK, ALU.mult, ALU.add))
                eng.wait_ge(set_dve, 21)
                for t in range(T):
                    step(v.tensor_scalar(bm[:, :, t], bmr[:, :, t], xb_sb[:, t:t + 1], 1.0 / D ** -0.5,
                                         ALU.add, ALU.mult))
                eng.wait_ge(set_dve, 23)
                step(v.tensor_copy(bms[:, :, :, 0], bm[:]))
                eng.wait_ge(set_dve, 24)
                step(v.tensor_tensor(bmr[:], bm[:], bms[:, :, :, 0], ALU.subtract))
                eng.wait_ge(set_dve, 25)
                step(v.tensor_copy(bms[:, :, :, 1], bmr[:]))
                eng.wait_ge(set_dve, 26)
                step(v.tensor_tensor(bms[:, :, :, 2], bmr[:], bms[:, :, :, 1], ALU.subtract))
                eng.wait_ge(set_dve, 27)

        def core_of(kind):
            s = {n: sem(f"{kind}_{n}") for n in (
                "kq_turned", "kq_copied", "scored", "max_found", "max_split", "split_chain", "q_turned", "q_copied",
                "rescored", "exp_done", "summed", "sum_copied", "sum_turned", "sum_used", "attn_added", "attn_chain")}
            XB, YB, ZB = bank[4], bank[5], bank[6]
            xb16, yb16 = XB[:].bitcast(BF16), YB[:].bitcast(BF16)

            def lagged(c, t, lag, every, size, last=False):
                d = t - lag
                if d % every:
                    return None
                u = d // every
                if u >= 0:
                    return (None if last else (c, u, 0))
                return (c - 1, u + size, 1)

            def pe_step(eng, c, par, t, ready, first=False, last=False):
                def unit(lag, every, size):
                    got = lagged(c, t, lag, every, size, last)
                    return None if got is None or (first and got[2]) else got

                if t % 2 == 0 and not last:
                    u, n = t // 4, t // 2 % 2
                    src, width = ((ks, W), (qs, TOP))[n]
                    if t == 0:
                        ready(eng, c)
                    reach(eng, s["kq_copied"], 8 * c + 2 * u + n)
                    for h in range(G):
                        for tt in range(T):
                            ins = pe.transpose(xb16[0:width, (h * T + tt) * P:(h * T + tt + 1) * P],
                                               src[par][:, tt, u * G + h, 0:width], identb[:])
                    ins.then_inc(s["kq_turned"], 1)
                if got := unit(4, 1, H):
                    cc, h, _ = got
                    reach(eng, s["kq_copied"], 8 * cc + 2 * (h // G) + 2)
                    reach(eng, s["max_found"], 16 * cc + h - 1)
                    for tt in range(T):
                        ins = pe.matmul(bank[h % 2][:, tt * N:(tt + 1) * N], qT[0:TOP, h, tt * P:(tt + 1) * P],
                                        kT[0:TOP, h, :], start=True, stop=True)
                    ins.then_inc(s["scored"], 1)
                if got := unit(8, 2, H // 2):
                    cc, p, back = got
                    src = qs[(par + back) % 2]
                    eng.wait_ge(s["max_split"], 8 * cc + p + 1)
                    reach(eng, s["q_copied"], 8 * cc + p)
                    for h in range(2):
                        for tt in range(T):
                            ins = pe.transpose(yb16[0:W, (h * T + tt) * P:(h * T + tt + 1) * P],
                                               src[:, tt, 2 * p + h, 0:W], identb[:])
                    ins.then_inc(s["q_turned"], 1)
                if got := unit(11, 1, H):
                    cc, h, _ = got
                    reach(eng, s["q_copied"], 8 * cc + h // 2 + 1)
                    reach(eng, s["exp_done"], 16 * cc + h - 1)
                    for tt in range(T):
                        ins = pe.matmul(bank[2 + h % 2][:, tt * N:(tt + 1) * N], kT[0:W, h, tt * P:(tt + 1) * P],
                                        q2[h // 2 % 2][0:W, (h % 2) * N:(h % 2 + 1) * N], start=True, stop=True)
                    ins.then_inc(s["rescored"], 1)
                if got := unit(16, 4, NG):
                    cc, g, back = got
                    vv = va[(par + back) % 2]
                    eng.wait_ge(s["exp_done"], 16 * cc + G * g + G)
                    reach(eng, s["sum_used"], 4 * cc + g)
                    for tt in range(T):
                        for j in range(G):
                            h = g * G + j
                            ins = pe.matmul(ZB[32 * j:32 * j + VW, 0:N], vv[:, tt, h, :],
                                            ex[:, h % (2 * G), tt * N:(tt + 1) * N],
                                            start=(tt == 0), stop=(tt == T - 1))
                    ins.then_inc(s["summed"], 1)
                if got := unit(18, 4, NG):
                    cc, g, _ = got
                    eng.wait_ge(s["sum_copied"], 4 * cc + g + 1)
                    for tt in range(T):
                        ins = pe.transpose(ZB[:, N + tt * P:N + (tt + 1) * P], oT[g % 2][:, tt * P:(tt + 1) * P],
                                           ident[:])
                    ins.then_inc(s["sum_turned"], 1)

            def act_step(eng, c, par, t, first=False, last=False):
                def unit(lag, every, size):
                    got = lagged(c, t, lag, every, size, last)
                    return None if got is None or (first and got[2]) else got

                if got := unit(11, 1, H):
                    cc, h, _ = got
                    eng.wait_ge(s["rescored"], 16 * cc + h + 1)
                    reach(eng, s["summed"], 4 * cc + h // G - 1)
                    a.activation(ex[:, h % (2 * G), :], bank[2 + h % 2][:], ACT.Exp, scale=float(D) ** -0.5)\
                        .then_inc(s["exp_done"], 1)
                if got := unit(17, 4, NG):
                    cc, g, _ = got
                    eng.wait_ge(s["summed"], 4 * cc + g + 1)
                    reach(eng, s["sum_turned"], 4 * cc + g - 1)
                    a.activation(oT[g % 2][:], ZB[:, 0:N], ACT.Copy).then_inc(s["sum_copied"], 1)
                if t % 2 == 0 and not last:
                    u, n = t // 4, t // 2 % 2
                    dst, width, read = ((kT, W, "rescored"), (qT, TOP, "scored"))[n]
                    eng.wait_ge(s["kq_turned"], 8 * c + 2 * u + n + 1)
                    reach(eng, s[read], 16 * (c - 1) + G * u + G)
                    a.activation(dst[0:width, u * G:(u + 1) * G, :],
                                 xb16[0:width, :].rearrange("p (h n) -> p h n", h=G), ACT.Copy)\
                        .then_inc(s["kq_copied"], 1)

            def dve_step(eng, c, par, t, first=False, last=False):
                def unit(lag, every, size):
                    got = lagged(c, t, lag, every, size, last)
                    return None if got is None or (first and got[2]) else got

                if got := unit(4, 1, H):
                    cc, h, _ = got
                    eng.wait_ge(s["scored"], 16 * cc + h + 1)
                    v.tensor_reduce(nm[:, :, h], bank[h % 2][:].rearrange("p (t n) -> p t n", t=T), AX, ALU.max,
                                    negate=True).then_inc(s["max_found"], 1)
                if got := unit(9, 2, H // 2):
                    cc, p, _ = got
                    eng.wait_ge(s["q_turned"], 8 * cc + p + 1)
                    reach(eng, s["rescored"], 16 * cc + 2 * p - 2)
                    v.tensor_copy(q2[p % 2][:], yb16[0:W, 0:2 * N]).then_inc(s["q_copied"], 1)
                if got := unit(19, 4, NG):
                    cc, g, _ = got
                    zo = ZB[:, N:2 * N].rearrange("p (u d) -> p u d", d=VW)
                    eng.wait_ge(s["sum_turned"], 4 * cc + g + 1)
                    v.reciprocal(rden[:], zo[:, :, D]).then_inc(s["attn_chain"], 1)
                    eng.wait_ge(s["attn_chain"], 4 * cc + g + 1)
                    reach(eng, s["attn_added"], 4 * cc + g)
                    v.tensor_tensor(otmp[:].rearrange("p t (j d) -> p (t j) d", d=D), zo[:, :, 0:D],
                                    rden[:].unsqueeze(2).to_broadcast([P, T * G, D]), ALU.mult)\
                        .then_inc(s["sum_used"], 1)
                    eng.wait_ge(s["sum_used"], 4 * cc + g + 1)
                    xg = xrow(cc).rearrange("p (t c) -> p t c", t=T)[:, :, g * G * D:(g + 1) * G * D]
                    v.tensor_tensor(xg, xg, otmp[:], ALU.add).then_inc(s["attn_added"], 1)

            def pool_step(eng, c, par, t, first=False, last=False):
                got = lagged(c, t, 6, 2, H // 2, last)
                if got is not None and not (first and got[2]):
                    cc, p, back = got
                    dst = qs[(par + back) % 2]
                    n2, m2 = nm[:, :, 2 * p:2 * p + 2], nmr[:, :, 2 * p:2 * p + 2]
                    part = [dst[:, :, 2 * p:2 * p + 2, TOP + i] for i in range(3)]
                    base = 24 * cc + 3 * p
                    eng.wait_ge(s["max_found"], 16 * cc + 2 * p + 2)
                    alone(eng)
                    pl.tensor_copy(part[0], n2).then_inc(s["split_chain"], 1)
                    eng.wait_ge(s["split_chain"], base + 1)
                    pl.tensor_tensor(m2, n2, part[0], ALU.subtract).then_inc(s["split_chain"], 1)
                    eng.wait_ge(s["split_chain"], base + 2)
                    alone(eng)
                    pl.tensor_copy(part[1], m2).then_inc(s["split_chain"], 1)
                    eng.wait_ge(s["split_chain"], base + 3)
                    pl.tensor_tensor(part[2], m2, part[1], ALU.subtract).then_inc(s["max_split"], 1)

            return s, pe_step, act_step, dve_step, pool_step

        def split(eng, steps, b, tag, src, dst, hi, mid, lo):
            view = dst.rearrange("p h (n d) -> p h n d", d=D)

            def at(terms):
                return view[:, :, terms[0]:terms[1]:terms[2], :]

            def copies(ap, terms):
                return ap.unsqueeze(2).to_broadcast([P, H, len(range(*terms)), D])

            alone(eng)
            pl.tensor_copy(at(hi), copies(src, hi)).then_inc(steps.sem, 1)
            steps.wait(eng, f"{tag}_hi", b)
            pl.tensor_tensor(rem[:], src, view[:, :, hi[0], :], ALU.subtract).then_inc(steps.sem, 1)
            steps.wait(eng, f"{tag}_rest", b)
            alone(eng)
            pl.tensor_copy(at(mid), copies(rem[:], mid)).then_inc(steps.sem, 1)
            steps.wait(eng, f"{tag}_mid", b)
            pl.tensor_tensor(view[:, :, lo[0], :], rem[:], view[:, :, mid[0], :], ALU.subtract)\
                .then_inc(steps.sem, 1)
            steps.wait(eng, f"{tag}_lo", b)
            alone(eng)

        def ln_stats(steps, eng, b, src, st, m, ve_):
            alone(eng)
            for tt in range(T):
                v.bn_stats(st[:, tt, :], src[tt]).then_inc(steps.sem, 1)
            for tt in range(T):
                steps.wait(eng, f"stats{tt}", b)
                alone(eng)
                v.bn_aggr(m[:, tt, :], st[:, tt, :]).then_inc(steps.sem, 1)
            steps.wait(eng, "aggr1", b)
            v.tensor_scalar(ve_[:], m[:, :, 1], EPS_LN, None, ALU.add).then_inc(steps.sem, 1)

        def ln_root(steps, eng, b, rooted, ve_, rs_):
            steps.wait(eng, "veps", b)
            pl.tensor_tensor(rs_[:], ve_[:], mhalf[:], ALU.pow).then_inc(rooted, 1)

        def ln_norm(steps, eng, b, rooted, src, m, rs_, dst):
            eng.wait_ge(rooted, b + 1)
            for tt in range(T):
                v.tensor_scalar(dst[tt], src[tt], m[:, tt, 0:1], rs_[:, tt:tt + 1], ALU.subtract, ALU.mult)\
                    .then_inc(steps.sem, 1)

        LN = "stats0 stats1 aggr0 aggr1 veps xn0 xn1"
        MB = bank[7]
        M_SELF, M_CROSS = 6, 3

        def turn4(dst, src):
            for i in range(2):
                for j in range(2):
                    ins = pe.transpose(dst(i, j), src(i, j), ident[:])
            return ins

        def rows_of(ap, tt):
            return ap.rearrange("p (t c) -> p t c", t=T)[:, tt, :]

        s, pe_core, act_core, dve_core, pool_core = core_of("self")
        m_full = sem("m_full")
        self_rooted = sem("self_rooted")
        SD = Steps(sem("self_dve"), f"{LN} z0 elu0 z1 elu1 v lep_mid0 lep_mid1 lep_before0 lep_before1 "
                                    "lep_after0 lep_after1 lep_added")
        SA = Steps(sem("self_act"), "xnT exp0 exp1 vT")
        SG = Steps(sem("self_pool"), " ".join(
            f"cos{t} sin{t} even{t} odd{t} " + " ".join(f"{o}{t}_{n}" for o in "kq" for n in ("hi", "rest", "mid", "lo"))
            for t in range(T)) + " values")

        def self_dve(eng, b, par, t, prev):
            xr = xrow(b)
            if t == 0:
                ln_stats(SD, eng, b, [rows_of(xr, tt) for tt in range(T)], stats, mv, veps)
            if t == 1:
                reach(eng, m_full, M_SELF * (b - 1) + 1)
                ln_norm(SD, eng, b, self_rooted, [rows_of(xr, tt) for tt in range(T)], mv, rstd,
                        [xn[:, tt, :] for tt in range(T)])
            for tt in range(T):
                if t == 5 + 2 * tt:
                    eng.wait_ge(m_full, M_SELF * b + 2 + tt)
                    if prev:
                        SG.wait(eng, f"sin{tt}", b - 1)
                    v.tensor_tensor(z[:, tt, :], MB[:], bq_sb[:, 0:2 * C], ALU.add).then_inc(SD.sem, 1)
                if t == 6 + 2 * tt:
                    SA.wait(eng, f"exp{tt}", b)
                    v.scalar_tensor_tensor(z[:, tt, :], ez[:, tt, :], 1.0, z[:, tt, :], ALU.min, ALU.max)\
                        .then_inc(SD.sem, 1)
            if t == 9:
                eng.wait_ge(m_full, M_SELF * b + 4)
                if prev:
                    SG.wait(eng, "values", b - 1)
                v.tensor_tensor(vtok[:], MB[:].rearrange("p (t c) -> p t c", t=T),
                                bq_sb[:, 2 * C:3 * C].unsqueeze(1).to_broadcast([P, T, C]), ALU.add)\
                    .then_inc(SD.sem, 1)
            if t == 12:
                SA.wait(eng, "vT", b)
                reach(eng, m_full, M_SELF * b)
                for k in range(K2):
                    v.tensor_scalar(lep[:, k, :], vTs[:, k, :], wl_sb[:, k, 1:2], bl_sb[:, k:k + 1],
                                    ALU.mult, ALU.add).then_inc(SD.sem, 1)
                for k in range(K2):
                    SD.wait(eng, f"lep_mid{k}", b)
                    v.scalar_tensor_tensor(lep[:, k, 1:N], vTs[:, k, 0:N - 1], wl_sb[:, k, 0:1],
                                           lep[:, k, 1:N], ALU.mult, ALU.add).then_inc(SD.sem, 1)
                for k in range(K2):
                    SD.wait(eng, f"lep_before{k}", b)
                    v.scalar_tensor_tensor(lep[:, k, 0:N - 1], vTs[:, k, 1:N], wl_sb[:, k, 2:3],
                                           lep[:, k, 0:N - 1], ALU.mult, ALU.add).then_inc(SD.sem, 1)
            if t == 14:
                eng.wait_ge(m_full, M_SELF * b + 6)
                v.tensor_tensor(xr, xr, MB[:], ALU.add).then_inc(SD.sem, 1)

        def self_act(eng, b, par, t, prev):
            if t == 3:
                eng.wait_ge(m_full, M_SELF * b + 1)
                reach(eng, m_full, M_SELF * (b - 1) + 4)
                a.activation(xnT[:].rearrange("p k n -> p (k n)"), MB[:], ACT.Copy).then_inc(SA.sem, 1)
            for tt in range(T):
                if t == 5 + 2 * tt:
                    SD.wait(eng, f"z{tt}", b)
                    a.activation(ez[:, tt, :], z[:, tt, :], ACT.Exp, bias=minus1[:]).then_inc(SA.sem, 1)
            if t == 11:
                eng.wait_ge(m_full, M_SELF * b + 5)
                if prev:
                    SD.wait(eng, "lep_after1", b - 1)
                a.activation(vTs[:].rearrange("p k n -> p (k n)"), MB[:], ACT.Copy).then_inc(SA.sem, 1)

        def self_pe(eng, b, par, t, prev):
            if t == 2:
                if prev:
                    SD.wait(eng, "lep_added", b - 1)
                SD.wait(eng, "xn1", b)
                turn4(lambda k, tt: MB[:, k * N + tt * P:k * N + (tt + 1) * P],
                      lambda k, tt: xn[:, tt, k * P:(k + 1) * P]).then_inc(m_full, 1)
            for tt in range(T):
                if t == 4 + 2 * tt:
                    SA.wait(eng, "xnT", b)
                    if tt:
                        SD.wait(eng, "z0", b)
                    for k in range(K2):
                        ins = pe.matmul(MB[:], xnT[:, k, tt * P:(tt + 1) * P], wq_sb[:, k, 0:2 * C],
                                        start=(k == 0), stop=(k == K2 - 1))
                    ins.then_inc(m_full, 1)
            if t == 8:
                SD.wait(eng, "z1", b)
                for tt in range(T):
                    for k in range(K2):
                        ins = pe.matmul(MB[:, tt * C:(tt + 1) * C], xnT[:, k, tt * P:(tt + 1) * P],
                                        wq_sb[:, k, 2 * C:3 * C], start=(k == 0), stop=(k == K2 - 1))
                ins.then_inc(m_full, 1)
            if t == 10:
                SD.wait(eng, "v", b)
                turn4(lambda k, tt: MB[:, k * N + tt * P:k * N + (tt + 1) * P],
                      lambda k, tt: vtok[:, tt, k * P:(k + 1) * P]).then_inc(m_full, 1)
            if t == 13:
                SD.wait(eng, "lep_after1", b)
                SA.wait(eng, "vT", b)
                turn4(lambda tt, k: MB[:, tt * C + k * P:tt * C + (k + 1) * P],
                      lambda tt, k: lep[:, k, tt * P:(tt + 1) * P]).then_inc(m_full, 1)

        def self_pool(eng, b, par, t, prev):
            if t == 0:
                ln_root(SD, eng, b, self_rooted, veps, rstd)
            for tt in range(T):
                if t == 7 + 3 * tt:
                    SD.wait(eng, f"elu{tt}", b)
                    pairs = z[:, tt, :].rearrange("p (h e two) -> p h two e", two=2, e=RH)
                    for tab, dst in ((cos_sb, rc), (sin_sb, rs)):
                        wide = tab[:, tt, :].unsqueeze(1).to_broadcast([P, 2 * H, RH])
                        for i in range(2):
                            ins = pl.tensor_tensor(dst[:, :, i, :], pairs[:, :, i, :], wide, ALU.mult)
                        ins.then_inc(SG.sem, 1)
                    SG.wait(eng, f"sin{tt}", b)
                    pl.tensor_tensor(r[:, :, 0:RH], rc[:, :, 0, :], rs[:, :, 1, :], ALU.subtract).then_inc(SG.sem, 1)
                    pl.tensor_tensor(r[:, :, RH:D], rs[:, :, 0, :], rc[:, :, 1, :], ALU.add).then_inc(SG.sem, 1)
                    SG.wait(eng, f"odd{tt}", b)
                if t == 8 + 3 * tt:
                    reach(eng, s["kq_turned"], 8 * (b - 1))
                    split(eng, SG, b, f"k{tt}", r[:, H:2 * H, :], ks[par][:, tt, :, 0:DATA], K_HI, K_MID, K_LO)
                if t == 9 + 3 * tt:
                    reach(eng, s["q_turned"], 8 * (b - 1))
                    split(eng, SG, b, f"q{tt}", r[:, 0:H, :], qs[par][:, tt, :, 0:DATA], Q_HI, Q_MID, Q_LO)
            if t == 14:
                reach(eng, s["summed"], NG * (b - 1))
                SD.wait(eng, "v", b)
                alone(eng)
                for tt in range(T):
                    ins = pl.tensor_copy(va[par][:, tt, :, 0:D], vtok[:, tt, :].rearrange("p (h d) -> p h d", d=D))
                ins.then_inc(SG.sem, 1)

        def sweep(eng, body, peeled, tails):
            for c in range(peeled):
                body(c, c % 2, c)
            with eng.Fori(peeled // 2, B // 2 - 1) as i:
                body(2 * i, 0, peeled)
                body(2 * i + 1, 1, peeled + 1)
            for c in range(B - 2, B + tails):
                body(c, c % 2, c)

        def run_self(eng, core, prep):
            for t in range(H):
                prep(eng, 0, 0, t, False)

            def body(c, par, n):
                for t in range(H):
                    core(c, par, t, n == 0, n >= B)
                    if n < B - 1:
                        prep(eng, c + 1, 1 - par, t, True)
            sweep(eng, body, 2, 1)

        with nc.Block() as block:
            @block.tensor
            def _(eng):
                run_self(eng, lambda c, par, t, first, last: pe_core(
                    eng, c, par, t, lambda e, cc: SG.wait(e, "values", cc), first, last), self_pe)

            @block.scalar
            def _(eng):
                run_self(eng, lambda c, par, t, first, last: act_core(eng, c, par, t, first, last), self_act)

            @block.vector
            def _(eng):
                run_self(eng, lambda c, par, t, first, last: dve_core(eng, c, par, t, first, last), self_dve)

            @block.gpsimd
            def _(eng):
                run_self(eng, lambda c, par, t, first, last: pool_core(eng, c, par, t, first, last), self_pool)

        s2, pe_core2, act_core2, dve_core2, pool_core2 = core_of("cross")
        m2_full = sem("m2_full")
        cross_rooted = sem("cross_rooted")
        route_rooted = sem("route_rooted")
        CD = Steps(sem("cross_dve"), LN)
        CG = Steps(sem("cross_pool"), " ".join(f"{o}{t}_{n}" for o in "kq" for t in range(T)
                                               for n in ("hi", "rest", "mid", "lo")) + " bias values")
        RD = Steps(sem("route_dve"), f"{LN} top_logit esum_inv gates top0 top1 left0 left1 chosen wsum wmax winv "
                                     "wpart weights before0 before1 fits slot val topv0 topv1 index token next")
        RA = Steps(sem("route_act"), "x3T exp0 exp1")
        in_ctx = [sem(f"in_ctx{i}") for i in range(2)]
        rows_st = [sem(f"rows_st{i}") for i in range(2)]
        x3t_st = [sem(f"x3t_st{i}") for i in range(2)]
        scattered = [sem(f"scattered{i}") for i in range(2)]

        def cross_dve(eng, b, par, t, prev):
            xr = xrow(b)
            if t == 0:
                ln_stats(CD, eng, b, [rows_of(xr, tt) for tt in range(T)], stats, mv, veps)
            if t == 1:
                if prev:
                    CG.wait(eng, "q1_rest", b - 1)
                ln_norm(CD, eng, b, cross_rooted, [rows_of(xr, tt) for tt in range(T)], mv, rstd,
                        [xn[:, tt, :] for tt in range(T)])

        def cross_pool(eng, b, par, t, prev):
            if t == 0:
                ln_root(CD, eng, b, cross_rooted, veps, rstd)
            for tt in range(T):
                if t == 1 + 2 * tt:
                    if tt == 0:
                        eng.wait_ge(in_ctx[par], ctx_count(b, par))
                    reach(eng, s2["kq_turned"], 8 * (b - 1))
                    split(eng, CG, b, f"k{tt}", cx[par][:, tt, 0:C].rearrange("p (h d) -> p h d", d=D),
                          ks[par][:, tt, :, 0:DATA], K_HI, K_MID, K_LO)
                if t == 7 + 2 * tt:
                    CD.wait(eng, "xn1", b)
                    reach(eng, s2["q_turned"], 8 * (b - 1))
                    split(eng, CG, b, f"q{tt}", xn[:, tt, :].rearrange("p (h d) -> p h d", d=D),
                          qs[par][:, tt, :, 0:DATA], Q_HI, Q_MID, Q_LO)
            if t == 11:
                for tt in range(T):
                    src = bms[:].rearrange("p b t n -> p (b t n)")[:, bass.ds(b * (3 * T) + 3 * tt, 3)]
                    ins = pl.tensor_copy(ks[par][:, tt, :, BIAS:BIAS + 3], src.unsqueeze(1).to_broadcast([P, H, 3]))
                ins.then_inc(CG.sem, 1)
            if t == 14:
                reach(eng, s2["summed"], NG * (b - 1))
                alone(eng)
                for tt in range(T):
                    ins = pl.tensor_copy(va[par][:, tt, :, 0:D],
                                         cx[par][:, tt, C:2 * C].rearrange("p (h d) -> p h d", d=D))
                ins.then_inc(CG.sem, 1)

        def ctx_count(b, par):
            return (b - par) * 8 + 16

        def route_dve(eng, b, par, t, prev):
            xr, rw = xrow(b), row[par]

            def step(ins):
                ins.then_inc(RD.sem, 1)
            if t == 1:
                eng.wait_ge(s2["attn_added"], NG * b + NG)
                ln_stats(RD, eng, b, [rows_of(xr, tt) for tt in range(T)], stats3, mv3, veps3)
            if t == 2:
                reach(eng, rows_st[par], (b - par) * 8)
                ln_norm(RD, eng, b, route_rooted, [rows_of(xr, tt) for tt in range(T)], mv3, rstd3,
                        [rw[:, tt, 0:C] for tt in range(T)])
            if t == 6:
                eng.wait_ge(m2_full, M_CROSS * b + 2)
                step(v.tensor_reduce(nml[:], MB[:, 0:T * E].rearrange("p (t e) -> p t e", t=T), AX, ALU.max,
                                     negate=True))
            if t == 8:
                RA.wait(eng, "exp1", b)
                step(v.reciprocal(ersum[:], esum[:]))
                RD.wait(eng, "esum_inv", b)
                step(v.tensor_tensor(gates[:], eg[:], ersum[:].unsqueeze(2).to_broadcast([P, T, E]), ALU.mult))
                RD.wait(eng, "gates", b)
                alone(eng)
                for tt in range(T):
                    step(v.max(top[:, tt, :], gates[:, tt, :]))
                for tt in range(T):
                    RD.wait(eng, f"top{tt}", b)
                    alone(eng)
                    step(v.match_replace(left[:, tt, :], top[:, tt, :], gates[:, tt, :], -1.0))
            if t == 9:
                RD.wait(eng, "left1", b)
                step(v.tensor_scalar(chosen[:], left[:], 0.0, None, ALU.is_lt))
                step(v.tensor_reduce(wsum[:], top[:], AX, ALU.add))
                RD.wait(eng, "wsum", b)
                step(v.tensor_scalar(wsum2[:], wsum[:], EPS, None, ALU.max))
                RD.wait(eng, "wmax", b)
                step(v.reciprocal(wr[:], wsum2[:]))
                step(v.tensor_tensor(eg[:], gates[:], chosen[:], ALU.mult))
                RD.wait(eng, "wpart", b)
                step(v.tensor_tensor(rw[:, :, C:ROW], eg[:], wr[:].unsqueeze(2).to_broadcast([P, T, E]), ALU.mult))
            if t == 11:
                eng.wait_ge(m2_full, M_CROSS * b + 3)
                step(v.tensor_tensor(before[:], before[:], chosen[:, 0, :], ALU.add))
                RD.wait(eng, "before0", b)
                step(v.tensor_tensor(before[:], before[:], chosen[:, 1, :], ALU.add))
                rank = MB[:, 0:T * E].rearrange("p (t e) -> p t e", t=T)
                step(v.scalar_tensor_tensor(vd[:], rank, float(CAP), chosen[:], ALU.is_lt, ALU.mult))
                step(v.tensor_tensor(sl[:], ebase[:].unsqueeze(1).to_broadcast([P, T, E]), rank, ALU.subtract))
                RD.wait(eng, "slot", b)
                step(v.tensor_tensor(val[:], sl[:], vd[:], ALU.mult))
                RD.wait(eng, "val", b)
                alone(eng)
                for tt in range(T):
                    step(v.max(topv[:, tt, :], val[:, tt, :]))
            if t == 12:
                reach(eng, scattered[par], (b - par) * 8 * T * TOPK)
                RD.wait(eng, "topv1", b)
                step(v.tensor_scalar(sidx[par][:], topv[:], -1.0, FAR, ALU.mult, ALU.add))
                step(v.tensor_copy(stok[par][:], tok_f[:]))
                RD.wait(eng, "token", b)
                step(v.tensor_scalar(tok_f[:], tok_f[:], float(N), None, ALU.add))

        def route_act(eng, b, par, t, prev):
            if t == 4:
                eng.wait_ge(m2_full, M_CROSS * b + 1)
                reach(eng, x3t_st[par], (b - par) * 8)
                a.activation(x3T[par][:].rearrange("p k n -> p (k n)"), MB[:], ACT.Copy).then_inc(RA.sem, 1)
            if t == 7:
                RD.wait(eng, "top_logit", b)
                for tt in range(T):
                    a.activation(eg[:, tt, :], MB[:, tt * E:(tt + 1) * E], ACT.Exp, bias=nml[:, tt:tt + 1],
                                 accum_out=esum[:, tt:tt + 1]).then_inc(RA.sem, 1)

        def route_pe(eng, b, par, t, prev):
            if t == 3:
                if prev:
                    RD.wait(eng, "slot", b - 1)
                RD.wait(eng, "xn1", b)
                turn4(lambda k, tt: MB[:, k * N + tt * P:k * N + (tt + 1) * P],
                      lambda k, tt: row[par][:, tt, k * P:(k + 1) * P]).then_inc(m2_full, 1)
            if t == 5:
                RA.wait(eng, "x3T", b)
                for tt in range(T):
                    for k in range(K2):
                        ins = pe.matmul(MB[:, tt * E:(tt + 1) * E], x3T[par][:, k, tt * P:(tt + 1) * P],
                                        wg_sb[:, k, :], start=(k == 0), stop=(k == K2 - 1))
                ins.then_inc(m2_full, 1)
            if t == 10:
                RD.wait(eng, "weights", b)
                RA.wait(eng, "exp1", b)
                if prev:
                    RD.wait(eng, "before1", b - 1)
                for tt in range(T):
                    out = MB[:, tt * E:(tt + 1) * E]
                    pe.matmul(out, onesb[:], before[:], start=True, stop=False)
                    if tt:
                        pe.matmul(out, onesb[:], chosen[:, 0, :], start=False, stop=False)
                    ins = pe.matmul(out, lower[:], chosen[:, tt, :], start=False, stop=True)
                ins.then_inc(m2_full, 1)

        def route_pool(eng, b, par, t, prev):
            if t == 1:
                ln_root(RD, eng, b, route_rooted, veps3, rstd3)

        def scatter_pool(eng, b, par, t):
            if t == 0:
                RD.wait(eng, "token", b)
                alone(eng)
            tt, j = t // TOPK, t % TOPK
            pl.indirect_dma_start(out=slot_tok, out_offset=bass.IndirectOffsetOnAxis(ap=sidx[par][:, tt, j:j + 1], axis=0),
                                  in_=stok[par][:, tt:tt + 1], in_offset=None, bounds_check=SLOTS - 1,
                                  oob_is_err=False).then_inc(scattered[par], 16)

        def run_cross(eng, core, prep=None, route=None, scatter=None):
            if prep:
                for t in range(H):
                    prep(eng, 0, 0, t, False)

            def body(c, par, n):
                for t in range(H):
                    if n <= B:
                        core(c, par, t, n == 0, n >= B)
                    if prep and n < B - 1:
                        prep(eng, c + 1, 1 - par, t, True)
                    if route and 2 <= n < B + 2:
                        route(eng, c - 2, par, t, n > 2)
                    if scatter and n >= 3:
                        scatter(eng, c - 3, 1 - par, t)
            sweep(eng, body, 4, 3)

        with nc.Block() as block:
            @block.sync
            def _(eng):
                def load(b, par, prev):
                    if prev:
                        CG.wait(eng, "values", b - 2)
                    eng.dma_start(cx[par][:], ctx_rows(b)).then_inc(in_ctx[par], 16)

                def ctx_rows(b):
                    return ctx_in[bass.ds(b, 1), :, :].rearrange("o (t p) c -> p (o t) c", p=P)

                def store(b, par):
                    RD.wait(eng, "weights", b)
                    eng.dma_start(rows[bass.ds(b * N, N), :].rearrange("(t p) c -> p t c", p=P), row[par][:])\
                        .then_inc(rows_st[par], 16)
                    RA.wait(eng, "x3T", b)
                    alone(eng)
                    eng.dma_start(xt_dram[:, :, bass.ds(b * N, N)], x3T[par][:]).then_inc(x3t_st[par], 16)

                load(0, 0, False)
                load(1, 1, False)

                def body(c, par, n):
                    if n < B - 2:
                        load(c + 2, par, True)
                    if 2 <= n < B + 2:
                        store(c - 2, par)
                sweep(eng, body, 4, 2)
                for par in range(2):
                    eng.wait_ge(rows_st[par], 8 * B)
                    eng.wait_ge(x3t_st[par], 8 * B)

            @block.tensor
            def _(eng):
                run_cross(eng, lambda c, par, t, first, last: pe_core2(
                    eng, c, par, t, lambda e, cc: CG.wait(e, "values", cc), first, last), None, route_pe)

            @block.scalar
            def _(eng):
                run_cross(eng, lambda c, par, t, first, last: act_core2(eng, c, par, t, first, last), None, route_act)

            @block.vector
            def _(eng):
                run_cross(eng, lambda c, par, t, first, last: dve_core2(eng, c, par, t, first, last),
                          cross_dve, route_dve)

            @block.gpsimd
            def _(eng):
                run_cross(eng, lambda c, par, t, first, last: pool_core2(eng, c, par, t, first, last),
                          cross_pool, route_pool, scatter_pool)
                for par in range(2):
                    eng.wait_ge(scattered[par], 8 * B * T * TOPK)

        attn.close()

        ffn = ExitStack()
        fsb = lambda name, shape, dt=F32: sb(name, shape, dt, ffn)
        w1 = fsb("w1", [P, K2, 2 * FF])
        w2 = fsb("w2", [P, FT, C])
        xc = [fsb(f"xc{i}", [P, K2, CH]) for i in range(2)]
        sg = [fsb(f"sg{i}", [P, CH]) for i in range(2)]
        gT = [fsb(f"gT{i}", [P, FT, CH]) for i in range(2)]
        ys = [fsb(f"ys{i}", [P, CH // P * C]) for i in range(2)]
        in_sw = sem("in_sw")
        in_xc = [sem(f"in_xc{i}") for i in range(2)]
        hid = sem("hid")
        acted = sem("acted")
        gated = sem("gated")
        outed = sem("outed")
        y_made = sem("y_made")
        y_st = [sem(f"y_st{i}") for i in range(2)]
        NCH = NTOK // CH

        with nc.Block() as block:
            def chunks(eng, body, tail=False):
                body(0, 0, False)
                body(1, 1, True)
                with eng.Fori(1, NCH // 2) as i:
                    body(2 * i, 0, True)
                    body(2 * i + 1, 1, True)

            @block.sync
            def _(eng):
                eng.dma_start(w1[:], sw1.rearrange("(k p) n -> p k n", p=P)).then_inc(in_sw, 16)
                eng.dma_start(w2[:], sw2.rearrange("(k p) n -> p k n", p=P)).then_inc(in_sw, 16)

                def load(q, par):
                    reach(eng, hid, FT * (q - 1))
                    eng.dma_start(xc[par][:], xt_dram[:, :, bass.ds(q * CH, CH)]).then_inc(in_xc[par], 16)

                def store(q, par):
                    eng.wait_ge(y_made, 2 * q + 2)
                    eng.dma_start(y[bass.ds(q * CH, CH), :].rearrange("(t p) c -> p t c", p=P),
                                  ys[par][:].rearrange("p (t c) -> p t c", c=C)).then_inc(y_st[par], 16)

                load(0, 0)
                load(1, 1)
                with eng.Fori(1, NCH // 2) as i:
                    load(2 * i, 0)
                    store(2 * i - 2, 0)
                    load(2 * i + 1, 1)
                    store(2 * i - 1, 1)
                store(NCH - 2, 0)
                store(NCH - 1, 1)
                for par in range(2):
                    eng.wait_ge(y_st[par], 8 * NCH)

            @block.tensor
            def _(eng):
                def hidden(q, par, js):
                    for j in js:
                        reach(eng, gated, FT * q + j - 1)
                        for half in range(2):
                            for k in range(K2):
                                f = half * FF + j * P
                                ins = pe.matmul(bank[2 * (j % 2) + half][:], w1[:, k, f:f + P], xc[par][:, k, :],
                                                start=(k == 0), stop=(k == K2 - 1))
                        ins.then_inc(hid, 1)

                def output(q, par):
                    eng.wait_ge(gated, FT * q + FT)
                    reach(eng, y_made, 2 * (q - 1))
                    for tt in range(CH // P):
                        out = bank[4 + 2 * par + tt // 2][:, tt % 2 * C:(tt % 2 + 1) * C]
                        for j in range(FT):
                            ins = pe.matmul(out, gT[par][:, j, tt * P:(tt + 1) * P], w2[:, j, :],
                                            start=(j == 0), stop=(j == FT - 1))
                        if tt % 2:
                            ins.then_inc(outed, 1)

                def body(q, par, prev):
                    eng.wait_ge(in_xc[par], (q - par) * 8 + 16)
                    hidden(q, par, range(2))
                    if prev:
                        output(q - 1, 1 - par)
                    hidden(q, par, range(2, FT))
                eng.wait_ge(in_sw, 32)
                chunks(eng, body)
                output(NCH - 1, 1)

            @block.scalar
            def _(eng):
                def body(q, par, prev):
                    for j in range(FT):
                        eng.wait_ge(hid, FT * q + j + 1)
                        reach(eng, gated, FT * q + j - 1)
                        a.activation(sg[j % 2][:], bank[2 * (j % 2) + 1][:], ACT.Silu).then_inc(acted, 1)
                chunks(eng, body)

            @block.vector
            def _(eng):
                def finish(q, par):
                    reach(eng, y_st[par], (q - par) * 8)
                    for i in range(2):
                        eng.wait_ge(outed, 2 * q + i + 1)
                        v.tensor_tensor(ys[par][:, i * 2 * C:(i + 1) * 2 * C], bank[4 + 2 * par + i][:],
                                        X[:, bass.ds(q * (CH // P * C) + i * 2 * C, 2 * C)], ALU.add)\
                            .then_inc(y_made, 1)

                def body(q, par, prev):
                    for j in range(FT):
                        eng.wait_ge(acted, FT * q + j + 1)
                        reach(eng, outed, 2 * (q - 1))
                        v.tensor_tensor(gT[par][:, j, :], bank[2 * (j % 2)][:], sg[j % 2][:], ALU.mult)\
                            .then_inc(gated, 1)
                        if j == 2 and prev:
                            finish(q - 1, 1 - par)
                chunks(eng, body)
                finish(NCH - 1, 1)

        idx = [fsb(f"idx{i}", [HC, 2], I32) for i in range(2)]
        xg = [fsb(f"xg{i}", [HC, 2, ROW]) for i in range(2)]
        xgT = [fsb(f"xgT{i}", [P, K2, CAP]) for i in range(2)]
        sge = [fsb(f"sge{i}", [P, FT // 2 * CAP]) for i in range(2)]
        gTe = [fsb(f"gTe{i}", [P, FT * CAP]) for i in range(2)]
        yse = [fsb(f"yse{i}", [HC, 2, C]) for i in range(2)]
        in_idx = [sem(f"in_idx{i}") for i in range(2)]
        fetched = [sem(f"fetched{i}") for i in range(2)]
        added = [sem(f"added{i}") for i in range(2)]
        e_turned, e_copied, e_hid, e_acted, e_gated, e_out, e_scaled = (sem(n) for n in (
            "e_turned", "e_copied", "e_hid", "e_acted", "e_gated", "e_out", "e_scaled"))
        HALF = FT // 2 * CAP

        with nc.Block() as block:
            def experts(eng, body):
                body(0, 0, 0)
                body(1, 1, 1)
                with eng.Fori(1, E // 2 - 1) as i:
                    body(2 * i, 0, 2)
                    body(2 * i + 1, 1, 3)
                body(E - 2, 0, E - 2)
                body(E - 1, 1, E - 1)

            @block.sync
            def _(eng):
                names = slot_tok.rearrange("(e p c) o -> e p (c o)", c=2, p=HC)

                def body(e, par, n):
                    reach(eng, added[par], (e - par) * 16)
                    eng.dma_start(idx[par][:], names[bass.ds(e, 1), :, :].rearrange("o p c -> p (o c)"))\
                        .then_inc(in_idx[par], 16)
                    if n >= 2:
                        reach(eng, e_out, e - 1)
                        eng.dma_start(ew_sb[par][:], ew[bass.ds(e, 1), :, :].rearrange("o p n -> p (o n)"))\
                            .then_inc(loaded_ew[par], 16)
                experts(eng, body)

            @block.gpsimd
            def _(eng):
                def fetch(e, par):
                    eng.wait_ge(in_idx[par], (e - par) * 8 + 16)
                    reach(eng, e_turned, e - 1)
                    reach(eng, e_scaled, e - 1)
                    alone(eng)
                    for c in range(2):
                        pl.indirect_dma_start(out=xg[par][:, c, :], out_offset=None, in_=rows,
                                              in_offset=bass.IndirectOffsetOnAxis(ap=idx[par][:, c:c + 1].bitcast(U32), axis=0))\
                            .then_inc(fetched[par], 16)

                def body(e, par, n):
                    if n < E - 1:
                        fetch(e + 1, 1 - par)
                    eng.wait_ge(e_scaled, e + 1)
                    if n >= 1:
                        eng.wait_ge(added[1 - par], (e + par) * 16)
                    alone(eng)
                    for c in range(2):
                        pl.indirect_dma_start(out=y, out_offset=bass.IndirectOffsetOnAxis(ap=idx[par][:, c:c + 1].bitcast(U32), axis=0),
                                              in_=yse[par][:, c, :], in_offset=None, compute_op=ALU.add)\
                            .then_inc(added[par], 16)
                fetch(0, 0)
                experts(eng, body)
                for par in range(2):
                    eng.wait_ge(added[par], 16 * E)

            @block.tensor
            def _(eng):
                TB = bank[4]

                def turn(e, par):
                    eng.wait_ge(fetched[par], (e - par) * 16 + 32)
                    reach(eng, e_copied, e)
                    for k in range(K2):
                        for c in range(2):
                            ins = pe.transpose(TB[:, k * CAP + c * HC:k * CAP + (c + 1) * HC],
                                               xg[par][:, c, k * P:(k + 1) * P], ident[0:HC, 0:HC])
                    ins.then_inc(e_turned, 1)

                def body(e, par, n):
                    wa = ew_sb[par][:, 0:2 * K2 * FF].rearrange("p (k f) -> p k f", k=K2)
                    wb = ew_sb[par][:, 2 * K2 * FF:].rearrange("p (j c) -> p j c", c=C)
                    eng.wait_ge(loaded_ew[par], (e - par) * 8 + 16)
                    eng.wait_ge(e_copied, e + 1)
                    for half in range(2):
                        reach(eng, e_gated, 2 * e + half - 1)
                        for side in range(2):
                            for j in range(FT // 2):
                                f = side * FF + (half * (FT // 2) + j) * P
                                for k in range(K2):
                                    ins = pe.matmul(bank[2 * half + side][:, j * CAP:(j + 1) * CAP],
                                                    wa[:, k, f:f + P], xgT[par][:, k, :],
                                                    start=(k == 0), stop=(k == K2 - 1))
                        ins.then_inc(e_hid, 1)
                    if n < E - 1:
                        turn(e + 1, 1 - par)
                    reach(eng, e_scaled, e - 1)
                    for c in range(2):
                        for j in range(FT):
                            if c == 0 and j % (FT // 2) == 0:
                                eng.wait_ge(e_gated, 2 * e + j // (FT // 2) + 1)
                            ins = pe.matmul(bank[5 + par][0:HC, c * C:(c + 1) * C],
                                            gTe[par][:, j * CAP + c * HC:j * CAP + (c + 1) * HC], wb[:, j, :],
                                            start=(j == 0), stop=(j == FT - 1))
                    ins.then_inc(e_out, 1)
                turn(0, 0)
                experts(eng, body)

            @block.scalar
            def _(eng):
                def copy(e, par):
                    eng.wait_ge(e_turned, e + 1)
                    reach(eng, e_hid, 2 * (e - 1))
                    a.activation(xgT[par][:].rearrange("p k n -> p (k n)"), bank[4][:, 0:K2 * CAP], ACT.Copy)\
                        .then_inc(e_copied, 1)

                def body(e, par, n):
                    for half in range(2):
                        eng.wait_ge(e_hid, 2 * e + half + 1)
                        reach(eng, e_gated, 2 * e + half - 1)
                        a.activation(sge[half][:], bank[2 * half + 1][:, 0:HALF], ACT.Silu).then_inc(e_acted, 1)
                    if n < E - 1:
                        copy(e + 1, 1 - par)
                copy(0, 0)
                experts(eng, body)

            @block.vector
            def _(eng):
                def body(e, par, n):
                    for half in range(2):
                        eng.wait_ge(e_acted, 2 * e + half + 1)
                        reach(eng, e_out, e - 1)
                        v.tensor_tensor(gTe[par][:, half * HALF:(half + 1) * HALF], bank[2 * half][:, 0:HALF],
                                        sge[half][:], ALU.mult).then_inc(e_gated, 1)
                    eng.wait_ge(e_out, e + 1)
                    reach(eng, added[par], (e - par) * 16)
                    for c in range(2):
                        ins = v.tensor_scalar(yse[par][:, c, :], bank[5 + par][0:HC, c * C:(c + 1) * C],
                                              xg[par][:, c, bass.ds(e + C, 1)], None, ALU.mult)
                    ins.then_inc(e_scaled, 1)
                experts(eng, body)
        ffn.close()


_INPUTS = ["x", "ctx_2048", "itok_Bx1_68_817", "w_qkv", "b_qkv", "w_lepe", "b_lepe", "xb", "wg", "sw1", "sw2",
           "ew", "cos_t", "sin_t"]


def rope_tables():
    position = np.arange(N, dtype=np.float32)[:, None]
    rate = np.exp(np.arange(0, D, 2, dtype=np.float32) * np.float32(-np.log(10000.0) / D))
    angle = position * rate.astype(np.float32)
    return np.cos(angle), np.sin(angle)


def kernel(**inputs):
    import concourse.bacc as bacc
    from concourse.bass_utils import run_bass_kernel_spmd

    g = {k: np.asarray(v) for k, v in inputs.items()}
    cos_t, sin_t = rope_tables()
    first = g["L0_ffn_expert_w1"].transpose(0, 2, 1).reshape(E, K2, P, 2 * FF).transpose(0, 2, 1, 3)
    second = g["L0_ffn_expert_w2"].transpose(0, 2, 1).reshape(E, FT, P, C).transpose(0, 2, 1, 3)
    arrays = {
        "x": g["x"], "ctx_2048": g["ctx_2048"], "itok_Bx1_68_817": g["itok_Bx1_68_817"],
        "w_qkv": g["L0_attn_w_qkv"].T, "b_qkv": g["L0_attn_b_qkv"],
        "w_lepe": g["L0_attn_w_lepe"].reshape(C, 3), "b_lepe": g["L0_attn_b_lepe"].reshape(K2, P).T,
        "xb": g["L0_xattn_b"].reshape(T, P).T,
        "wg": g["L0_ffn_wg"].T, "sw1": g["L0_ffn_shared_w1"].T, "sw2": g["L0_ffn_shared_w2"].T,
        "ew": np.concatenate([first.reshape(E, P, -1), second.reshape(E, P, -1)], axis=2),
        "cos_t": cos_t, "sin_t": sin_t,
    }
    nc = bacc.Bacc("TRN2", target_bir_lowering=False, num_devices=1)
    args, sent = [], {}
    for name in _INPUTS:
        sent[f"in_{name}"] = np.ascontiguousarray(arrays[name])
        args.append(nc.dram_tensor(f"in_{name}", sent[f"in_{name}"].shape, mybir.dt.from_np(sent[f"in_{name}"].dtype),
                                   kind="ExternalInput").ap())
    args.append(nc.dram_tensor("out", (ROWS, C), F32, kind="ExternalOutput").ap())
    decoder_layer(nc, *args)
    result = run_bass_kernel_spmd(nc, [sent], core_ids=[0])
    return result.results[0]["out"][:NTOK].reshape(B, N, C)
```

```python
from contextlib import ExitStack

import concourse.bass as bass
import numpy as np
from concourse import mybir

P = 128
B, N, C = 16, 256, 256
H = 16
D = C // H
T = N // P
K2 = C // P
TERMS = 6
DATA = TERMS * D
BIAS = DATA
TOP = DATA + 3
W = DATA + 6
G = 4
NG = H // G
VW = 32
RH = D // 2

E, TOPK, CAP, FF = 64, 8, 160, 768
FT = FF // P
HC = CAP // 2
SLOTS = E * CAP
ROW = C + E
NTOK = B * N
ROWS = NTOK + CAP
FAR = 16384.0
MASK = -1.0e12
EPS_LN = 1.0e-5
EPS = float(np.finfo(np.float32).eps)
CH = 512

F32, BF16, I32, U32 = mybir.dt.float32, mybir.dt.bfloat16, mybir.dt.int32, mybir.dt.uint32
ALU = mybir.AluOpType
ACT = mybir.ActivationFunctionType
AX = mybir.AxisListType.X

Q_HI, Q_MID, Q_LO = (0, 6, 2), (1, 5, 2), (5, 6, 1)
K_HI, K_MID, K_LO = (3, 6, 1), (0, 2, 1), (2, 3, 1)


def reach(eng, sem, value):
    if isinstance(value, int) and value <= 0:
        return
    eng.wait_ge(sem, value)


class Steps:

    def __init__(self, sem, names):
        self.sem, self.names = sem, names.split()

    def done(self, name, b):
        return b * len(self.names) + self.names.index(name) + 1

    def wait(self, eng, name, b):
        reach(eng, self.sem, self.done(name, b))


def decoder_layer(nc, x, ctx_in, itok, w_qkv, b_qkv, w_lepe, b_lepe, xb, wg, sw1, sw2, ew, cos_t,
                  sin_t, y):
    v, a, pl, pe, sp = nc.vector, nc.scalar, nc.gpsimd, nc.tensor, nc.sync
    slot_tok = nc.dram_tensor("slot_tok", (SLOTS, 1), I32, kind="Internal").ap()
    rows = nc.dram_tensor("rows", (ROWS, ROW), F32, kind="Internal").ap()
    xt_dram = nc.dram_tensor("xt_dram", (P, K2, NTOK), F32, kind="Internal").ap()

    stack = ExitStack()
    with stack:
        def sb(name, shape, dt=F32, scope=stack):
            return scope.enter_context(nc.sbuf_tensor(name, shape, dt))

        def sem(name):
            return stack.enter_context(nc.semaphore(name))

        bank = [stack.enter_context(nc.psum_tensor(f"bank{i}", [P, 512], F32)) for i in range(8)]

        X = sb("X", [P, B * T * C])
        ident = sb("ident", [P, P])
        identb = sb("identb", [P, P], BF16)
        ew_sb = [sb(f"ew{i}", [P, 2 * K2 * FF + FT * C]) for i in range(2)]
        loaded_ew = [sem(f"loaded_ew{i}") for i in range(2)]

        def xrow(b):
            return X[:, bass.ds(b * (T * C), T * C)]

        attn = ExitStack()
        asb = lambda name, shape, dt=F32: sb(name, shape, dt, attn)
        wq_sb = asb("wq_sb", [P, K2, 3 * C])
        wg_sb = asb("wg_sb", [P, K2, E])
        bq_sb = asb("bq_sb", [P, 3 * C])
        cos_sb = asb("cos_sb", [P, T, RH])
        sin_sb = asb("sin_sb", [P, T, RH])
        wl_sb = asb("wl_sb", [P, K2, 3])
        bl_sb = asb("bl_sb", [P, K2])
        xb_sb = asb("xb_sb", [P, T])
        seq_i = asb("seq_i", [P, B], I32)
        seq_f = asb("seq_f", [P, B])
        pos_i = asb("pos_i", [P, T], I32)
        pos_f = asb("pos_f", [P, T])
        minus1 = asb("minus1", [P, 1])
        mhalf = asb("mhalf", [P, T])
        bm = asb("bm", [P, B, T])
        bmr = asb("bmr", [P, B, T])
        bms = asb("bms", [P, B, T, 3], BF16)
        lower = asb("lower", [P, P], BF16)
        onesb = asb("onesb", [P, P], BF16)
        onesf = asb("onesf", [P, P])
        init_i = asb("init_i", [E, CAP], I32)
        zrow = asb("zrow", [HC, 2, ROW])
        ebase = asb("ebase", [P, E])
        ebase_i = asb("ebase_i", [P, E], I32)
        tok_f = asb("tok_f", [P, T])
        tok_i = asb("tok_i", [P, T], I32)
        before = asb("before", [P, E], BF16)

        ks = [asb(f"ks{i}", [P, T, H, W], BF16) for i in range(2)]
        qs = [asb(f"qs{i}", [P, T, H, W], BF16) for i in range(2)]
        va = [asb(f"va{i}", [P, T, H, VW]) for i in range(2)]
        kT = asb("kT", [W, H, N], BF16)
        qT = asb("qT", [TOP, H, N], BF16)
        q2 = [asb(f"q2_{i}", [W, 2 * N], BF16) for i in range(2)]
        ex = asb("ex", [P, 2 * G, T * N])
        oT = [asb(f"oT{i}", [P, N]) for i in range(2)]
        nm = asb("nm", [P, T, H])
        nmr = asb("nmr", [P, T, H])
        rden = asb("rden", [P, T * G])
        otmp = asb("otmp", [P, T, G * D])

        stats = asb("stats", [P, T, 6])
        mv = asb("mv", [P, T, 2])
        rstd = asb("rstd", [P, T])
        veps = asb("veps", [P, T])
        xn = asb("xn", [P, T, C])
        xnT = asb("xnT", [P, K2, N])
        z = asb("z", [P, T, 2 * C])
        ez = asb("ez", [P, T, 2 * C])
        rc = asb("rc", [P, 2 * H, 2, RH])
        rs = asb("rs", [P, 2 * H, 2, RH])
        r = asb("r", [P, 2 * H, D])
        rem = {o: asb(f"rem_{o}", [P, H, D]) for o in "kq"}
        lep = asb("lep", [P, K2, N])
        vtok = asb("vtok", [P, T, C])
        vTs = asb("vTs", [P, K2, N])

        cx = [asb(f"cx{i}", [P, T, 2 * C]) for i in range(2)]
        row = [asb(f"row{i}", [P, T, ROW]) for i in range(2)]
        stats3 = asb("stats3", [P, T, 6])
        mv3 = asb("mv3", [P, T, 2])
        rstd3 = asb("rstd3", [P, T])
        veps3 = asb("veps3", [P, T])
        x3T = [asb(f"x3T{i}", [P, K2, N]) for i in range(2)]
        nml = asb("nml", [P, T])
        eg = asb("eg", [P, T, E])
        esum = asb("esum", [P, T])
        ersum = asb("ersum", [P, T])
        gates = asb("gates", [P, T, E])
        top = asb("top", [P, T, TOPK])
        left = asb("left", [P, T, E])
        chosen = asb("chosen", [P, T, E], BF16)
        wsum = asb("wsum", [P, T])
        wsum2 = asb("wsum2", [P, T])
        wr = asb("wr", [P, T])
        vd = asb("vd", [P, T, E])
        sl = asb("sl", [P, T, E])
        val = asb("val", [P, T, E])
        topv = asb("topv", [P, T, TOPK])
        sidx = [asb(f"sidx{i}", [P, T, TOPK], U32) for i in range(2)]
        stok = [asb(f"stok{i}", [P, T], I32) for i in range(2)]

        in_w = sem("in_w")
        in_x = sem("in_x")
        init_st = sem("init_st")
        set_pool = sem("set_pool")
        set_dve = sem("set_dve")

        passed = {}

        def alone(eng):
            name = str(eng.engine).split(".")[-1]
            if name not in passed:
                passed[name] = sem(f"passed_{name}")
            eng.sem_inc(passed[name], 1)

        with nc.Block() as block:
            NW = 10

            @block.sync
            def _(eng):
                for dst, src in (
                    (wq_sb[:], w_qkv.rearrange("(k p) n -> p k n", p=P)),
                    (wg_sb[:], wg.rearrange("(k p) n -> p k n", p=P)),
                    (bq_sb[:], b_qkv.partition_broadcast(P)),
                    (cos_sb[:], cos_t.rearrange("(t p) n -> p t n", p=P)),
                    (sin_sb[:], sin_t.rearrange("(t p) n -> p t n", p=P)),
                    (wl_sb[:], w_lepe.rearrange("(k p) n -> p k n", p=P)),
                    (bl_sb[:], b_lepe),
                    (xb_sb[:], xb),
                    (seq_i[:], itok.rearrange("b o -> (b o)").partition_broadcast(P)),
                ):
                    eng.dma_start(dst, src).then_inc(in_w, 16)
                eng.dma_start(X[:].rearrange("p (b t c) -> p b t c", b=B, t=T),
                              x.rearrange("b (t p) c -> p b t c", p=P)).then_inc(in_x, 16)
                for i in range(2):
                    eng.dma_start(ew_sb[i][:], ew[i]).then_inc(loaded_ew[i], 16)
                eng.wait_ge(set_pool, 12)
                eng.dma_start(slot_tok.rearrange("(e s) o -> e (s o)", e=E), init_i[:]).then_inc(init_st, 16)
                eng.dma_start(rows[NTOK:ROWS, :].rearrange("(p a) n -> p a n", a=2), zrow[:]).then_inc(init_st, 16)
                eng.dma_start(y[NTOK:ROWS, :].rearrange("(p a) n -> p a n", a=2), zrow[:, :, 0:C]).then_inc(init_st, 16)
                eng.wait_ge(init_st, 48)
                eng.wait_ge(in_w, 16 * 9)
                eng.wait_ge(in_x, 16)

            @block.gpsimd
            def _(eng):
                pl.memset(ident[:], 0.0).then_inc(set_pool, 1)
                pl.memset(onesf[:], 1.0).then_inc(set_pool, 1)
                pl.memset(zrow[:], 0.0).then_inc(set_pool, 1)
                pl.memset(before[:], 0.0).then_inc(set_pool, 1)
                pl.memset(minus1[:], -1.0).then_inc(set_pool, 1)
                pl.memset(mhalf[:], -0.5).then_inc(set_pool, 1)
                eng.wait_ge(set_pool, 2)
                pl.affine_select(out=ident[:], in_=ident[:], compare_op=ALU.not_equal, fill=1.0, base=0,
                                 pattern=[[-1, P]], channel_multiplier=1).then_inc(set_pool, 1)
                pl.affine_select(out=onesf[:], in_=onesf[:], compare_op=ALU.is_gt, fill=0.0, base=0,
                                 pattern=[[1, P]], channel_multiplier=-1).then_inc(set_pool, 1)
                pl.iota(pos_i[:], pattern=[[P, T]], base=0, channel_multiplier=1).then_inc(set_pool, 1)
                pl.iota(init_i[:], pattern=[[1, CAP]], base=NTOK, channel_multiplier=0).then_inc(set_pool, 1)
                pl.iota(ebase_i[:], pattern=[[-CAP, E]], base=int(FAR), channel_multiplier=0)\
                    .then_inc(set_pool, 1)
                pl.memset(onesb[:], 1.0).then_inc(set_pool, 1)

            @block.vector
            def _(eng):
                def step(ins):
                    ins.then_inc(set_dve, 1)

                for i in range(2):
                    step(v.memset(qs[i][:, :, :, BIAS:BIAS + 3], 1.0))
                    step(v.memset(ks[i][:, :, :, BIAS:BIAS + 3], 0.0))
                    step(v.memset(ks[i][:, :, :, TOP:TOP + 3], 1.0))
                    step(v.memset(va[i][:], 0.0))
                eng.wait_ge(set_dve, 8)
                for i in range(2):
                    step(v.memset(va[i][:, :, :, D:D + 1], 1.0))
                eng.wait_ge(set_pool, 12)
                step(v.tensor_copy(identb[:], ident[:]))
                step(v.tensor_copy(lower[:], onesf[:]))
                step(v.tensor_copy(pos_f[:], pos_i[:]))
                step(v.tensor_copy(tok_f[:], pos_i[:]))
                step(v.tensor_copy(ebase[:], ebase_i[:]))
                eng.wait_ge(in_w, 16 * 9)
                step(v.tensor_scalar(bq_sb[:, 0:2 * C], bq_sb[:, 0:2 * C], 1.0, None, ALU.add))
                step(v.tensor_copy(seq_f[:], seq_i[:]))
                eng.wait_ge(set_dve, 17)
                for t in range(T):
                    step(v.tensor_scalar(bm[:, :, t], seq_f[:], pos_f[:, t:t + 1], None, ALU.is_gt))
                eng.wait_ge(set_dve, 19)
                for t in range(T):
                    step(v.tensor_scalar(bmr[:, :, t], bm[:, :, t], -MASK, MASK, ALU.mult, ALU.add))
                eng.wait_ge(set_dve, 21)
                for t in range(T):
                    step(v.tensor_scalar(bm[:, :, t], bmr[:, :, t], xb_sb[:, t:t + 1], 1.0 / D ** -0.5,
                                         ALU.add, ALU.mult))
                eng.wait_ge(set_dve, 23)
                step(v.tensor_copy(bms[:, :, :, 0], bm[:]))
                eng.wait_ge(set_dve, 24)
                step(v.tensor_tensor(bmr[:], bm[:], bms[:, :, :, 0], ALU.subtract))
                eng.wait_ge(set_dve, 25)
                step(v.tensor_copy(bms[:, :, :, 1], bmr[:]))
                eng.wait_ge(set_dve, 26)
                step(v.tensor_tensor(bms[:, :, :, 2], bmr[:], bms[:, :, :, 1], ALU.subtract))
                eng.wait_ge(set_dve, 27)

        def core_of(kind):
            s = {n: sem(f"{kind}_{n}") for n in (
                "kq_turned", "kq_copied", "scored", "max_found", "max_split", "split_chain", "q_turned", "q_copied",
                "rescored", "exp_done", "summed", "sum_copied", "sum_turned", "sum_used", "attn_added", "attn_chain")}
            XB, YB, ZB = bank[4], bank[5], bank[6]
            xb16, yb16 = XB[:].bitcast(BF16), YB[:].bitcast(BF16)

            def lagged(c, t, lag, every, size, last=False):
                d = t - lag
                if d % every:
                    return None
                u = d // every
                if u >= 0:
                    return (None if last else (c, u, 0))
                return (c - 1, u + size, 1)

            def pe_step(eng, c, par, t, ready, first=False, last=False):
                def unit(lag, every, size):
                    got = lagged(c, t, lag, every, size, last)
                    return None if got is None or (first and got[2]) else got

                if t % 2 == 0 and not last:
                    u, n = t // 4, t // 2 % 2
                    src, width = ((ks, W), (qs, TOP))[n]
                    if t == 0:
                        ready(eng, c)
                    reach(eng, s["kq_copied"], 8 * c + 2 * u + n)
                    for h in range(G):
                        for tt in range(T):
                            ins = pe.transpose(xb16[0:width, (h * T + tt) * P:(h * T + tt + 1) * P],
                                               src[par][:, tt, u * G + h, 0:width], identb[:])
                    ins.then_inc(s["kq_turned"], 1)
                if got := unit(4, 1, H):
                    cc, h, _ = got
                    reach(eng, s["kq_copied"], 8 * cc + 2 * (h // G) + 2)
                    reach(eng, s["max_found"], 16 * cc + h - 1)
                    for tt in range(T):
                        ins = pe.matmul(bank[h % 2][:, tt * N:(tt + 1) * N], qT[0:TOP, h, tt * P:(tt + 1) * P],
                                        kT[0:TOP, h, :], start=True, stop=True)
                    ins.then_inc(s["scored"], 1)
                if got := unit(8, 2, H // 2):
                    cc, p, back = got
                    src = qs[(par + back) % 2]
                    eng.wait_ge(s["max_split"], 8 * cc + p + 1)
                    reach(eng, s["q_copied"], 8 * cc + p)
                    for h in range(2):
                        for tt in range(T):
                            ins = pe.transpose(yb16[0:W, (h * T + tt) * P:(h * T + tt + 1) * P],
                                               src[:, tt, 2 * p + h, 0:W], identb[:])
                    ins.then_inc(s["q_turned"], 1)
                if got := unit(11, 1, H):
                    cc, h, _ = got
                    reach(eng, s["q_copied"], 8 * cc + h // 2 + 1)
                    reach(eng, s["exp_done"], 16 * cc + h - 1)
                    for tt in range(T):
                        ins = pe.matmul(bank[2 + h % 2][:, tt * N:(tt + 1) * N], kT[0:W, h, tt * P:(tt + 1) * P],
                                        q2[h // 2 % 2][0:W, (h % 2) * N:(h % 2 + 1) * N], start=True, stop=True)
                    ins.then_inc(s["rescored"], 1)
                if got := unit(16, 4, NG):
                    cc, g, back = got
                    vv = va[(par + back) % 2]
                    eng.wait_ge(s["exp_done"], 16 * cc + G * g + G)
                    reach(eng, s["sum_used"], 4 * cc + g)
                    for tt in range(T):
                        for j in range(G):
                            h = g * G + j
                            ins = pe.matmul(ZB[32 * j:32 * j + VW, 0:N], vv[:, tt, h, :],
                                            ex[:, h % (2 * G), tt * N:(tt + 1) * N],
                                            start=(tt == 0), stop=(tt == T - 1))
                    ins.then_inc(s["summed"], 1)
                if got := unit(18, 4, NG):
                    cc, g, _ = got
                    eng.wait_ge(s["sum_copied"], 4 * cc + g + 1)
                    for tt in range(T):
                        ins = pe.transpose(ZB[:, N + tt * P:N + (tt + 1) * P], oT[g % 2][:, tt * P:(tt + 1) * P],
                                           ident[:])
                    ins.then_inc(s["sum_turned"], 1)

            def act_step(eng, c, par, t, first=False, last=False):
                def unit(lag, every, size):
                    got = lagged(c, t, lag, every, size, last)
                    return None if got is None or (first and got[2]) else got

                if got := unit(11, 1, H):
                    cc, h, _ = got
                    eng.wait_ge(s["rescored"], 16 * cc + h + 1)
                    reach(eng, s["summed"], 4 * cc + h // G - 1)
                    a.activation(ex[:, h % (2 * G), :], bank[2 + h % 2][:], ACT.Exp, scale=float(D) ** -0.5)\
                        .then_inc(s["exp_done"], 1)
                if got := unit(17, 4, NG):
                    cc, g, _ = got
                    eng.wait_ge(s["summed"], 4 * cc + g + 1)
                    reach(eng, s["sum_turned"], 4 * cc + g - 1)
                    a.activation(oT[g % 2][:], ZB[:, 0:N], ACT.Copy).then_inc(s["sum_copied"], 1)
                if t % 2 == 0 and not last:
                    u, n = t // 4, t // 2 % 2
                    dst, width, read = ((kT, W, "rescored"), (qT, TOP, "scored"))[n]
                    eng.wait_ge(s["kq_turned"], 8 * c + 2 * u + n + 1)
                    reach(eng, s[read], 16 * (c - 1) + G * u + G)
                    a.activation(dst[0:width, u * G:(u + 1) * G, :],
                                 xb16[0:width, :].rearrange("p (h n) -> p h n", h=G), ACT.Copy)\
                        .then_inc(s["kq_copied"], 1)

            def dve_step(eng, c, par, t, first=False, last=False):
                def unit(lag, every, size):
                    got = lagged(c, t, lag, every, size, last)
                    return None if got is None or (first and got[2]) else got

                if got := unit(4, 1, H):
                    cc, h, _ = got
                    eng.wait_ge(s["scored"], 16 * cc + h + 1)
                    v.tensor_reduce(nm[:, :, h], bank[h % 2][:].rearrange("p (t n) -> p t n", t=T), AX, ALU.max,
                                    negate=True).then_inc(s["max_found"], 1)
                if got := unit(9, 2, H // 2):
                    cc, p, _ = got
                    eng.wait_ge(s["q_turned"], 8 * cc + p + 1)
                    reach(eng, s["rescored"], 16 * cc + 2 * p - 2)
                    v.tensor_copy(q2[p % 2][:], yb16[0:W, 0:2 * N]).then_inc(s["q_copied"], 1)
                if got := unit(19, 4, NG):
                    cc, g, _ = got
                    zo = ZB[:, N:2 * N].rearrange("p (u d) -> p u d", d=VW)
                    eng.wait_ge(s["sum_turned"], 4 * cc + g + 1)
                    v.reciprocal(rden[:], zo[:, :, D]).then_inc(s["attn_chain"], 1)
                    eng.wait_ge(s["attn_chain"], 4 * cc + g + 1)
                    reach(eng, s["attn_added"], 4 * cc + g)
                    v.tensor_tensor(otmp[:].rearrange("p t (j d) -> p (t j) d", d=D), zo[:, :, 0:D],
                                    rden[:].unsqueeze(2).to_broadcast([P, T * G, D]), ALU.mult)\
                        .then_inc(s["sum_used"], 1)
                    eng.wait_ge(s["sum_used"], 4 * cc + g + 1)
                    xg = xrow(cc).rearrange("p (t c) -> p t c", t=T)[:, :, g * G * D:(g + 1) * G * D]
                    v.tensor_tensor(xg, xg, otmp[:], ALU.add).then_inc(s["attn_added"], 1)

            def pool_step(eng, c, par, t, first=False, last=False):
                got = lagged(c, t, 6, 2, H // 2, last)
                if got is not None and not (first and got[2]):
                    cc, p, back = got
                    dst = qs[(par + back) % 2]
                    n2, m2 = nm[:, :, 2 * p:2 * p + 2], nmr[:, :, 2 * p:2 * p + 2]
                    part = [dst[:, :, 2 * p:2 * p + 2, TOP + i] for i in range(3)]
                    base = 24 * cc + 3 * p
                    eng.wait_ge(s["max_found"], 16 * cc + 2 * p + 2)
                    alone(eng)
                    pl.tensor_copy(part[0], n2).then_inc(s["split_chain"], 1)
                    eng.wait_ge(s["split_chain"], base + 1)
                    pl.tensor_tensor(m2, n2, part[0], ALU.subtract).then_inc(s["split_chain"], 1)
                    eng.wait_ge(s["split_chain"], base + 2)
                    alone(eng)
                    pl.tensor_copy(part[1], m2).then_inc(s["split_chain"], 1)
                    eng.wait_ge(s["split_chain"], base + 3)
                    pl.tensor_tensor(part[2], m2, part[1], ALU.subtract).then_inc(s["max_split"], 1)

            return s, pe_step, act_step, dve_step, pool_step

        def terms_of(dst, terms):
            return dst.rearrange("p h (n d) -> p h n d", d=D)[:, :, terms[0]:terms[1]:terms[2], :]

        def part_of(dst, terms):
            return terms_of(dst, terms)[:, :, 0, :]

        def copies(ap, terms):
            return ap.unsqueeze(2).to_broadcast([P, H, len(range(*terms)), D])

        TERMS = {"k": (K_HI, K_MID, K_LO), "q": (Q_HI, Q_MID, Q_LO)}

        def split_hi(dve, o, src, dst):
            v.tensor_copy(terms_of(dst, TERMS[o][0]), copies(src, TERMS[o][0])).then_inc(dve.sem, 1)

        def split_rest(eng, dve, pool, b, o, tt, src, dst):
            dve.wait(eng, f"{o}{tt}_hi", b)
            reach(eng, pool.sem, pool.done(f"{o}{1 - tt}_lo", b - 1 + tt))
            pl.tensor_tensor(rem[o][:], src, part_of(dst, TERMS[o][0]), ALU.subtract).then_inc(pool.sem, 1)

        def split_mid(eng, dve, pool, b, o, tt, dst):
            pool.wait(eng, f"{o}{tt}_rest", b)
            v.tensor_copy(terms_of(dst, TERMS[o][1]), copies(rem[o][:], TERMS[o][1])).then_inc(dve.sem, 1)

        def split_lo(eng, dve, pool, b, o, tt, dst):
            dve.wait(eng, f"{o}{tt}_mid", b)
            pl.tensor_tensor(part_of(dst, TERMS[o][2]), rem[o][:], part_of(dst, TERMS[o][1]), ALU.subtract)\
                .then_inc(pool.sem, 1)

        def ln_stats(steps, eng, b, src, st, m, ve_):
            alone(eng)
            for tt in range(T):
                v.bn_stats(st[:, tt, :], src[tt]).then_inc(steps.sem, 1)
            for tt in range(T):
                steps.wait(eng, f"stats{tt}", b)
                alone(eng)
                v.bn_aggr(m[:, tt, :], st[:, tt, :]).then_inc(steps.sem, 1)
            steps.wait(eng, "aggr1", b)
            v.tensor_scalar(ve_[:], m[:, :, 1], EPS_LN, None, ALU.add).then_inc(steps.sem, 1)

        def ln_root(steps, eng, b, rooted, ve_, rs_):
            steps.wait(eng, "veps", b)
            pl.tensor_tensor(rs_[:], ve_[:], mhalf[:], ALU.pow).then_inc(rooted, 1)

        def ln_norm(steps, eng, b, rooted, src, m, rs_, dst):
            eng.wait_ge(rooted, b + 1)
            for tt in range(T):
                v.tensor_scalar(dst[tt], src[tt], m[:, tt, 0:1], rs_[:, tt:tt + 1], ALU.subtract, ALU.mult)\
                    .then_inc(steps.sem, 1)

        LN = "stats0 stats1 aggr0 aggr1 veps xn0 xn1"
        MB = bank[7]
        M_SELF, M_CROSS = 6, 3

        def turn4(dst, src):
            for i in range(2):
                for j in range(2):
                    ins = pe.transpose(dst(i, j), src(i, j), ident[:])
            return ins

        def rows_of(ap, tt):
            return ap.rearrange("p (t c) -> p t c", t=T)[:, tt, :]

        s, pe_core, act_core, dve_core, pool_core = core_of("self")
        m_full = sem("m_full")
        self_rooted = sem("self_rooted")
        SD = Steps(sem("self_dve"), f"{LN} z0 elu0 z1 elu1 v k0_hi q0_hi k0_mid q0_mid values lep_before0 lep_before1 "
                                    "lep_after0 lep_after1 k1_hi q1_hi k1_mid q1_mid lep_added")
        SA = Steps(sem("self_act"), "xnT exp0 exp1 vT lep_mid0 lep_mid1")
        SG = Steps(sem("self_pool"), " ".join(f"cos{t} sin{t} even{t} odd{t} k{t}_rest q{t}_rest k{t}_lo q{t}_lo"
                                              for t in range(T)))
        ROTATE = (7, 11)
        STACK = {"k": (ks, slice(H, 2 * H)), "q": (qs, slice(0, H))}

        def self_dve(eng, b, par, t, prev):
            xr = xrow(b)
            if t == 0:
                ln_stats(SD, eng, b, [rows_of(xr, tt) for tt in range(T)], stats, mv, veps)
            if t == 1:
                reach(eng, m_full, M_SELF * (b - 1) + 1)
                ln_norm(SD, eng, b, self_rooted, [rows_of(xr, tt) for tt in range(T)], mv, rstd,
                        [xn[:, tt, :] for tt in range(T)])
            for tt in range(T):
                if t == 5 + 2 * tt:
                    eng.wait_ge(m_full, M_SELF * b + 2 + tt)
                    if prev:
                        SG.wait(eng, f"sin{tt}", b - 1)
                    v.tensor_tensor(z[:, tt, :], MB[:], bq_sb[:, 0:2 * C], ALU.add).then_inc(SD.sem, 1)
                if t == 6 + 2 * tt:
                    SA.wait(eng, f"exp{tt}", b)
                    v.scalar_tensor_tensor(z[:, tt, :], ez[:, tt, :], 1.0, z[:, tt, :], ALU.min, ALU.max)\
                        .then_inc(SD.sem, 1)
            if t == 9:
                eng.wait_ge(m_full, M_SELF * b + 4)
                if prev:
                    SD.wait(eng, "values", b - 1)
                v.tensor_tensor(vtok[:], MB[:].rearrange("p (t c) -> p t c", t=T),
                                bq_sb[:, 2 * C:3 * C].unsqueeze(1).to_broadcast([P, T, C]), ALU.add)\
                    .then_inc(SD.sem, 1)
            for tt in range(T):
                if t == ROTATE[tt] + 3:
                    reach(eng, s["kq_turned"], 8 * (b - 1))
                    reach(eng, s["q_turned"], 8 * (b - 1))
                    SG.wait(eng, f"odd{tt}", b)
                    for o in "kq":
                        stack_, heads = STACK[o]
                        split_hi(SD, o, r[:, heads, :], stack_[par][:, tt, :, 0:DATA])
                if t == ROTATE[tt] + 4:
                    for o in "kq":
                        split_mid(eng, SD, SG, b, o, tt, STACK[o][0][par][:, tt, :, 0:DATA])
            if t == 12:
                reach(eng, s["summed"], NG * (b - 1))
                SD.wait(eng, "v", b)
                v.tensor_copy(va[par][:, :, :, 0:D], vtok[:].rearrange("p t (h d) -> p t h d", d=D)).then_inc(SD.sem, 1)
            if t == 13:
                for k in range(K2):
                    SA.wait(eng, f"lep_mid{k}", b)
                    v.scalar_tensor_tensor(lep[:, k, 1:N], vTs[:, k, 0:N - 1], wl_sb[:, k, 0:1],
                                           lep[:, k, 1:N], ALU.mult, ALU.add).then_inc(SD.sem, 1)
                for k in range(K2):
                    SD.wait(eng, f"lep_before{k}", b)
                    v.scalar_tensor_tensor(lep[:, k, 0:N - 1], vTs[:, k, 1:N], wl_sb[:, k, 2:3],
                                           lep[:, k, 0:N - 1], ALU.mult, ALU.add).then_inc(SD.sem, 1)
            if t == 15:
                eng.wait_ge(m_full, M_SELF * b + 6)
                v.tensor_tensor(xr, xr, MB[:], ALU.add).then_inc(SD.sem, 1)

        def self_act(eng, b, par, t, prev):
            if t == 3:
                eng.wait_ge(m_full, M_SELF * b + 1)
                reach(eng, m_full, M_SELF * (b - 1) + 4)
                a.activation(xnT[:].rearrange("p k n -> p (k n)"), MB[:], ACT.Copy).then_inc(SA.sem, 1)
            for tt in range(T):
                if t == 5 + 2 * tt:
                    SD.wait(eng, f"z{tt}", b)
                    a.activation(ez[:, tt, :], z[:, tt, :], ACT.Exp, bias=minus1[:]).then_inc(SA.sem, 1)
            if t == 11:
                eng.wait_ge(m_full, M_SELF * b + 5)
                if prev:
                    SD.wait(eng, "lep_after1", b - 1)
                a.activation(vTs[:].rearrange("p k n -> p (k n)"), MB[:], ACT.Copy).then_inc(SA.sem, 1)
            if t == 12:
                SA.wait(eng, "vT", b)
                for k in range(K2):
                    a.activation(lep[:, k, :], vTs[:, k, :], ACT.Identity, scale=wl_sb[:, k, 1:2],
                                 bias=bl_sb[:, k:k + 1]).then_inc(SA.sem, 1)

        def self_pe(eng, b, par, t, prev):
            if t == 2:
                if prev:
                    SD.wait(eng, "lep_added", b - 1)
                SD.wait(eng, "xn1", b)
                turn4(lambda k, tt: MB[:, k * N + tt * P:k * N + (tt + 1) * P],
                      lambda k, tt: xn[:, tt, k * P:(k + 1) * P]).then_inc(m_full, 1)
            for tt in range(T):
                if t == 4 + 2 * tt:
                    SA.wait(eng, "xnT", b)
                    if tt:
                        SD.wait(eng, "z0", b)
                    for k in range(K2):
                        ins = pe.matmul(MB[:], xnT[:, k, tt * P:(tt + 1) * P], wq_sb[:, k, 0:2 * C],
                                        start=(k == 0), stop=(k == K2 - 1))
                    ins.then_inc(m_full, 1)
            if t == 8:
                SD.wait(eng, "z1", b)
                for tt in range(T):
                    for k in range(K2):
                        ins = pe.matmul(MB[:, tt * C:(tt + 1) * C], xnT[:, k, tt * P:(tt + 1) * P],
                                        wq_sb[:, k, 2 * C:3 * C], start=(k == 0), stop=(k == K2 - 1))
                ins.then_inc(m_full, 1)
            if t == 10:
                SD.wait(eng, "v", b)
                turn4(lambda k, tt: MB[:, k * N + tt * P:k * N + (tt + 1) * P],
                      lambda k, tt: vtok[:, tt, k * P:(k + 1) * P]).then_inc(m_full, 1)
            if t == 14:
                SD.wait(eng, "lep_after1", b)
                SA.wait(eng, "vT", b)
                turn4(lambda tt, k: MB[:, tt * C + k * P:tt * C + (k + 1) * P],
                      lambda tt, k: lep[:, k, tt * P:(tt + 1) * P]).then_inc(m_full, 1)

        def self_pool(eng, b, par, t, prev):
            if t == 0:
                ln_root(SD, eng, b, self_rooted, veps, rstd)
            for tt in range(T):
                s0, pairs = ROTATE[tt], z[:, tt, :].rearrange("p (h e two) -> p h two e", two=2, e=RH)
                for n, (tab, dst) in enumerate(((cos_sb, rc), (sin_sb, rs))):
                    if t == s0 + n:
                        if n == 0:
                            SD.wait(eng, f"elu{tt}", b)
                            reach(eng, SG.sem, SG.done(f"odd{1 - tt}", b - 1 + tt))
                        wide = tab[:, tt, :].unsqueeze(1).to_broadcast([P, 2 * H, RH])
                        for i in range(2):
                            ins = pl.tensor_tensor(dst[:, :, i, :], pairs[:, :, i, :], wide, ALU.mult)
                        ins.then_inc(SG.sem, 1)
                if t == s0 + 2:
                    SG.wait(eng, f"sin{tt}", b)
                    reach(eng, SG.sem, SG.done(f"q{1 - tt}_rest", b - 1 + tt))
                    pl.tensor_tensor(r[:, :, 0:RH], rc[:, :, 0, :], rs[:, :, 1, :], ALU.subtract).then_inc(SG.sem, 1)
                    pl.tensor_tensor(r[:, :, RH:D], rs[:, :, 0, :], rc[:, :, 1, :], ALU.add).then_inc(SG.sem, 1)
                if t == s0 + 3:
                    SG.wait(eng, f"odd{tt}", b)
                    for o in "kq":
                        stack_, heads = STACK[o]
                        split_rest(eng, SD, SG, b, o, tt, r[:, heads, :], stack_[par][:, tt, :, 0:DATA])
                if t == s0 + 4:
                    for o in "kq":
                        split_lo(eng, SD, SG, b, o, tt, STACK[o][0][par][:, tt, :, 0:DATA])

        def sweep(eng, body, peeled, tails):
            for c in range(peeled):
                body(c, c % 2, c)
            with eng.Fori(peeled // 2, B // 2 - 1) as i:
                body(2 * i, 0, peeled)
                body(2 * i + 1, 1, peeled + 1)
            for c in range(B - 2, B + tails):
                body(c, c % 2, c)

        def run_self(eng, core, prep):
            for t in range(H):
                prep(eng, 0, 0, t, False)

            def body(c, par, n):
                for t in range(H):
                    core(c, par, t, n == 0, n >= B)
                    if n < B - 1:
                        prep(eng, c + 1, 1 - par, t, True)
            sweep(eng, body, 2, 1)

        with nc.Block() as block:
            @block.tensor
            def _(eng):
                run_self(eng, lambda c, par, t, first, last: pe_core(
                    eng, c, par, t, lambda e, cc: SG.wait(e, "q1_lo", cc), first, last), self_pe)

            @block.scalar
            def _(eng):
                run_self(eng, lambda c, par, t, first, last: act_core(eng, c, par, t, first, last), self_act)

            @block.vector
            def _(eng):
                run_self(eng, lambda c, par, t, first, last: dve_core(eng, c, par, t, first, last), self_dve)

            @block.gpsimd
            def _(eng):
                run_self(eng, lambda c, par, t, first, last: pool_core(eng, c, par, t, first, last), self_pool)

        s2, pe_core2, act_core2, dve_core2, pool_core2 = core_of("cross")
        m2_full = sem("m2_full")
        cross_rooted = sem("cross_rooted")
        route_rooted = sem("route_rooted")
        CD = Steps(sem("cross_dve"), f"{LN} " + " ".join(f"{o}{t}_{n}" for o in "kq" for t in range(T)
                                                         for n in ("hi", "mid")) + " bias values")
        CG = Steps(sem("cross_pool"), " ".join(f"{o}{t}_{n}" for o in "kq" for t in range(T)
                                               for n in ("rest", "lo")))
        RD = Steps(sem("route_dve"), f"{LN} top_logit esum_inv gates top0 top1 left0 left1 chosen wsum wmax winv "
                                     "wpart weights before0 before1 fits slot val topv0 topv1 index token next")
        RA = Steps(sem("route_act"), "x3T exp0 exp1")
        in_ctx = [sem(f"in_ctx{i}") for i in range(2)]
        rows_st = [sem(f"rows_st{i}") for i in range(2)]
        x3t_st = [sem(f"x3t_st{i}") for i in range(2)]
        scattered = [sem(f"scattered{i}") for i in range(2)]

        def cross_dve(eng, b, par, t, prev):
            xr = xrow(b)
            if t == 0:
                ln_stats(CD, eng, b, [rows_of(xr, tt) for tt in range(T)], stats, mv, veps)
            if t == 1:
                if prev:
                    CG.wait(eng, "q1_rest", b - 1)
                    CD.wait(eng, "q1_hi", b - 1)
                ln_norm(CD, eng, b, cross_rooted, [rows_of(xr, tt) for tt in range(T)], mv, rstd,
                        [xn[:, tt, :] for tt in range(T)])
            for o, tt, src, dst in cross_parts(par):
                if t == CUT[o][tt]:
                    if o == "k" and tt == 0:
                        eng.wait_ge(in_ctx[par], ctx_count(b, par))
                    if o == "q":
                        CD.wait(eng, "xn1", b)
                    reach(eng, s2["kq_turned" if o == "k" else "q_turned"], 8 * (b - 1))
                    split_hi(CD, o, src, dst)
                if t == CUT[o][tt] + 1:
                    split_mid(eng, CD, CG, b, o, tt, dst)
            if t == 11:
                bias = bms[:].rearrange("p b t n -> p (b t n)")[:, bass.ds(b * (3 * T), 3 * T)]\
                    .rearrange("p (t n) -> p t n", t=T)
                v.tensor_copy(ks[par][:, :, :, BIAS:BIAS + 3], bias.unsqueeze(2).to_broadcast([P, T, H, 3]))\
                    .then_inc(CD.sem, 1)
            if t == 14:
                reach(eng, s2["summed"], NG * (b - 1))
                v.tensor_copy(va[par][:, :, :, 0:D], cx[par][:, :, C:2 * C].rearrange("p t (h d) -> p t h d", d=D))\
                    .then_inc(CD.sem, 1)

        CUT = {"k": (2, 4), "q": (6, 8)}

        def cross_parts(par):
            for o, whole, dst in (("k", cx[par], ks[par]), ("q", xn, qs[par])):
                for tt in range(T):
                    yield o, tt, whole[:, tt, 0:C].rearrange("p (h d) -> p h d", d=D), dst[:, tt, :, 0:DATA]

        def cross_pool(eng, b, par, t, prev):
            if t == 0:
                ln_root(CD, eng, b, cross_rooted, veps, rstd)
            for o, tt, src, dst in cross_parts(par):
                if t == CUT[o][tt]:
                    split_rest(eng, CD, CG, b, o, tt, src, dst)
                if t == CUT[o][tt] + 1:
                    split_lo(eng, CD, CG, b, o, tt, dst)

        def ctx_count(b, par):
            return (b - par) * 8 + 16

        def cross_ready(eng, b):
            CD.wait(eng, "values", b)
            CG.wait(eng, "q1_lo", b)

        def route_dve(eng, b, par, t, prev):
            xr, rw = xrow(b), row[par]

            def step(ins):
                ins.then_inc(RD.sem, 1)
            if t == 1:
                eng.wait_ge(s2["attn_added"], NG * b + NG)
                ln_stats(RD, eng, b, [rows_of(xr, tt) for tt in range(T)], stats3, mv3, veps3)
            if t == 2:
                reach(eng, rows_st[par], (b - par) * 8)
                ln_norm(RD, eng, b, route_rooted, [rows_of(xr, tt) for tt in range(T)], mv3, rstd3,
                        [rw[:, tt, 0:C] for tt in range(T)])
            if t == 6:
                eng.wait_ge(m2_full, M_CROSS * b + 2)
                step(v.tensor_reduce(nml[:], MB[:, 0:T * E].rearrange("p (t e) -> p t e", t=T), AX, ALU.max,
                                     negate=True))
            if t == 8:
                RA.wait(eng, "exp1", b)
                step(v.reciprocal(ersum[:], esum[:]))
                RD.wait(eng, "esum_inv", b)
                step(v.tensor_tensor(gates[:], eg[:], ersum[:].unsqueeze(2).to_broadcast([P, T, E]), ALU.mult))
                RD.wait(eng, "gates", b)
                alone(eng)
                for tt in range(T):
                    step(v.max(top[:, tt, :], gates[:, tt, :]))
                for tt in range(T):
                    RD.wait(eng, f"top{tt}", b)
                    alone(eng)
                    step(v.match_replace(left[:, tt, :], top[:, tt, :], gates[:, tt, :], -1.0))
            if t == 9:
                RD.wait(eng, "left1", b)
                step(v.tensor_scalar(chosen[:], left[:], 0.0, None, ALU.is_lt))
                step(v.tensor_reduce(wsum[:], top[:], AX, ALU.add))
                RD.wait(eng, "wsum", b)
                step(v.tensor_scalar(wsum2[:], wsum[:], EPS, None, ALU.max))
                RD.wait(eng, "wmax", b)
                step(v.reciprocal(wr[:], wsum2[:]))
                step(v.tensor_tensor(eg[:], gates[:], chosen[:], ALU.mult))
                RD.wait(eng, "wpart", b)
                step(v.tensor_tensor(rw[:, :, C:ROW], eg[:], wr[:].unsqueeze(2).to_broadcast([P, T, E]), ALU.mult))
            if t == 11:
                eng.wait_ge(m2_full, M_CROSS * b + 3)
                step(v.tensor_tensor(before[:], before[:], chosen[:, 0, :], ALU.add))
                RD.wait(eng, "before0", b)
                step(v.tensor_tensor(before[:], before[:], chosen[:, 1, :], ALU.add))
                rank = MB[:, 0:T * E].rearrange("p (t e) -> p t e", t=T)
                step(v.scalar_tensor_tensor(vd[:], rank, float(CAP), chosen[:], ALU.is_lt, ALU.mult))
                step(v.tensor_tensor(sl[:], ebase[:].unsqueeze(1).to_broadcast([P, T, E]), rank, ALU.subtract))
                RD.wait(eng, "slot", b)
                step(v.tensor_tensor(val[:], sl[:], vd[:], ALU.mult))
                RD.wait(eng, "val", b)
                alone(eng)
                for tt in range(T):
                    step(v.max(topv[:, tt, :], val[:, tt, :]))
            if t == 12:
                reach(eng, scattered[par], (b - par) * 8 * T * TOPK)
                RD.wait(eng, "topv1", b)
                step(v.tensor_scalar(sidx[par][:], topv[:], -1.0, FAR, ALU.mult, ALU.add))
                step(v.tensor_copy(stok[par][:], tok_f[:]))
                RD.wait(eng, "token", b)
                step(v.tensor_scalar(tok_f[:], tok_f[:], float(N), None, ALU.add))

        def route_act(eng, b, par, t, prev):
            if t == 4:
                eng.wait_ge(m2_full, M_CROSS * b + 1)
                reach(eng, x3t_st[par], (b - par) * 8)
                a.activation(x3T[par][:].rearrange("p k n -> p (k n)"), MB[:], ACT.Copy).then_inc(RA.sem, 1)
            if t == 7:
                RD.wait(eng, "top_logit", b)
                for tt in range(T):
                    a.activation(eg[:, tt, :], MB[:, tt * E:(tt + 1) * E], ACT.Exp, bias=nml[:, tt:tt + 1],
                                 accum_out=esum[:, tt:tt + 1]).then_inc(RA.sem, 1)

        def route_pe(eng, b, par, t, prev):
            if t == 3:
                if prev:
                    RD.wait(eng, "slot", b - 1)
                RD.wait(eng, "xn1", b)
                turn4(lambda k, tt: MB[:, k * N + tt * P:k * N + (tt + 1) * P],
                      lambda k, tt: row[par][:, tt, k * P:(k + 1) * P]).then_inc(m2_full, 1)
            if t == 5:
                RA.wait(eng, "x3T", b)
                for tt in range(T):
                    for k in range(K2):
                        ins = pe.matmul(MB[:, tt * E:(tt + 1) * E], x3T[par][:, k, tt * P:(tt + 1) * P],
                                        wg_sb[:, k, :], start=(k == 0), stop=(k == K2 - 1))
                ins.then_inc(m2_full, 1)
            if t == 10:
                RD.wait(eng, "weights", b)
                RA.wait(eng, "exp1", b)
                if prev:
                    RD.wait(eng, "before1", b - 1)
                for tt in range(T):
                    out = MB[:, tt * E:(tt + 1) * E]
                    pe.matmul(out, onesb[:], before[:], start=True, stop=False)
                    if tt:
                        pe.matmul(out, onesb[:], chosen[:, 0, :], start=False, stop=False)
                    ins = pe.matmul(out, lower[:], chosen[:, tt, :], start=False, stop=True)
                ins.then_inc(m2_full, 1)

        def route_pool(eng, b, par, t, prev):
            if t == 1:
                ln_root(RD, eng, b, route_rooted, veps3, rstd3)

        def scatter_pool(eng, b, par, t):
            if t == 0:
                RD.wait(eng, "token", b)
                alone(eng)
            tt, j = t // TOPK, t % TOPK
            pl.indirect_dma_start(out=slot_tok, out_offset=bass.IndirectOffsetOnAxis(ap=sidx[par][:, tt, j:j + 1], axis=0),
                                  in_=stok[par][:, tt:tt + 1], in_offset=None, bounds_check=SLOTS - 1,
                                  oob_is_err=False).then_inc(scattered[par], 16)

        def run_cross(eng, core, prep=None, route=None, scatter=None):
            if prep:
                for t in range(H):
                    prep(eng, 0, 0, t, False)

            def body(c, par, n):
                for t in range(H):
                    if n <= B:
                        core(c, par, t, n == 0, n >= B)
                    if prep and n < B - 1:
                        prep(eng, c + 1, 1 - par, t, True)
                    if route and 2 <= n < B + 2:
                        route(eng, c - 2, par, t, n > 2)
                    if scatter and n >= 3:
                        scatter(eng, c - 3, 1 - par, t)
            sweep(eng, body, 4, 3)

        with nc.Block() as block:
            @block.sync
            def _(eng):
                def load(b, par, prev):
                    if prev:
                        CD.wait(eng, "values", b - 2)
                        CG.wait(eng, "k1_rest", b - 2)
                    eng.dma_start(cx[par][:], ctx_rows(b)).then_inc(in_ctx[par], 16)

                def ctx_rows(b):
                    return ctx_in[bass.ds(b, 1), :, :].rearrange("o (t p) c -> p (o t) c", p=P)

                def store(b, par):
                    RD.wait(eng, "weights", b)
                    eng.dma_start(rows[bass.ds(b * N, N), :].rearrange("(t p) c -> p t c", p=P), row[par][:])\
                        .then_inc(rows_st[par], 16)
                    RA.wait(eng, "x3T", b)
                    alone(eng)
                    eng.dma_start(xt_dram[:, :, bass.ds(b * N, N)], x3T[par][:]).then_inc(x3t_st[par], 16)

                load(0, 0, False)
                load(1, 1, False)

                def body(c, par, n):
                    if n < B - 2:
                        load(c + 2, par, True)
                    if 2 <= n < B + 2:
                        store(c - 2, par)
                sweep(eng, body, 4, 2)
                for par in range(2):
                    eng.wait_ge(rows_st[par], 8 * B)
                    eng.wait_ge(x3t_st[par], 8 * B)

            @block.tensor
            def _(eng):
                run_cross(eng, lambda c, par, t, first, last: pe_core2(
                    eng, c, par, t, cross_ready, first, last), None, route_pe)

            @block.scalar
            def _(eng):
                run_cross(eng, lambda c, par, t, first, last: act_core2(eng, c, par, t, first, last), None, route_act)

            @block.vector
            def _(eng):
                run_cross(eng, lambda c, par, t, first, last: dve_core2(eng, c, par, t, first, last),
                          cross_dve, route_dve)

            @block.gpsimd
            def _(eng):
                run_cross(eng, lambda c, par, t, first, last: pool_core2(eng, c, par, t, first, last),
                          cross_pool, route_pool, scatter_pool)
                for par in range(2):
                    eng.wait_ge(scattered[par], 8 * B * T * TOPK)

        attn.close()

        ffn = ExitStack()
        fsb = lambda name, shape, dt=F32: sb(name, shape, dt, ffn)
        w1 = fsb("w1", [P, K2, 2 * FF])
        w2 = fsb("w2", [P, FT, C])
        xc = [fsb(f"xc{i}", [P, K2, CH]) for i in range(2)]
        sg = [fsb(f"sg{i}", [P, CH]) for i in range(2)]
        gT = [fsb(f"gT{i}", [P, FT, CH]) for i in range(2)]
        ys = [fsb(f"ys{i}", [P, CH // P * C]) for i in range(2)]
        in_sw = sem("in_sw")
        in_xc = [sem(f"in_xc{i}") for i in range(2)]
        hid = sem("hid")
        acted = sem("acted")
        gated = sem("gated")
        outed = sem("outed")
        y_made = sem("y_made")
        y_st = [sem(f"y_st{i}") for i in range(2)]
        NCH = NTOK // CH

        with nc.Block() as block:
            def chunks(eng, body, tail=False):
                body(0, 0, False)
                body(1, 1, True)
                with eng.Fori(1, NCH // 2) as i:
                    body(2 * i, 0, True)
                    body(2 * i + 1, 1, True)

            @block.sync
            def _(eng):
                eng.dma_start(w1[:], sw1.rearrange("(k p) n -> p k n", p=P)).then_inc(in_sw, 16)
                eng.dma_start(w2[:], sw2.rearrange("(k p) n -> p k n", p=P)).then_inc(in_sw, 16)

                def load(q, par):
                    reach(eng, hid, FT * (q - 1))
                    eng.dma_start(xc[par][:], xt_dram[:, :, bass.ds(q * CH, CH)]).then_inc(in_xc[par], 16)

                def store(q, par):
                    eng.wait_ge(y_made, 2 * q + 2)
                    eng.dma_start(y[bass.ds(q * CH, CH), :].rearrange("(t p) c -> p t c", p=P),
                                  ys[par][:].rearrange("p (t c) -> p t c", c=C)).then_inc(y_st[par], 16)

                load(0, 0)
                load(1, 1)
                with eng.Fori(1, NCH // 2) as i:
                    load(2 * i, 0)
                    store(2 * i - 2, 0)
                    load(2 * i + 1, 1)
                    store(2 * i - 1, 1)
                store(NCH - 2, 0)
                store(NCH - 1, 1)
                for par in range(2):
                    eng.wait_ge(y_st[par], 8 * NCH)

            @block.tensor
            def _(eng):
                def hidden(q, par, js):
                    for j in js:
                        reach(eng, gated, FT * q + j - 1)
                        for half in range(2):
                            for k in range(K2):
                                f = half * FF + j * P
                                ins = pe.matmul(bank[2 * (j % 2) + half][:], w1[:, k, f:f + P], xc[par][:, k, :],
                                                start=(k == 0), stop=(k == K2 - 1))
                        ins.then_inc(hid, 1)

                def output(q, par):
                    eng.wait_ge(gated, FT * q + FT)
                    reach(eng, y_made, 2 * (q - 1))
                    for tt in range(CH // P):
                        out = bank[4 + 2 * par + tt // 2][:, tt % 2 * C:(tt % 2 + 1) * C]
                        for j in range(FT):
                            ins = pe.matmul(out, gT[par][:, j, tt * P:(tt + 1) * P], w2[:, j, :],
                                            start=(j == 0), stop=(j == FT - 1))
                        if tt % 2:
                            ins.then_inc(outed, 1)

                def body(q, par, prev):
                    eng.wait_ge(in_xc[par], (q - par) * 8 + 16)
                    hidden(q, par, range(2))
                    if prev:
                        output(q - 1, 1 - par)
                    hidden(q, par, range(2, FT))
                eng.wait_ge(in_sw, 32)
                chunks(eng, body)
                output(NCH - 1, 1)

            @block.scalar
            def _(eng):
                def body(q, par, prev):
                    for j in range(FT):
                        eng.wait_ge(hid, FT * q + j + 1)
                        reach(eng, gated, FT * q + j - 1)
                        a.activation(sg[j % 2][:], bank[2 * (j % 2) + 1][:], ACT.Silu).then_inc(acted, 1)
                chunks(eng, body)

            @block.vector
            def _(eng):
                def finish(q, par):
                    reach(eng, y_st[par], (q - par) * 8)
                    for i in range(2):
                        eng.wait_ge(outed, 2 * q + i + 1)
                        v.tensor_tensor(ys[par][:, i * 2 * C:(i + 1) * 2 * C], bank[4 + 2 * par + i][:],
                                        X[:, bass.ds(q * (CH // P * C) + i * 2 * C, 2 * C)], ALU.add)\
                            .then_inc(y_made, 1)

                def body(q, par, prev):
                    for j in range(FT):
                        eng.wait_ge(acted, FT * q + j + 1)
                        reach(eng, outed, 2 * (q - 1))
                        v.tensor_tensor(gT[par][:, j, :], bank[2 * (j % 2)][:], sg[j % 2][:], ALU.mult)\
                            .then_inc(gated, 1)
                        if j == 2 and prev:
                            finish(q - 1, 1 - par)
                chunks(eng, body)
                finish(NCH - 1, 1)

        RING = 4
        idx = [fsb(f"idx{i}", [HC, 2], I32) for i in range(RING)]
        xg = [fsb(f"xg{i}", [HC, 2, ROW]) for i in range(RING)]
        xgT = [fsb(f"xgT{i}", [P, K2, CAP]) for i in range(2)]
        sge = [fsb(f"sge{i}", [P, FT // 2 * CAP]) for i in range(2)]
        gTe = [fsb(f"gTe{i}", [P, FT * CAP]) for i in range(2)]
        yse = [fsb(f"yse{i}", [HC, 2, C]) for i in range(2)]
        in_idx = [sem(f"in_idx{i}") for i in range(RING)]
        fetched = [sem(f"fetched{i}") for i in range(RING)]
        added = [sem(f"added{i}") for i in range(2)]
        e_turned, e_copied, e_hid, e_acted, e_gated, e_out, e_scaled = (sem(n) for n in (
            "e_turned", "e_copied", "e_hid", "e_acted", "e_gated", "e_out", "e_scaled"))
        HALF = FT // 2 * CAP

        with nc.Block() as block:
            def experts(eng, body):
                for e in range(RING):
                    body(e, e, e)
                with eng.Fori(1, E // RING - 1) as i:
                    for k in range(RING):
                        body(RING * i + k, k, RING + k)
                for e in range(E - RING, E):
                    body(e, e % RING, e)

            def uses(e, k):
                return (e - k) * (16 // RING) + 16

            @block.sync
            def _(eng):
                names = slot_tok.rearrange("(e p c) o -> e p (c o)", c=2, p=HC)

                def load_idx(e, k):
                    reach(eng, added[k % 2], (e - k % 2) * 16 - 16 * RING + 32)
                    eng.dma_start(idx[k][:], names[bass.ds(e, 1), :, :].rearrange("o p c -> p (o c)"))\
                        .then_inc(in_idx[k], 16)

                def body(e, k, n):
                    if n < E - 2:
                        load_idx(e + 2, (k + 2) % RING)
                    if n >= 2:
                        reach(eng, e_out, e - 1)
                        eng.dma_start(ew_sb[k % 2][:], ew[bass.ds(e, 1), :, :].rearrange("o p n -> p (o n)"))\
                            .then_inc(loaded_ew[k % 2], 16)
                load_idx(0, 0)
                load_idx(1, 1)
                experts(eng, body)

            @block.gpsimd
            def _(eng):
                def fetch(e, k):
                    eng.wait_ge(in_idx[k], uses(e, k))
                    reach(eng, e_scaled, e - RING + 1)
                    alone(eng)
                    for c in range(2):
                        pl.indirect_dma_start(out=xg[k][:, c, :], out_offset=None, in_=rows,
                                              in_offset=bass.IndirectOffsetOnAxis(ap=idx[k][:, c:c + 1].bitcast(U32), axis=0))\
                            .then_inc(fetched[k], 16)

                def body(e, k, n):
                    par = k % 2
                    if n < E - 2:
                        fetch(e + 2, (k + 2) % RING)
                    eng.wait_ge(e_scaled, e + 1)
                    if n >= 1:
                        eng.wait_ge(added[1 - par], (e + par) * 16)
                    alone(eng)
                    for c in range(2):
                        pl.indirect_dma_start(out=y, out_offset=bass.IndirectOffsetOnAxis(ap=idx[k][:, c:c + 1].bitcast(U32), axis=0),
                                              in_=yse[par][:, c, :], in_offset=None, compute_op=ALU.add)\
                            .then_inc(added[par], 16)
                fetch(0, 0)
                fetch(1, 1)
                experts(eng, body)
                for par in range(2):
                    eng.wait_ge(added[par], 16 * E)

            @block.tensor
            def _(eng):
                TB = bank[4]

                def turn(e, k4):
                    eng.wait_ge(fetched[k4], 2 * uses(e, k4))
                    reach(eng, e_copied, e)
                    for k in range(K2):
                        for c in range(2):
                            ins = pe.transpose(TB[:, k * CAP + c * HC:k * CAP + (c + 1) * HC],
                                               xg[k4][:, c, k * P:(k + 1) * P], ident[0:HC, 0:HC])
                    ins.then_inc(e_turned, 1)

                def body(e, k4, n):
                    par = k4 % 2
                    wa = ew_sb[par][:, 0:2 * K2 * FF].rearrange("p (k f) -> p k f", k=K2)
                    wb = ew_sb[par][:, 2 * K2 * FF:].rearrange("p (j c) -> p j c", c=C)
                    eng.wait_ge(loaded_ew[par], (e - par) * 8 + 16)
                    eng.wait_ge(e_copied, e + 1)
                    for half in range(2):
                        reach(eng, e_gated, 2 * e + half - 1)
                        for side in range(2):
                            for j in range(FT // 2):
                                f = side * FF + (half * (FT // 2) + j) * P
                                for k in range(K2):
                                    ins = pe.matmul(bank[2 * half + side][:, j * CAP:(j + 1) * CAP],
                                                    wa[:, k, f:f + P], xgT[par][:, k, :],
                                                    start=(k == 0), stop=(k == K2 - 1))
                        ins.then_inc(e_hid, 1)
                    if n < E - 1:
                        turn(e + 1, (k4 + 1) % RING)
                    reach(eng, e_scaled, e - 1)
                    for c in range(2):
                        for j in range(FT):
                            if c == 0 and j % (FT // 2) == 0:
                                eng.wait_ge(e_gated, 2 * e + j // (FT // 2) + 1)
                            ins = pe.matmul(bank[5 + par][0:HC, c * C:(c + 1) * C],
                                            gTe[par][:, j * CAP + c * HC:j * CAP + (c + 1) * HC], wb[:, j, :],
                                            start=(j == 0), stop=(j == FT - 1))
                    ins.then_inc(e_out, 1)
                turn(0, 0)
                experts(eng, body)

            @block.scalar
            def _(eng):
                def copy(e, par):
                    eng.wait_ge(e_turned, e + 1)
                    reach(eng, e_hid, 2 * (e - 1))
                    a.activation(xgT[par][:].rearrange("p k n -> p (k n)"), bank[4][:, 0:K2 * CAP], ACT.Copy)\
                        .then_inc(e_copied, 1)

                def body(e, k4, n):
                    par = k4 % 2
                    for half in range(2):
                        eng.wait_ge(e_hid, 2 * e + half + 1)
                        reach(eng, e_gated, 2 * e + half - 1)
                        a.activation(sge[half][:], bank[2 * half + 1][:, 0:HALF], ACT.Silu).then_inc(e_acted, 1)
                    if n < E - 1:
                        copy(e + 1, 1 - par)
                copy(0, 0)
                experts(eng, body)

            @block.vector
            def _(eng):
                def body(e, k4, n):
                    par = k4 % 2
                    for half in range(2):
                        eng.wait_ge(e_acted, 2 * e + half + 1)
                        reach(eng, e_out, e - 1)
                        v.tensor_tensor(gTe[par][:, half * HALF:(half + 1) * HALF], bank[2 * half][:, 0:HALF],
                                        sge[half][:], ALU.mult).then_inc(e_gated, 1)
                    eng.wait_ge(e_out, e + 1)
                    reach(eng, added[par], (e - par) * 16)
                    for c in range(2):
                        ins = v.tensor_scalar(yse[par][:, c, :], bank[5 + par][0:HC, c * C:(c + 1) * C],
                                              xg[k4][:, c, bass.ds(e + C, 1)], None, ALU.mult)
                    ins.then_inc(e_scaled, 1)
                experts(eng, body)
        ffn.close()


_INPUTS = ["x", "ctx_2048", "itok_Bx1_68_817", "w_qkv", "b_qkv", "w_lepe", "b_lepe", "xb", "wg", "sw1", "sw2",
           "ew", "cos_t", "sin_t"]


def rope_tables():
    position = np.arange(N, dtype=np.float32)[:, None]
    rate = np.exp(np.arange(0, D, 2, dtype=np.float32) * np.float32(-np.log(10000.0) / D))
    angle = position * rate.astype(np.float32)
    return np.cos(angle), np.sin(angle)


def kernel(**inputs):
    import concourse.bacc as bacc
    from concourse.bass_utils import run_bass_kernel_spmd

    g = {k: np.asarray(v) for k, v in inputs.items()}
    cos_t, sin_t = rope_tables()
    first = g["L0_ffn_expert_w1"].transpose(0, 2, 1).reshape(E, K2, P, 2 * FF).transpose(0, 2, 1, 3)
    second = g["L0_ffn_expert_w2"].transpose(0, 2, 1).reshape(E, FT, P, C).transpose(0, 2, 1, 3)
    arrays = {
        "x": g["x"], "ctx_2048": g["ctx_2048"], "itok_Bx1_68_817": g["itok_Bx1_68_817"],
        "w_qkv": g["L0_attn_w_qkv"].T, "b_qkv": g["L0_attn_b_qkv"],
        "w_lepe": g["L0_attn_w_lepe"].reshape(C, 3), "b_lepe": g["L0_attn_b_lepe"].reshape(K2, P).T,
        "xb": g["L0_xattn_b"].reshape(T, P).T,
        "wg": g["L0_ffn_wg"].T, "sw1": g["L0_ffn_shared_w1"].T, "sw2": g["L0_ffn_shared_w2"].T,
        "ew": np.concatenate([first.reshape(E, P, -1), second.reshape(E, P, -1)], axis=2),
        "cos_t": cos_t, "sin_t": sin_t,
    }
    nc = bacc.Bacc("TRN2", target_bir_lowering=False, num_devices=1)
    args, sent = [], {}
    for name in _INPUTS:
        sent[f"in_{name}"] = np.ascontiguousarray(arrays[name])
        args.append(nc.dram_tensor(f"in_{name}", sent[f"in_{name}"].shape, mybir.dt.from_np(sent[f"in_{name}"].dtype),
                                   kind="ExternalInput").ap())
    args.append(nc.dram_tensor("out", (ROWS, C), F32, kind="ExternalOutput").ap())
    decoder_layer(nc, *args)
    result = run_bass_kernel_spmd(nc, [sent], core_ids=[0])
    return result.results[0]["out"][:NTOK].reshape(B, N, C)
```

```python
from contextlib import ExitStack

import concourse.bass as bass
import numpy as np
from concourse import mybir

P = 128
B, N, C = 16, 256, 256
H = 16
D = C // H
T = N // P
K2 = C // P
TERMS = 6
DATA = TERMS * D
BIAS = DATA
TOP = DATA + 3
W = DATA + 6
G = 4
NG = H // G
VW = 32
RH = D // 2

E, TOPK, CAP, FF = 64, 8, 160, 768
FT = FF // P
HC = CAP // 2
SLOTS = E * CAP
ROW = C + E
NTOK = B * N
ROWS = NTOK + CAP
FAR = 16384.0
MASK = -1.0e12
EPS_LN = 1.0e-5
EPS = float(np.finfo(np.float32).eps)
CH = 512

F32, F32R, BF16, I32, U32 = mybir.dt.float32, mybir.dt.float32r, mybir.dt.bfloat16, mybir.dt.int32, mybir.dt.uint32
ALU = mybir.AluOpType
ACT = mybir.ActivationFunctionType
AX = mybir.AxisListType.X

Q_HI, Q_MID, Q_LO = (0, 6, 2), (1, 5, 2), (5, 6, 1)
K_HI, K_MID, K_LO = (3, 6, 1), (0, 2, 1), (2, 3, 1)


def reach(eng, sem, value):
    if isinstance(value, int) and value <= 0:
        return
    eng.wait_ge(sem, value)


class Steps:

    def __init__(self, sem, names):
        self.sem, self.names = sem, names.split()

    def done(self, name, b):
        return b * len(self.names) + self.names.index(name) + 1

    def wait(self, eng, name, b):
        reach(eng, self.sem, self.done(name, b))


def decoder_layer(nc, x, ctx_in, itok, w_qkv, b_qkv, w_lepe, b_lepe, xb, wg, sw, ew, cos_t,
                  sin_t, y):
    v, a, pl, pe, sp = nc.vector, nc.scalar, nc.gpsimd, nc.tensor, nc.sync
    slot_tok = nc.dram_tensor("slot_tok", (SLOTS, 1), I32, kind="Internal").ap()
    rows = nc.dram_tensor("rows", (ROWS, ROW), F32, kind="Internal").ap()
    xt_dram = nc.dram_tensor("xt_dram", (P, K2, NTOK), F32, kind="Internal").ap()

    stack = ExitStack()
    with stack:
        def sb(name, shape, dt=F32, scope=stack):
            return scope.enter_context(nc.sbuf_tensor(name, shape, dt))

        def sem(name):
            return stack.enter_context(nc.semaphore(name))

        bank = [stack.enter_context(nc.psum_tensor(f"bank{i}", [P, 512], F32)) for i in range(8)]

        X = sb("X", [P, B * T * C])
        ident = sb("ident", [P, P])
        identb = sb("identb", [P, P], BF16)
        ew_sb = [sb(f"ew{i}", [P, 2 * K2 * FF + FT * C]) for i in range(2)]
        xc = [sb(f"xc{i}", [P, K2, CH]) for i in range(2)]
        in_xc = [sem(f"in_xc{i}") for i in range(2)]
        sidx = [sb(f"sidx{i}", [P, TOPK], U32) for i in range(2)]
        stok = [sb(f"stok{i}", [P, 1], I32) for i in range(2)]
        late_idx = sb("late_idx", [P, B * TOPK], U32)
        late_tok = sb("late_tok", [P, B], I32)
        loaded_ew = [sem(f"loaded_ew{i}") for i in range(2)]

        def expert_weights(i):
            return (ew_sb[i][:, 0:2 * K2 * FF].rearrange("p (k f) -> p k f", k=K2),
                    ew_sb[i][:, 2 * K2 * FF:].rearrange("p (j c) -> p j c", c=C))

        def xrow(b):
            return X[:, bass.ds(b * (T * C), T * C)]

        attn = ExitStack()
        asb = lambda name, shape, dt=F32: sb(name, shape, dt, attn)
        wg_sb = asb("wg_sb", [P, K2, E])
        xb_sb = asb("xb_sb", [P, T])
        seq_i = asb("seq_i", [P, B], I32)
        seq_f = asb("seq_f", [P, B])
        keyed = asb("keyed", [P, B])
        root = asb("root", [P, T])
        pos_i = asb("pos_i", [P, T], I32)
        pos_f = asb("pos_f", [P, T])
        minus1 = asb("minus1", [P, 1])
        mhalf = asb("mhalf", [P, T])
        bm = asb("bm", [P, B, T])
        bmr = asb("bmr", [P, B, T])
        bms = asb("bms", [P, B, T, 3], BF16)
        lower = asb("lower", [P, P], BF16)
        onesb = asb("onesb", [P, P], BF16)
        onesf = asb("onesf", [P, P])
        init_i = asb("init_i", [E, CAP], I32)
        zrow = asb("zrow", [HC, 2, ROW])
        ebase = asb("ebase", [P, E])
        ebase_i = asb("ebase_i", [P, E], I32)
        tok_f = asb("tok_f", [P, T])
        tok_i = asb("tok_i", [P, T], I32)
        before = asb("before", [P, E], BF16)

        ks = [asb(f"ks{i}", [P, T, H, W], BF16) for i in range(2)]
        qs = [asb(f"qs{i}", [P, T, H, W], BF16) for i in range(2)]
        va = [asb(f"va{i}", [P, T, H, VW]) for i in range(2)]
        kT = [asb(f"kT{i}", [W, H, N], BF16) for i in range(2)]
        qT = asb("qT", [TOP, H, N], BF16)
        q2 = [asb(f"q2_{i}", [W, 2 * N], BF16) for i in range(2)]
        ex = asb("ex", [P, 2 * G, T * N])
        oT = [asb(f"oT{i}", [P, N]) for i in range(2)]
        nm = asb("nm", [P, T, H])
        nmr = asb("nmr", [P, T, 2])
        rden = asb("rden", [P, T * G])
        otmp = asb("otmp", [P, T, G * D])

        stats = asb("stats", [P, T, 6])
        mv = asb("mv", [P, T, 2])
        rstd = asb("rstd", [P, T])
        veps = asb("veps", [P, T])
        xn = asb("xn", [P, T, C])
        rem = {(o, tt): asb(f"rem_{o}{tt}", [P, H, D]) for o in "kq" for tt in range(T)}

        own = ExitStack()
        osb = lambda name, shape, dt=F32: sb(name, shape, dt, own)
        bl_sb = osb("bl_sb", [P, K2])
        wl_sb = osb("wl_sb", [P, K2, 3])
        sin_sb = osb("sin_sb", [P, T, RH])
        cos_sb = osb("cos_sb", [P, T, RH])
        bq_sb = osb("bq_sb", [P, 3 * C])
        wq_sb = osb("wq_sb", [P, K2, 3 * C])
        xnT = osb("xnT", [P, K2, N])
        z = osb("z", [P, T, 2 * C])
        ez = osb("ez", [P, T, 2 * C])
        rc = osb("rc", [P, 2 * H, 2, RH])
        rs = osb("rs", [P, 2 * H, 2, RH])
        r = [osb(f"r{tt}", [P, 2 * H, D]) for tt in range(T)]
        lep = osb("lep", [P, K2, N])
        vtok = osb("vtok", [P, T, C])
        vTs = osb("vTs", [P, K2, N])
        in_w = sem("in_w")
        in_x = [sem(f"in_x{i}") for i in range(2)]
        in_sw = sem("in_sw")
        SOON = 3
        SHARED = 1
        init_st = sem("init_st")
        set_pool = sem("set_pool")
        set_dve = sem("set_dve")

        passed = {}

        def alone(eng):
            name = str(eng.engine).split(".")[-1]
            if name not in passed:
                passed[name] = sem(f"passed_{name}")
            eng.sem_inc(passed[name], 1)

        with nc.Block() as block:
            NW = 10

            @block.sync
            def _(eng):
                for dst, src in (
                    (wq_sb[:], w_qkv.rearrange("(k p) n -> p k n", p=P)),
                    (wg_sb[:], wg.rearrange("(k p) n -> p k n", p=P)),
                    (bq_sb[:], b_qkv.partition_broadcast(P)),
                    (cos_sb[:], cos_t.rearrange("(t p) n -> p t n", p=P)),
                    (sin_sb[:], sin_t.rearrange("(t p) n -> p t n", p=P)),
                    (wl_sb[:], w_lepe.rearrange("(k p) n -> p k n", p=P)),
                    (bl_sb[:], b_lepe),
                    (xb_sb[:], xb),
                    (seq_i[:], itok.rearrange("b o -> (b o)").partition_broadcast(P)),
                ):
                    eng.dma_start(dst, src).then_inc(in_w, 16)
                for part, (b0, b1) in enumerate(((0, SOON), (SOON, B))):
                    eng.dma_start(X[:].rearrange("p (b t c) -> p b t c", b=B, t=T)[:, b0:b1],
                                  x[b0:b1].rearrange("b (t p) c -> p b t c", p=P)).then_inc(in_x[part], 16)
                eng.dma_start(ew_sb[SHARED][:], sw).then_inc(in_sw, 16)
                eng.dma_start(ew_sb[0][:], ew[0]).then_inc(loaded_ew[0], 16)
                eng.wait_ge(set_pool, 12)
                eng.dma_start(slot_tok.rearrange("(e s) o -> e (s o)", e=E), init_i[:]).then_inc(init_st, 16)
                eng.dma_start(rows[NTOK:ROWS, :].rearrange("(p a) n -> p a n", a=2), zrow[:]).then_inc(init_st, 16)
                eng.dma_start(y[NTOK:ROWS, :].rearrange("(p a) n -> p a n", a=2), zrow[:, :, 0:C]).then_inc(init_st, 16)
                eng.wait_ge(in_w, 16 * 9)
                eng.wait_ge(in_x[0], 16)

            @block.gpsimd
            def _(eng):
                pl.memset(ident[:], 0.0).then_inc(set_pool, 1)
                pl.memset(onesf[:], 1.0).then_inc(set_pool, 1)
                pl.memset(zrow[:], 0.0).then_inc(set_pool, 1)
                pl.memset(before[:], 0.0).then_inc(set_pool, 1)
                pl.memset(minus1[:], -1.0).then_inc(set_pool, 1)
                pl.memset(mhalf[:], -0.5).then_inc(set_pool, 1)
                eng.wait_ge(set_pool, 2)
                pl.affine_select(out=ident[:], in_=ident[:], compare_op=ALU.not_equal, fill=1.0, base=0,
                                 pattern=[[-1, P]], channel_multiplier=1).then_inc(set_pool, 1)
                pl.affine_select(out=onesf[:], in_=onesf[:], compare_op=ALU.is_gt, fill=0.0, base=0,
                                 pattern=[[1, P]], channel_multiplier=-1).then_inc(set_pool, 1)
                pl.iota(pos_i[:], pattern=[[P, T]], base=0, channel_multiplier=1).then_inc(set_pool, 1)
                pl.iota(init_i[:], pattern=[[1, CAP]], base=NTOK, channel_multiplier=0).then_inc(set_pool, 1)
                pl.iota(ebase_i[:], pattern=[[-CAP, E]], base=int(FAR), channel_multiplier=0)\
                    .then_inc(set_pool, 1)
                pl.memset(onesb[:], 1.0).then_inc(set_pool, 1)

            @block.vector
            def _(eng):
                def step(ins):
                    ins.then_inc(set_dve, 1)

                for i in range(2):
                    step(v.memset(qs[i][:, :, :, BIAS:BIAS + 3], 1.0))
                    step(v.memset(ks[i][:, :, :, BIAS:BIAS + 3], 0.0))
                    step(v.memset(ks[i][:, :, :, TOP:TOP + 3], 1.0))
                    step(v.memset(va[i][:], 0.0))
                eng.wait_ge(set_dve, 8)
                for i in range(2):
                    step(v.memset(va[i][:, :, :, D:D + 1], 1.0))
                eng.wait_ge(set_pool, 12)
                step(v.tensor_copy(identb[:], ident[:]))
                step(v.tensor_copy(lower[:], onesf[:]))
                step(v.tensor_copy(pos_f[:], pos_i[:]))
                step(v.tensor_copy(tok_f[:], pos_i[:]))
                step(v.tensor_copy(ebase[:], ebase_i[:]))
                eng.wait_ge(in_w, 16 * 9)
                step(v.tensor_scalar(bq_sb[:, 0:2 * C], bq_sb[:, 0:2 * C], 1.0, None, ALU.add))
                step(v.tensor_copy(seq_f[:], seq_i[:]))
                eng.wait_ge(set_dve, 17)
                for t in range(T):
                    step(v.tensor_scalar(bm[:, :, t], seq_f[:], pos_f[:, t:t + 1], None, ALU.is_gt))
                eng.wait_ge(set_dve, 19)
                for t in range(T):
                    step(v.tensor_scalar(bmr[:, :, t], bm[:, :, t], -MASK, MASK, ALU.mult, ALU.add))
                eng.wait_ge(set_dve, 21)
                for t in range(T):
                    step(v.tensor_scalar(bm[:, :, t], bmr[:, :, t], xb_sb[:, t:t + 1], 1.0 / D ** -0.5,
                                         ALU.add, ALU.mult))
                eng.wait_ge(set_dve, 23)
                step(v.tensor_copy(bms[:, :, :, 0], bm[:]))
                eng.wait_ge(set_dve, 24)
                step(v.tensor_tensor(bmr[:], bm[:], bms[:, :, :, 0], ALU.subtract))
                eng.wait_ge(set_dve, 25)
                step(v.tensor_copy(bms[:, :, :, 1], bmr[:]))
                eng.wait_ge(set_dve, 26)
                step(v.tensor_tensor(bms[:, :, :, 2], bmr[:], bms[:, :, :, 1], ALU.subtract))
                step(v.tensor_scalar(keyed[:], seq_f[:], 0.0, None, ALU.is_gt))
                eng.wait_ge(set_dve, 28)

        TURN, SCORE, RETURN, RESCORE, SUM = (2, 4), 6, 11, 13, 18

        def core_of(kind):
            s = {n: sem(f"{kind}_{n}") for n in (
                "kq_turned", "kq_copied", "scored", "max_found", "max_split", "split_chain", "q_turned", "q_copied",
                "rescored", "exp_done", "valued", "summed", "sum_copied", "sum_turned", "sum_used", "attn_added", "attn_chain")}
            XB, YB, ZB = bank[4], bank[5], bank[6]
            xb16, yb16 = XB[:].bitcast(BF16), YB[:].bitcast(BF16)

            def lagged(c, t, n, lag, every, size):
                d = t - lag
                if d % every:
                    return None
                u, back = d // every, 0
                while u < 0:
                    u, back = u + size, back + 1
                return (c - back, u, back) if 0 <= n - back < B else None

            def upper(x):
                return x[:].bitcast(BF16).rearrange("p t (h two) -> p t h two", two=2)[:, :, :, 1]

            def pe_step(eng, c, par, t, n, ready):
                def unit(lag, every, size):
                    return lagged(c, t, n, lag, every, size)

                if got := unit(SCORE, 1, H):
                    cc, h, back = got
                    reach(eng, s["kq_copied"], 8 * cc + 2 * (h // G) + 2)
                    reach(eng, s["max_found"], 16 * cc + h - 1)
                    for tt in range(T):
                        ins = pe.matmul(bank[h % 2][:, tt * N:(tt + 1) * N], qT[0:TOP, h, tt * P:(tt + 1) * P],
                                        kT[(par + back) % 2][0:TOP, h, :], start=True, stop=True)
                    ins.then_inc(s["scored"], 1)
                for first, (src, width) in enumerate(((ks, W), (qs, TOP))):
                    if got := unit(TURN[first], 4, NG):
                        cc, u, back = got
                        if u == 0 and first == 0:
                            ready(eng, cc)
                        reach(eng, s["kq_copied"], 8 * cc + 2 * u + first)
                        for h in range(G):
                            for tt in range(T):
                                ins = pe.transpose(xb16[0:width, (h * T + tt) * P:(h * T + tt + 1) * P],
                                                   src[(par + back) % 2][:, tt, u * G + h, 0:width], identb[:])
                        ins.then_inc(s["kq_turned"], 1)
                if got := unit(RESCORE, 1, H):
                    cc, h, back = got
                    reach(eng, s["q_copied"], 8 * cc + h // 2 + 1)
                    reach(eng, s["exp_done"], 16 * cc + h - 1)
                    for tt in range(T):
                        ins = pe.matmul(bank[2 + h % 2][:, tt * N:(tt + 1) * N], kT[(par + back) % 2][0:W, h, tt * P:(tt + 1) * P],
                                        q2[h // 2 % 2][0:W, (h % 2) * N:(h % 2 + 1) * N], start=True, stop=True)
                    ins.then_inc(s["rescored"], 1)
                if got := unit(RETURN, 2, H // 2):
                    cc, p, back = got
                    src = qs[(par + back) % 2]
                    eng.wait_ge(s["max_split"], 8 * cc + p + 1)
                    reach(eng, s["q_copied"], 8 * cc + p)
                    for h in range(2):
                        for tt in range(T):
                            ins = pe.transpose(yb16[0:W, (h * T + tt) * P:(h * T + tt + 1) * P],
                                               src[:, tt, 2 * p + h, 0:W], identb[:])
                    ins.then_inc(s["q_turned"], 1)
                if got := unit(SUM, 4, NG):
                    cc, g, back = got
                    vv = va[(par + back) % 2]
                    eng.wait_ge(s["valued"], cc + 1)
                    eng.wait_ge(s["exp_done"], 16 * cc + G * g + G)
                    reach(eng, s["sum_used"], 4 * cc + g)
                    for tt in range(T):
                        for j in range(G):
                            h = g * G + j
                            ins = pe.matmul(ZB[32 * j:32 * j + VW, 0:N], vv[:, tt, h, :],
                                            ex[:, h % (2 * G), tt * N:(tt + 1) * N],
                                            start=(tt == 0), stop=(tt == T - 1))
                    ins.then_inc(s["summed"], 1)
                if got := unit(SUM + 2, 4, NG):
                    cc, g, _ = got
                    eng.wait_ge(s["sum_copied"], 4 * cc + g + 1)
                    for tt in range(T):
                        ins = pe.transpose(ZB[:, N + tt * P:N + (tt + 1) * P], oT[g % 2][:, tt * P:(tt + 1) * P],
                                           ident[:])
                    ins.then_inc(s["sum_turned"], 1)

            def act_step(eng, c, par, t, n):
                def unit(lag, every, size):
                    return lagged(c, t, n, lag, every, size)

                for first in range(2):
                    if got := unit(TURN[first], 4, NG):
                        cc, u, back = got
                        dst, width, read, last = ((kT[(par + back) % 2], W, "rescored", cc - 2),
                                                  (qT, TOP, "scored", cc - 1))[first]
                        eng.wait_ge(s["kq_turned"], 8 * cc + 2 * u + first + 1)
                        reach(eng, s[read], 16 * last + G * u + G)
                        a.activation(dst[0:width, u * G:(u + 1) * G, :],
                                     xb16[0:width, :].rearrange("p (h n) -> p h n", h=G), ACT.Copy)\
                            .then_inc(s["kq_copied"], 1)
                if got := unit(SUM + 1, 4, NG):
                    cc, g, _ = got
                    eng.wait_ge(s["summed"], 4 * cc + g + 1)
                    reach(eng, s["sum_turned"], 4 * cc + g - 1)
                    a.activation(oT[g % 2][:], ZB[:, 0:N], ACT.Copy).then_inc(s["sum_copied"], 1)
                if got := unit(RESCORE, 1, H):
                    cc, h, _ = got
                    eng.wait_ge(s["rescored"], 16 * cc + h + 1)
                    reach(eng, s["summed"], 4 * cc + h // G - 1)
                    a.activation(ex[:, h % (2 * G), :], bank[2 + h % 2][:], ACT.Exp, scale=float(D) ** -0.5)\
                        .then_inc(s["exp_done"], 1)

            def dve_step(eng, c, par, t, n, values):
                def unit(lag, every, size):
                    return lagged(c, t, n, lag, every, size)

                if got := unit(SUM + 3, 4, NG):
                    cc, g, _ = got
                    zo = ZB[:, N:2 * N].rearrange("p (u d) -> p u d", d=VW)
                    eng.wait_ge(s["sum_turned"], 4 * cc + g + 1)
                    reach(eng, s["sum_used"], 4 * cc + g)
                    v.reciprocal(rden[:], zo[:, :, D]).then_inc(s["attn_chain"], 1)
                if pair := unit(RETURN + 1, 2, H // 2):
                    cc, p, _ = pair
                    eng.wait_ge(s["q_turned"], 8 * cc + p + 1)
                    reach(eng, s["rescored"], 16 * cc + 2 * p - 2)
                    v.tensor_copy(q2[p % 2][:], yb16[0:W, 0:2 * N]).then_inc(s["q_copied"], 1)
                if taken_in := unit(SUM + 4, 4, NG):
                    cc, g, _ = taken_in
                    eng.wait_ge(s["sum_used"], 4 * cc + g + 1)
                    xg = xrow(cc).rearrange("p (t c) -> p t c", t=T)[:, :, g * G * D:(g + 1) * G * D]
                    v.tensor_tensor(xg, xg, otmp[:], ALU.add).then_inc(s["attn_added"], 1)
                if score := unit(SCORE, 1, H):
                    cc, h, _ = score
                    eng.wait_ge(s["scored"], 16 * cc + h + 1)
                    v.tensor_reduce(nm[:, :, h], bank[h % 2][:].rearrange("p (t n) -> p t n", t=T), AX, ALU.max,
                                    negate=True).then_inc(s["max_found"], 1)
                if got:
                    eng.wait_ge(s["attn_chain"], 4 * got[0] + got[1] + 1)
                    reach(eng, s["attn_added"], 4 * got[0] + got[1])
                    v.tensor_tensor(otmp[:].rearrange("p t (j d) -> p (t j) d", d=D), zo[:, :, 0:D],
                                    rden[:].unsqueeze(2).to_broadcast([P, T * G, D]), ALU.mult)\
                        .then_inc(s["sum_used"], 1)
                if t == 3 and n < B:
                    reach(eng, s["summed"], NG * (c - 1))
                    v.tensor_copy(va[par][:, :, :, 0:D], values(eng, c, par)).then_inc(s["valued"], 1)

            def pool_step(eng, c, par, t, n):
                if got := lagged(c, t, n, SCORE + 2, 2, H // 2):
                    cc, p, back = got
                    dst = qs[(par + back) % 2]
                    heads = slice(2 * p, 2 * p + 2)
                    part = [dst[:, :, heads, TOP + i] for i in range(3)]
                    eng.wait_ge(s["max_found"], 16 * cc + 2 * p + 2)
                    reach(eng, s["max_split"], 8 * cc + p)
                    pl.tensor_tensor(nmr[:], nm[:, :, heads], upper(nm)[:, :, heads], ALU.subtract)
                    pl.tensor_copy(part[0], upper(nm)[:, :, heads]).then_inc(s["split_chain"], 1)
                    eng.wait_ge(s["split_chain"], 8 * cc + p + 1)
                    pl.tensor_tensor(part[2], nmr[:], upper(nmr), ALU.subtract)
                    pl.tensor_copy(part[1], upper(nmr)).then_inc(s["max_split"], 1)

            return s, pe_step, act_step, dve_step, pool_step

        def terms_of(dst, terms):
            return dst.rearrange("p h (n d) -> p h n d", d=D)[:, :, terms[0]:terms[1]:terms[2], :]

        def part_of(dst, terms):
            return terms_of(dst, terms)[:, :, 0, :]

        def copies(ap, terms):
            return ap.unsqueeze(2).to_broadcast([P, H, len(range(*terms)), D])

        PARTS = {"k": (K_HI, K_MID, K_LO), "q": (Q_HI, Q_MID, Q_LO)}

        def split_hi(act, o, src, dst):
            a.activation(terms_of(dst, PARTS[o][0]), copies(src, PARTS[o][0]), ACT.Copy).then_inc(act.sem, 1)

        def split_rest(eng, act, pool, b, o, tt, src, dst):
            act.wait(eng, f"{o}{tt}_hi", b)
            reach(eng, pool.sem, pool.done(f"{o}{tt}_lo", b - 1))
            pl.tensor_tensor(rem[o, tt][:], src, part_of(dst, PARTS[o][0]), ALU.subtract).then_inc(pool.sem, 1)

        def split_mid(eng, dve, pool, b, o, tt, dst):
            pool.wait(eng, f"{o}{tt}_rest", b)
            v.tensor_copy(terms_of(dst, PARTS[o][1]), copies(rem[o, tt][:], PARTS[o][1])).then_inc(dve.sem, 1)

        def split_lo(eng, dve, pool, b, o, tt, dst):
            dve.wait(eng, f"{o}{tt}_mid", b)
            pl.tensor_tensor(part_of(dst, PARTS[o][2]), rem[o, tt][:], part_of(dst, PARTS[o][1]), ALU.subtract)\
                .then_inc(pool.sem, 1)

        def ln_stats(steps, eng, b, src, st, m, ve_):
            alone(eng)
            for tt in range(T):
                v.bn_stats(st[:, tt, :], src[tt]).then_inc(steps.sem, 1)
            for tt in range(T):
                steps.wait(eng, f"stats{tt}", b)
                alone(eng)
                v.bn_aggr(m[:, tt, :], st[:, tt, :]).then_inc(steps.sem, 1)
            steps.wait(eng, "aggr1", b)
            v.tensor_scalar(ve_[:], m[:, :, 1], EPS_LN, None, ALU.add).then_inc(steps.sem, 1)

        def ln_root(steps, eng, b, rooted, ve_, rs_):
            steps.wait(eng, "veps", b)
            pl.tensor_tensor(rs_[:], ve_[:], mhalf[:], ALU.pow).then_inc(rooted, 1)

        def ln_norm(steps, eng, b, rooted, src, m, rs_, dst):
            eng.wait_ge(rooted, b + 1)
            for tt in range(T):
                v.tensor_scalar(dst[tt], src[tt], m[:, tt, 0:1], rs_[:, tt:tt + 1], ALU.subtract, ALU.mult)\
                    .then_inc(steps.sem, 1)

        LN = "stats0 stats1 aggr0 aggr1 veps xn0 xn1"
        MB = bank[7]
        M_SELF, M_CROSS = 6, 3

        def turn4(dst, src):
            for i in range(2):
                for j in range(2):
                    ins = pe.transpose(dst(i, j), src(i, j), ident[:])
            return ins

        def rows_of(ap, tt):
            return ap.rearrange("p (t c) -> p t c", t=T)[:, tt, :]

        s, pe_core, act_core, dve_core, pool_core = core_of("self")
        m_full = sem("m_full")
        self_rooted = sem("self_rooted")
        SL = Steps(sem("self_ln"), LN)
        SD = Steps(sem("self_dve"), f"z0 elu0 z1 elu1 v k0_mid lep_before0 lep_before1 lep_after0 lep_after1 "
                                    "q0_mid lep_added k1_mid q1_mid")
        SA = Steps(sem("self_act"), "exp0 exp1 vT k0_hi lep_mid0 lep_mid1 q0_hi k1_hi q1_hi")
        SX = Steps(sem("self_xnT"), "xnT")
        SG = Steps(sem("self_pool"), "cos0 sin0 even0 odd0 cos1 k0_rest sin1 k0_lo even1 odd1 q0_rest k1_rest "
                                     "q0_lo q1_rest k1_lo q1_lo")
        LN_AT = (0, 1, 7)
        ROTATE = ((4, 5, 6), (7, 9, 11))
        SPLIT = {("k", 0): (7, 8, 9, 10), ("k", 1): (12, 13, 15, 15),
                 ("q", 0): (11, 12, 13, 14), ("q", 1): (13, 14, 15, 15)}
        STACK = {"k": (ks, slice(H, 2 * H)), "q": (qs, slice(0, H))}

        def self_ln_dve(eng, b, t):
            xr = xrow(b)
            if t == LN_AT[0] and isinstance(b, int) and b == SOON:
                eng.wait_ge(in_x[1], 16)
            if t == LN_AT[0]:
                ln_stats(SL, eng, b, [rows_of(xr, tt) for tt in range(T)], stats, mv, veps)
            if t == LN_AT[2]:
                reach(eng, m_full, M_SELF * (b - 1) + 1)
                ln_norm(SL, eng, b, self_rooted, [rows_of(xr, tt) for tt in range(T)], mv, rstd,
                        [xn[:, tt, :] for tt in range(T)])

        def self_ln_pool(eng, b, t):
            if t == LN_AT[1]:
                ln_root(SL, eng, b, self_rooted, veps, rstd)

        def self_dve(eng, b, par, t, prev):
            xr = xrow(b)
            for tt in range(T):
                if t == 2 + 2 * tt:
                    eng.wait_ge(m_full, M_SELF * b + 2 + tt)
                    if prev:
                        SG.wait(eng, f"sin{tt}", b - 1)
                    v.tensor_tensor(z[:, tt, :], MB[:], bq_sb[:, 0:2 * C], ALU.add).then_inc(SD.sem, 1)
                if t == 3 + 2 * tt:
                    SA.wait(eng, f"exp{tt}", b)
                    v.scalar_tensor_tensor(z[:, tt, :], ez[:, tt, :], 1.0, z[:, tt, :], ALU.min, ALU.max)\
                        .then_inc(SD.sem, 1)
            if t == 6:
                eng.wait_ge(m_full, M_SELF * b + 4)
                reach(eng, s["valued"], b)
                v.tensor_tensor(vtok[:], MB[:].rearrange("p (t c) -> p t c", t=T),
                                bq_sb[:, 2 * C:3 * C].unsqueeze(1).to_broadcast([P, T, C]), ALU.add)\
                    .then_inc(SD.sem, 1)
            for (o, tt), when in SPLIT.items():
                stack_, heads = STACK[o]
                if t == when[2]:
                    split_mid(eng, SD, SG, b, o, tt, stack_[par][:, tt, :, 0:DATA])
            if t == 11:
                for k in range(K2):
                    SA.wait(eng, f"lep_mid{k}", b)
                    v.scalar_tensor_tensor(lep[:, k, 1:N], vTs[:, k, 0:N - 1], wl_sb[:, k, 0:1],
                                           lep[:, k, 1:N], ALU.mult, ALU.add).then_inc(SD.sem, 1)
            if t == 12:
                for k in range(K2):
                    SD.wait(eng, f"lep_before{k}", b)
                    v.scalar_tensor_tensor(lep[:, k, 0:N - 1], vTs[:, k, 1:N], wl_sb[:, k, 2:3],
                                           lep[:, k, 0:N - 1], ALU.mult, ALU.add).then_inc(SD.sem, 1)
            if t == 14:
                eng.wait_ge(m_full, M_SELF * b + 6)
                v.tensor_tensor(xr, xr, MB[:], ALU.add).then_inc(SD.sem, 1)

        def self_values(eng, b, par):
            SD.wait(eng, "v", b)
            return vtok[:].rearrange("p t (h d) -> p t h d", d=D)

        def self_turn_act(eng, b, t):
            if t == 15:
                eng.wait_ge(m_full, M_SELF * b + 1)
                reach(eng, m_full, M_SELF * (b - 1) + 4)
                a.activation(xnT[:].rearrange("p k n -> p (k n)"), MB[:], ACT.Copy).then_inc(SX.sem, 1)

        def self_act(eng, b, par, t, prev):
            for tt in range(T):
                if t == 2 + 2 * tt:
                    SD.wait(eng, f"z{tt}", b)
                    a.activation(ez[:, tt, :], z[:, tt, :], ACT.Exp, bias=minus1[:]).then_inc(SA.sem, 1)
            if t == 7:
                eng.wait_ge(m_full, M_SELF * b + 5)
                if prev:
                    SD.wait(eng, "lep_after1", b - 1)
                a.activation(vTs[:].rearrange("p k n -> p (k n)"), MB[:], ACT.Copy).then_inc(SA.sem, 1)
            for (o, tt), when in SPLIT.items():
                stack_, heads = STACK[o]
                if t == when[0]:
                    reach(eng, s["kq_turned" if o == "k" else "q_turned"], 8 * (b - 1))
                    SG.wait(eng, f"odd{tt}", b)
                    split_hi(SA, o, r[tt][:, heads, :], stack_[par][:, tt, :, 0:DATA])
            if t == 9:
                SA.wait(eng, "vT", b)
                for k in range(K2):
                    a.activation(lep[:, k, :], vTs[:, k, :], ACT.Identity, scale=wl_sb[:, k, 1:2],
                                 bias=bl_sb[:, k:k + 1]).then_inc(SA.sem, 1)

        def self_turn_pe(eng, b, t):
            if t == 15:
                if not (isinstance(b, int) and b == 0):
                    SD.wait(eng, "lep_added", b - 1)
                SL.wait(eng, "xn1", b)
                turn4(lambda k, tt: MB[:, k * N + tt * P:k * N + (tt + 1) * P],
                      lambda k, tt: xn[:, tt, k * P:(k + 1) * P]).then_inc(m_full, 1)

        def self_pe(eng, b, par, t, prev):
            for tt in range(T):
                if t == 1 + 2 * tt:
                    SX.wait(eng, "xnT", b)
                    if tt:
                        SD.wait(eng, "z0", b)
                    for k in range(K2):
                        ins = pe.matmul(MB[:], xnT[:, k, tt * P:(tt + 1) * P], wq_sb[:, k, 0:2 * C],
                                        start=(k == 0), stop=(k == K2 - 1))
                    ins.then_inc(m_full, 1)
            if t == 5:
                SD.wait(eng, "z1", b)
                for tt in range(T):
                    for k in range(K2):
                        ins = pe.matmul(MB[:, tt * C:(tt + 1) * C], xnT[:, k, tt * P:(tt + 1) * P],
                                        wq_sb[:, k, 2 * C:3 * C], start=(k == 0), stop=(k == K2 - 1))
                ins.then_inc(m_full, 1)
            if t == 7:
                SD.wait(eng, "v", b)
                turn4(lambda k, tt: MB[:, k * N + tt * P:k * N + (tt + 1) * P],
                      lambda k, tt: vtok[:, tt, k * P:(k + 1) * P]).then_inc(m_full, 1)
            if t == 13:
                SD.wait(eng, "lep_after1", b)
                SA.wait(eng, "vT", b)
                turn4(lambda tt, k: MB[:, tt * C + k * P:tt * C + (k + 1) * P],
                      lambda tt, k: lep[:, k, tt * P:(tt + 1) * P]).then_inc(m_full, 1)

        def self_pool(eng, b, par, t, prev):
            for tt in range(T):
                pairs = z[:, tt, :].rearrange("p (h e two) -> p h two e", two=2, e=RH)
                for n, (tab, dst) in enumerate(((cos_sb, rc), (sin_sb, rs))):
                    if t == ROTATE[tt][n]:
                        if n == 0:
                            SD.wait(eng, f"elu{tt}", b)
                            reach(eng, SG.sem, SG.done(f"odd{1 - tt}", b - 1 + tt))
                        wide = tab[:, tt, :].unsqueeze(1).to_broadcast([P, 2 * H, RH])
                        for i in range(2):
                            ins = pl.tensor_tensor(dst[:, :, i, :], pairs[:, :, i, :], wide, ALU.mult)
                        ins.then_inc(SG.sem, 1)
                if t == ROTATE[tt][2]:
                    SG.wait(eng, f"sin{tt}", b)
                    reach(eng, SG.sem, SG.done(f"q{tt}_rest", b - 1))
                    pl.tensor_tensor(r[tt][:, :, 0:RH], rc[:, :, 0, :], rs[:, :, 1, :], ALU.subtract).then_inc(SG.sem, 1)
                    pl.tensor_tensor(r[tt][:, :, RH:D], rs[:, :, 0, :], rc[:, :, 1, :], ALU.add).then_inc(SG.sem, 1)
            for (o, tt), when in SPLIT.items():
                stack_, heads = STACK[o]
                if t == when[1]:
                    SG.wait(eng, f"odd{tt}", b)
                    split_rest(eng, SA, SG, b, o, tt, r[tt][:, heads, :], stack_[par][:, tt, :, 0:DATA])
                if t == when[3]:
                    split_lo(eng, SD, SG, b, o, tt, stack_[par][:, tt, :, 0:DATA])

        def sweep(eng, body, peeled, tails):
            for c in range(peeled):
                body(c, c % 2, c)
            with eng.Fori(peeled // 2, B // 2 - 1) as i:
                body(2 * i, 0, peeled)
                body(2 * i + 1, 1, peeled + 1)
            for c in range(B - 2, B + tails):
                body(c, c % 2, c)

        def run_self(eng, core, prep, norm, prep_first=False):
            def ready(b, par, t, n, prev):
                if n < B:
                    prep(eng, b, par, t, prev)
                if n < B - 1:
                    norm(eng, b + 1, t)

            for t in range(H):
                norm(eng, 0, t)
            for t in range(H):
                ready(0, 0, t, 0, False)

            def body(c, par, n):
                for t in range(H):
                    if prep_first:
                        ready(c + 1, 1 - par, t, n + 1, True)
                    core(c, par, t, n)
                    if not prep_first:
                        ready(c + 1, 1 - par, t, n + 1, True)
            sweep(eng, body, 2, 2)

        with nc.Block() as block:
            @block.sync
            def _(eng):
                eng.wait_ge(init_st, 48)

            @block.tensor
            def _(eng):
                run_self(eng, lambda c, par, t, n: pe_core(
                    eng, c, par, t, n, lambda e, cc: SG.wait(e, "q1_lo", cc)), self_pe, self_turn_pe)

            @block.scalar
            def _(eng):
                run_self(eng, lambda c, par, t, n: act_core(eng, c, par, t, n), self_act,
                         self_turn_act)

            @block.vector
            def _(eng):
                run_self(eng, lambda c, par, t, n: dve_core(eng, c, par, t, n, self_values), self_dve,
                         self_ln_dve)

            @block.gpsimd
            def _(eng):
                run_self(eng, lambda c, par, t, n: pool_core(eng, c, par, t, n), self_pool,
                         self_ln_pool, prep_first=True)

        own.close()
        cx = [osb(f"cx{i}", [P, T, 2 * C]) for i in range(2)]
        row = [osb(f"row{i}", [P, T, ROW]) for i in range(2)]
        stats3 = osb("stats3", [P, T, 6])
        mv3 = osb("mv3", [P, T, 2])
        rstd3 = osb("rstd3", [P, T])
        veps3 = osb("veps3", [P, T])
        x3T = [osb(f"x3T{i}", [P, K2, N]) for i in range(2)]
        nml = osb("nml", [P, T])
        eg = osb("eg", [P, T, E])
        esum = osb("esum", [P, T])
        ersum = osb("ersum", [P, T])
        gates = osb("gates", [P, T, E])
        top = osb("top", [P, T, TOPK])
        left = osb("left", [P, T, E])
        chosen = osb("chosen", [P, T, E], BF16)
        wsum = osb("wsum", [P, T])
        wsum2 = osb("wsum2", [P, T])
        wr = osb("wr", [P, T])
        vd = osb("vd", [P, T, E])
        sl = osb("sl", [P, T, E])
        val = osb("val", [P, T, E])
        topv = osb("topv", [P, T, TOPK])

        s2, pe_core2, act_core2, dve_core2, pool_core2 = core_of("cross")
        m2_full = sem("m2_full")
        cross_root, cross_rooted = sem("cross_root"), sem("cross_rooted")
        route_rooted = sem("route_rooted")
        CA = Steps(sem("cross_act"), "k0_hi k1_hi q0_hi q1_hi")
        CD = Steps(sem("cross_dve"), f"{LN} k0_mid k1_mid bias q0_mid q1_mid")
        CG = Steps(sem("cross_pool"), "k0_rest k0_lo k1_rest k1_lo q0_rest q1_rest q0_lo q1_lo")
        RD = Steps(sem("route_dve"), f"{LN} top_logit esum_inv gates top0 top1 left0 left1 chosen wsum wmax winv "
                                     "wpart weights before0 before1 fits slot val topv0 topv1 index late_index token late_token next")
        RA = Steps(sem("route_act"), "x3T exp0 exp1")
        in_ctx = [sem(f"in_ctx{i}") for i in range(2)]
        rows_st = [sem(f"rows_st{i}") for i in range(2)]
        x3t_st = [sem(f"x3t_st{i}") for i in range(2)]
        scattered = [sem(f"scattered{i}") for i in range(2)]

        def cross_dve(eng, b, par, t, prev):
            xr = xrow(b)
            if t == 0:
                ln_stats(CD, eng, b, [rows_of(xr, tt) for tt in range(T)], stats, mv, veps)
            if t == 2:
                if prev:
                    CG.wait(eng, "q1_rest", b - 1)
                ln_norm(CD, eng, b, cross_rooted, [rows_of(xr, tt) for tt in range(T)], mv, rstd,
                        [xn[:, tt, :] for tt in range(T)])
            for o, tt, src, dst in cross_parts(par):
                if t == CUT[o, tt][2]:
                    split_mid(eng, CD, CG, b, o, tt, dst)
            if t == 8:
                bias = bms[:].rearrange("p b t n -> p (b t n)")[:, bass.ds(b * (3 * T), 3 * T)]\
                    .rearrange("p (t n) -> p t n", t=T)
                v.tensor_copy(ks[par][:, :, :, BIAS:BIAS + 3], bias.unsqueeze(2).to_broadcast([P, T, H, 3]))\
                    .then_inc(CD.sem, 1)

        CUT = {("k", 0): (3, 4, 5, 6), ("k", 1): (5, 6, 7, 8), ("q", 0): (9, 10, 11, 12), ("q", 1): (10, 11, 12, 13)}

        def cross_parts(par):
            for o, whole, dst in (("k", cx[par], ks[par]), ("q", xn, qs[par])):
                for tt in range(T):
                    yield o, tt, whole[:, tt, 0:C].rearrange("p (h d) -> p h d", d=D), dst[:, tt, :, 0:DATA]

        def cross_act(eng, b, par, t, prev):
            for o, tt, src, dst in cross_parts(par):
                if t == CUT[o, tt][0]:
                    if o == "k" and tt == 0:
                        eng.wait_ge(in_ctx[par], ctx_count(b, par))
                    if o == "q":
                        CD.wait(eng, "xn1", b)
                    reach(eng, s2["kq_turned" if o == "k" else "q_turned"], 8 * (b - 1))
                    split_hi(CA, o, src, dst)

        def cross_pool(eng, b, par, t, prev):
            if t == 0:
                CD.wait(eng, "veps", b)
                pl.tensor_tensor(root[:], veps[:], mhalf[:], ALU.pow).then_inc(cross_root, 1)
            if t == 1:
                eng.wait_ge(cross_root, b + 1)
                alone(eng)
                pl.tensor_tensor(rstd[:], root[:], keyed[:, bass.ds(b, 1)].to_broadcast([P, T]), ALU.mult)\
                    .then_inc(cross_rooted, 1)
            for o, tt, src, dst in cross_parts(par):
                if t == CUT[o, tt][1]:
                    split_rest(eng, CA, CG, b, o, tt, src, dst)
                if t == CUT[o, tt][3]:
                    split_lo(eng, CD, CG, b, o, tt, dst)

        def cross_values(eng, b, par):
            eng.wait_ge(in_ctx[par], ctx_count(b, par))
            return cx[par][:, :, C:2 * C].rearrange("p t (h d) -> p t h d", d=D)

        def ctx_count(b, par):
            return (b - par) * 8 + 16

        def route_dve(eng, b, par, t, prev):
            xr, rw = xrow(b), row[par]

            def step(ins):
                ins.then_inc(RD.sem, 1)
            if t == 2:
                eng.wait_ge(s2["attn_added"], NG * b + NG)
                ln_stats(RD, eng, b, [rows_of(xr, tt) for tt in range(T)], stats3, mv3, veps3)
            if t == 3:
                reach(eng, rows_st[par], (b - par) * 8)
                ln_norm(RD, eng, b, route_rooted, [rows_of(xr, tt) for tt in range(T)], mv3, rstd3,
                        [rw[:, tt, 0:C] for tt in range(T)])
            if t == 7:
                eng.wait_ge(m2_full, M_CROSS * b + 2)
                step(v.tensor_reduce(nml[:], MB[:, 0:T * E].rearrange("p (t e) -> p t e", t=T), AX, ALU.max,
                                     negate=True))
            if t == 9:
                RA.wait(eng, "exp1", b)
                step(v.reciprocal(ersum[:], esum[:]))
                RD.wait(eng, "esum_inv", b)
                step(v.tensor_tensor(gates[:], eg[:], ersum[:].unsqueeze(2).to_broadcast([P, T, E]), ALU.mult))
                RD.wait(eng, "gates", b)
                alone(eng)
                for tt in range(T):
                    step(v.max(top[:, tt, :], gates[:, tt, :]))
                for tt in range(T):
                    RD.wait(eng, f"top{tt}", b)
                    alone(eng)
                    step(v.match_replace(left[:, tt, :], top[:, tt, :], gates[:, tt, :], -1.0))
            if t == 10:
                RD.wait(eng, "left1", b)
                step(v.tensor_scalar(chosen[:], left[:], 0.0, None, ALU.is_lt))
                step(v.tensor_reduce(wsum[:], top[:], AX, ALU.add))
                RD.wait(eng, "wsum", b)
                step(v.tensor_scalar(wsum2[:], wsum[:], EPS, None, ALU.max))
                RD.wait(eng, "wmax", b)
                step(v.reciprocal(wr[:], wsum2[:]))
                step(v.tensor_tensor(eg[:], gates[:], chosen[:], ALU.mult))
                RD.wait(eng, "wpart", b)
                step(v.tensor_tensor(rw[:, :, C:ROW], eg[:], wr[:].unsqueeze(2).to_broadcast([P, T, E]), ALU.mult))
            if t == 12:
                eng.wait_ge(m2_full, M_CROSS * b + 3)
                step(v.tensor_tensor(before[:], before[:], chosen[:, 0, :], ALU.add))
                RD.wait(eng, "before0", b)
                step(v.tensor_tensor(before[:], before[:], chosen[:, 1, :], ALU.add))
                rank = MB[:, 0:T * E].rearrange("p (t e) -> p t e", t=T)
                step(v.scalar_tensor_tensor(vd[:], rank, float(CAP), chosen[:], ALU.is_lt, ALU.mult))
                step(v.tensor_tensor(sl[:], ebase[:].unsqueeze(1).to_broadcast([P, T, E]), rank, ALU.subtract))
                RD.wait(eng, "slot", b)
                step(v.tensor_tensor(val[:], sl[:], vd[:], ALU.mult))
                RD.wait(eng, "val", b)
                alone(eng)
                for tt in range(T):
                    step(v.max(topv[:, tt, :], val[:, tt, :]))
            if t == 13:
                reach(eng, scattered[par], (b - par) * 8 * TOPK)
                RD.wait(eng, "topv1", b)
                step(v.tensor_scalar(sidx[par][:], topv[:, 0, :], -1.0, FAR, ALU.mult, ALU.add))
                step(v.tensor_scalar(late_idx[:, bass.ds(b * TOPK, TOPK)], topv[:, 1, :], -1.0, FAR, ALU.mult, ALU.add))
                step(v.tensor_copy(stok[par][:], tok_f[:, 0:1]))
                step(v.tensor_copy(late_tok[:, bass.ds(b, 1)], tok_f[:, 1:2]))
                RD.wait(eng, "late_token", b)
                step(v.tensor_scalar(tok_f[:], tok_f[:], float(N), None, ALU.add))

        def route_act(eng, b, par, t, prev):
            if t == 5:
                eng.wait_ge(m2_full, M_CROSS * b + 1)
                reach(eng, x3t_st[par], (b - par) * 8)
                a.activation(x3T[par][:].rearrange("p k n -> p (k n)"), MB[:], ACT.Copy).then_inc(RA.sem, 1)
            if t == 8:
                RD.wait(eng, "top_logit", b)
                for tt in range(T):
                    a.activation(eg[:, tt, :], MB[:, tt * E:(tt + 1) * E], ACT.Exp, bias=nml[:, tt:tt + 1],
                                 accum_out=esum[:, tt:tt + 1]).then_inc(RA.sem, 1)

        def route_pe(eng, b, par, t, prev):
            if t == 4:
                if prev:
                    RD.wait(eng, "slot", b - 1)
                RD.wait(eng, "xn1", b)
                turn4(lambda k, tt: MB[:, k * N + tt * P:k * N + (tt + 1) * P],
                      lambda k, tt: row[par][:, tt, k * P:(k + 1) * P]).then_inc(m2_full, 1)
            if t == 6:
                RA.wait(eng, "x3T", b)
                for tt in range(T):
                    for k in range(K2):
                        ins = pe.matmul(MB[:, tt * E:(tt + 1) * E], x3T[par][:, k, tt * P:(tt + 1) * P],
                                        wg_sb[:, k, :], start=(k == 0), stop=(k == K2 - 1))
                ins.then_inc(m2_full, 1)
            if t == 11:
                RD.wait(eng, "weights", b)
                RA.wait(eng, "exp1", b)
                if prev:
                    RD.wait(eng, "before1", b - 1)
                for tt in range(T):
                    out = MB[:, tt * E:(tt + 1) * E]
                    pe.matmul(out, onesb[:], before[:], start=True, stop=False)
                    if tt:
                        pe.matmul(out, onesb[:], chosen[:, 0, :], start=False, stop=False)
                    ins = pe.matmul(out, lower[:], chosen[:, tt, :], start=False, stop=True)
                ins.then_inc(m2_full, 1)

        def route_pool(eng, b, par, t, prev):
            if t == 2:
                ln_root(RD, eng, b, route_rooted, veps3, rstd3)

        def scatter(index, token, done):
            pl.indirect_dma_start(out=slot_tok, out_offset=bass.IndirectOffsetOnAxis(ap=index, axis=0), in_=token,
                                  in_offset=None, bounds_check=SLOTS - 1, oob_is_err=False).then_inc(done, 16)

        def scatter_pool(eng, b, par, t):
            if t == 0:
                RD.wait(eng, "token", b)
                alone(eng)
            if t % 2 == 1:
                scatter(sidx[par][:, t // 2:t // 2 + 1], stok[par][:], scattered[par])

        def run_cross(eng, core, prep=None, route=None, scatter=None):
            if prep:
                for t in range(H):
                    prep(eng, 0, 0, t, False)

            def body(c, par, n):
                for t in range(H):
                    if n < B + 2:
                        core(c, par, t, n)
                    if prep and n < B - 1:
                        prep(eng, c + 1, 1 - par, t, True)
                    if route and 2 <= n < B + 2:
                        route(eng, c - 2, par, t, n > 2)
                    if scatter and n >= 3:
                        scatter(eng, c - 3, 1 - par, t)
            sweep(eng, body, 4, 2)

        with nc.Block() as block:
            @block.sync
            def _(eng):
                def load(b, par, prev):
                    if prev:
                        eng.wait_ge(s2["valued"], b - 1)
                        CG.wait(eng, "k1_rest", b - 2)
                    eng.dma_start(cx[par][:], ctx_rows(b)).then_inc(in_ctx[par], 16)

                def ctx_rows(b):
                    return ctx_in[bass.ds(b, 1), :, :].rearrange("o (t p) c -> p (o t) c", p=P)

                def store(b, par):
                    RD.wait(eng, "weights", b)
                    eng.dma_start(rows[bass.ds(b * N, N), :].rearrange("(t p) c -> p t c", p=P), row[par][:])\
                        .then_inc(rows_st[par], 16)
                    RA.wait(eng, "x3T", b)
                    alone(eng)
                    eng.dma_start(xt_dram[:, :, bass.ds(b * N, N)], x3T[par][:]).then_inc(x3t_st[par], 16)

                load(0, 0, False)
                load(1, 1, False)

                def body(c, par, n):
                    if n < B - 2:
                        load(c + 2, par, True)
                    if n == B:
                        for q in range(2):
                            eng.wait_ge(x3t_st[q], 8 * (B - 2))
                        for q in range(2):
                            eng.dma_start(xc[q][:], xt_dram[:, :, q * CH:(q + 1) * CH]).then_inc(in_xc[q], 16)
                    if 2 <= n < B + 2:
                        store(c - 2, par)
                sweep(eng, body, 4, 2)
                for par in range(2):
                    eng.wait_ge(rows_st[par], 8 * B)
                    eng.wait_ge(x3t_st[par], 8 * B)

            @block.tensor
            def _(eng):
                run_cross(eng, lambda c, par, t, n: pe_core2(
                    eng, c, par, t, n, lambda e, cc: CG.wait(e, "q1_lo", cc)), None, route_pe)

            @block.scalar
            def _(eng):
                run_cross(eng, lambda c, par, t, n: act_core2(eng, c, par, t, n), cross_act, route_act)

            @block.vector
            def _(eng):
                run_cross(eng, lambda c, par, t, n: dve_core2(eng, c, par, t, n, cross_values),
                          cross_dve, route_dve)

            @block.gpsimd
            def _(eng):
                run_cross(eng, lambda c, par, t, n: pool_core2(eng, c, par, t, n),
                          cross_pool, route_pool, scatter_pool)

        own.close()
        attn.close()

        ffn = ExitStack()
        fsb = lambda name, shape, dt=F32: sb(name, shape, dt, ffn)
        w1, w2 = expert_weights(SHARED)
        sg = [fsb(f"sg{i}", [P, CH]) for i in range(2)]
        gf = [fsb(f"gf{i}", [P, CH]) for i in range(2)]
        HI, LO = range(2)
        PASSES = ((HI, HI), (HI, LO), (LO, HI))
        xs = [[fsb(f"xs{i}_{p}", [P, K2, CH], F32R) for p in range(2)] for i in range(2)]
        gs = [[fsb(f"gs{i}_{p}", [P, FT, CH], F32R) for p in range(2)] for i in range(2)]
        w1s = [fsb(f"w1s{p}", [P, K2, 2 * FF], F32R) for p in range(2)]
        w2s = [fsb(f"w2s{p}", [P, FT, C], F32R) for p in range(2)]
        ys = [fsb(f"ys{i}", [P, CH // P * C]) for i in range(2)]
        hid = sem("hid")
        acted = sem("acted")
        gated = sem("gated")
        w_split = sem("w_split")
        x_hi, x_lo, g_hi, g_lo = (sem(n) for n in ("x_hi", "x_lo", "g_hi", "g_lo"))
        outed = sem("outed")
        y_made = sem("y_made")
        y_st = [sem(f"y_st{i}") for i in range(2)]
        NCH = NTOK // CH
        W_SPLITS = 2 * 2 * FT

        def tile_of(w, j):
            return w[:].rearrange("p k (half f) -> p (k half) f", half=2)[:, :, j * P:(j + 1) * P]

        late_now = [fsb(f"late_now{i}", [P, TOPK], U32) for i in range(2)]
        late_row = [fsb(f"late_row{i}", [P, 1], I32) for i in range(2)]
        taken = sem("taken")
        late = [sem(f"late{i}") for i in range(2)]

        with nc.Block() as block:
            @block.gpsimd
            def _(eng):
                def body(b, par):
                    reach(eng, late[par], (b - par) * 8 * TOPK)
                    alone(eng)
                    pl.tensor_copy(late_now[par][:], late_idx[:, bass.ds(b * TOPK, TOPK)]).then_inc(taken, 1)
                    pl.tensor_copy(late_row[par][:], late_tok[:, bass.ds(b, 1)]).then_inc(taken, 1)
                    eng.wait_ge(taken, 2 * b + 2)
                    alone(eng)
                    for j in range(TOPK):
                        scatter(late_now[par][:, j:j + 1], late_row[par][:], late[par])
                for j in range(TOPK):
                    scatter(sidx[(B - 1) % 2][:, j:j + 1], stok[(B - 1) % 2][:], scattered[(B - 1) % 2])
                body(0, 0)
                body(1, 1)
                with eng.Fori(1, B // 2) as i:
                    body(2 * i, 0)
                    body(2 * i + 1, 1)
                for par in range(2):
                    eng.wait_ge(scattered[par], 8 * B * TOPK)
                    eng.wait_ge(late[par], 8 * B * TOPK)

            def chunks(eng, body):
                body(0, 0, False)
                body(1, 1, True)
                with eng.Fori(1, NCH // 2 - 1) as i:
                    body(2 * i, 0, True)
                    body(2 * i + 1, 1, True)
                body(NCH - 2, 0, True)
                body(NCH - 1, 1, True)

            @block.sync
            def _(eng):
                def load(q, par):
                    reach(eng, x_lo, q - 1)
                    eng.dma_start(xc[par][:], xt_dram[:, :, bass.ds(q * CH, CH)]).then_inc(in_xc[par], 16)

                def store(q, par):
                    eng.wait_ge(y_made, 2 * q + 2)
                    eng.dma_start(y[bass.ds(q * CH, CH), :].rearrange("(t p) c -> p t c", p=P),
                                  ys[par][:].rearrange("p (t c) -> p t c", c=C)).then_inc(y_st[par], 16)

                with eng.Fori(1, NCH // 2) as i:
                    load(2 * i, 0)
                    store(2 * i - 2, 0)
                    load(2 * i + 1, 1)
                    store(2 * i - 1, 1)
                store(NCH - 2, 0)
                store(NCH - 1, 1)
                for par in range(2):
                    eng.wait_ge(y_st[par], 8 * NCH)

            @block.tensor
            def _(eng):
                def hidden(q, par, js):
                    for j in js:
                        reach(eng, w_split, 2 * j + 2)
                        reach(eng, gated, FT * q + j - 1)
                        for half in range(2):
                            f = half * FF + j * P
                            for k in range(K2):
                                for n, (a_, b_) in enumerate(PASSES):
                                    ins = pe.matmul(bank[2 * (j % 2) + half][:], w1s[a_][:, k, f:f + P],
                                                    xs[par][b_][:, k, :], start=(k == 0 and n == 0),
                                                    stop=(k == K2 - 1 and n == len(PASSES) - 1))
                        ins.then_inc(hid, 1)

                def output(q, par):
                    eng.wait_ge(w_split, W_SPLITS)
                    eng.wait_ge(g_lo, FT * q + FT)
                    reach(eng, y_made, 2 * (q - 1))
                    for tt in range(CH // P):
                        out = bank[4 + 2 * par + tt // 2][:, tt % 2 * C:(tt % 2 + 1) * C]
                        for j in range(FT):
                            for n, (a_, b_) in enumerate(PASSES):
                                ins = pe.matmul(out, gs[par][a_][:, j, tt * P:(tt + 1) * P], w2s[b_][:, j, :],
                                                start=(j == 0 and n == 0),
                                                stop=(j == FT - 1 and n == len(PASSES) - 1))
                        if tt % 2:
                            ins.then_inc(outed, 1)

                def body(q, par, prev):
                    eng.wait_ge(x_lo, q + 1)
                    hidden(q, par, range(2))
                    if prev:
                        output(q - 1, 1 - par)
                    hidden(q, par, range(2, FT))
                chunks(eng, body)
                output(NCH - 1, 1)

            @block.scalar
            def _(eng):
                def split_x(q, par):
                    eng.wait_ge(in_xc[par], (q - par) * 8 + 16)
                    reach(eng, hid, FT * (q - 1))
                    a.activation(xs[par][HI][:], xc[par][:], ACT.Copy).then_inc(x_hi, 1)

                def body(q, par, prev):
                    for j in range(FT):
                        eng.wait_ge(hid, FT * q + j + 1)
                        reach(eng, gated, FT * q + j - 1)
                        a.activation(sg[j % 2][:], bank[2 * (j % 2) + 1][:], ACT.Silu).then_inc(acted, 1)
                        if j == 2 and not (isinstance(q, int) and q == NCH - 1):
                            split_x(q + 1, 1 - par)
                        eng.wait_ge(gated, FT * q + j + 1)
                        reach(eng, outed, 2 * (q - 1))
                        a.activation(gs[par][HI][:, j, :], gf[j % 2][:], ACT.Copy).then_inc(g_hi, 1)

                split_x(0, 0)
                chunks(eng, body)

            @block.vector
            def _(eng):
                def finish(q, par):
                    reach(eng, y_st[par], (q - par) * 8)
                    for i in range(2):
                        eng.wait_ge(outed, 2 * q + i + 1)
                        v.tensor_tensor(ys[par][:, i * 2 * C:(i + 1) * 2 * C], bank[4 + 2 * par + i][:],
                                        X[:, bass.ds(q * (CH // P * C) + i * 2 * C, 2 * C)], ALU.add)\
                            .then_inc(y_made, 1)

                def split_x(q, par):
                    eng.wait_ge(x_hi, q + 1)
                    v.tensor_tensor(xs[par][LO][:], xc[par][:], xs[par][HI][:].bitcast(F32), ALU.subtract)\
                        .then_inc(x_lo, 1)

                def split_w(whole, parts, n):
                    v.tensor_copy(parts[HI], whole).then_inc(w_split, 1)
                    eng.wait_ge(w_split, 2 * n + 1)
                    v.tensor_tensor(parts[LO], whole, parts[HI].bitcast(F32), ALU.subtract).then_inc(w_split, 1)

                def rest(q, par, j):
                    eng.wait_ge(g_hi, FT * q + j + 1)
                    v.tensor_tensor(gs[par][LO][:, j, :], gf[j % 2][:], gs[par][HI][:, j, :].bitcast(F32),
                                    ALU.subtract).then_inc(g_lo, 1)

                def body(q, par, prev):
                    for j in range(FT):
                        eng.wait_ge(acted, FT * q + j + 1)
                        reach(eng, g_lo, FT * q + j - 1)
                        v.tensor_tensor(gf[j % 2][:], bank[2 * (j % 2)][:], sg[j % 2][:], ALU.mult)\
                            .then_inc(gated, 1)
                        if j >= 1:
                            rest(q, par, j - 1)
                        if j == 2 and prev:
                            finish(q - 1, 1 - par)
                        if j == 3 and not (isinstance(q, int) and q == NCH - 1):
                            split_x(q + 1, 1 - par)
                    rest(q, par, FT - 1)
                    if not prev:
                        for j in range(FT):
                            split_w(w2[:, j, :], [w[:, j, :] for w in w2s], FT + j)
                split_x(0, 0)
                eng.wait_ge(in_sw, 16)
                for j in range(FT):
                    split_w(tile_of(w1, j), [tile_of(w, j) for w in w1s], j)
                chunks(eng, body)
                finish(NCH - 1, 1)

        ffn.close()
        ffn = ExitStack()

        RING = 4
        idx = [fsb(f"idx{i}", [HC, 2], I32) for i in range(RING)]
        xg = [fsb(f"xg{i}", [HC, 2, ROW]) for i in range(RING)]
        xgT = [fsb(f"xgT{i}", [P, K2, CAP]) for i in range(2)]
        sge = [fsb(f"sge{i}", [P, FT // 2 * CAP]) for i in range(2)]
        gTe = [fsb(f"gTe{i}", [P, FT * CAP]) for i in range(2)]
        oTe = [fsb(f"oTe{i}", [P, K2 * CAP]) for i in range(2)]
        yse = [fsb(f"yse{i}", [HC, 2, C]) for i in range(2)]
        in_idx = [sem(f"in_idx{i}") for i in range(RING)]
        fetched = [sem(f"fetched{i}") for i in range(RING)]
        added = [sem(f"added{i}") for i in range(2)]
        e_turned, e_copied, e_hid, e_acted, e_gated, e_out, e_summed, e_back, e_scaled = (sem(n) for n in (
            "e_turned", "e_copied", "e_hid", "e_acted", "e_gated", "e_out", "e_summed", "e_back", "e_scaled"))
        HALF = FT // 2 * CAP

        with nc.Block() as block:
            def experts(eng, body):
                for e in range(RING):
                    body(e, e, e)
                with eng.Fori(1, E // RING - 1) as i:
                    for k in range(RING):
                        body(RING * i + k, k, RING + k)
                for e in range(E - RING, E):
                    body(e, e % RING, e)

            def uses(e, k):
                return (e - k) * (16 // RING) + 16

            @block.sync
            def _(eng):
                names = slot_tok.rearrange("(e p c) o -> e p (c o)", c=2, p=HC)

                def load_idx(e, k):
                    reach(eng, added[k % 2], (e - k % 2) * 16 - 16 * RING + 32)
                    eng.dma_start(idx[k][:], names[bass.ds(e, 1), :, :].rearrange("o p c -> p (o c)"))\
                        .then_inc(in_idx[k], 16)

                def body(e, k, n):
                    if n >= 1:
                        reach(eng, e_out, e - 1)
                        eng.dma_start(ew_sb[k % 2][:], ew[bass.ds(e, 1), :, :].rearrange("o p n -> p (o n)"))\
                            .then_inc(loaded_ew[k % 2], 16)
                    if n < E - 2:
                        load_idx(e + 2, (k + 2) % RING)
                load_idx(0, 0)
                load_idx(1, 1)
                experts(eng, body)

            @block.gpsimd
            def _(eng):
                def fetch(e, k):
                    eng.wait_ge(in_idx[k], uses(e, k))
                    reach(eng, e_scaled, e - RING + 1)
                    alone(eng)
                    for c in range(2):
                        pl.indirect_dma_start(out=xg[k][:, c, :], out_offset=None, in_=rows,
                                              in_offset=bass.IndirectOffsetOnAxis(ap=idx[k][:, c:c + 1].bitcast(U32), axis=0))\
                            .then_inc(fetched[k], 16)

                def body(e, k, n):
                    par = k % 2
                    if n < E - 2:
                        fetch(e + 2, (k + 2) % RING)
                    eng.wait_ge(e_scaled, e + 1)
                    if n >= 1:
                        eng.wait_ge(added[1 - par], (e + par) * 16)
                    alone(eng)
                    for c in range(2):
                        pl.indirect_dma_start(out=y, out_offset=bass.IndirectOffsetOnAxis(ap=idx[k][:, c:c + 1].bitcast(U32), axis=0),
                                              in_=yse[par][:, c, :], in_offset=None, compute_op=ALU.add)\
                            .then_inc(added[par], 16)
                fetch(0, 0)
                fetch(1, 1)
                experts(eng, body)
                for par in range(2):
                    eng.wait_ge(added[par], 16 * E)

            @block.tensor
            def _(eng):
                TB = bank[4]

                def turn(e, k4):
                    eng.wait_ge(fetched[k4], 2 * uses(e, k4))
                    reach(eng, e_copied, e)
                    for k in range(K2):
                        for c in range(2):
                            ins = pe.transpose(TB[:, k * CAP + c * HC:k * CAP + (c + 1) * HC],
                                               xg[k4][:, c, k * P:(k + 1) * P], ident[0:HC, 0:HC])
                    ins.then_inc(e_turned, 1)

                def turn_back(e, par):
                    eng.wait_ge(e_summed, e + 1)
                    reach(eng, e_scaled, e)
                    for c in range(2):
                        for k in range(K2):
                            ins = pe.transpose(bank[7][0:HC, c * C + k * P:c * C + (k + 1) * P],
                                               oTe[par][:, k * CAP + c * HC:k * CAP + (c + 1) * HC], ident[:])
                    ins.then_inc(e_back, 1)

                def body(e, k4, n):
                    par = k4 % 2
                    wa, wb = expert_weights(par)
                    eng.wait_ge(loaded_ew[par], (e - par) * 8 + 16)
                    eng.wait_ge(e_copied, e + 1)
                    for half in range(2):
                        reach(eng, e_gated, 2 * e + half - 1)
                        for side in range(2):
                            for j in range(FT // 2):
                                f = side * FF + (half * (FT // 2) + j) * P
                                for k in range(K2):
                                    ins = pe.matmul(bank[2 * half + side][:, j * CAP:(j + 1) * CAP],
                                                    wa[:, k, f:f + P], xgT[par][:, k, :],
                                                    start=(k == 0), stop=(k == K2 - 1))
                        ins.then_inc(e_hid, 1)
                        if half == 0 and n >= 1:
                            turn_back(e - 1, 1 - par)
                    if n < E - 1:
                        turn(e + 1, (k4 + 1) % RING)
                    reach(eng, e_summed, e)
                    for half in range(2):
                        eng.wait_ge(e_gated, 2 * e + half + 1)
                        for c in range(K2):
                            for j in range(half * (FT // 2), (half + 1) * (FT // 2)):
                                ins = pe.matmul(bank[5 + c][:, 0:CAP], wb[:, j, c * P:(c + 1) * P],
                                                gTe[par][:, j * CAP:(j + 1) * CAP],
                                                start=(j == 0), stop=(j == FT - 1))
                    ins.then_inc(e_out, 1)
                turn(0, 0)
                experts(eng, body)
                turn_back(E - 1, 1)

            @block.scalar
            def _(eng):
                def copy(e, par):
                    eng.wait_ge(e_turned, e + 1)
                    reach(eng, e_hid, 2 * (e - 1))
                    a.activation(xgT[par][:].rearrange("p k n -> p (k n)"), bank[4][:, 0:K2 * CAP], ACT.Copy)\
                        .then_inc(e_copied, 1)

                def copy_sums(e, par):
                    eng.wait_ge(e_out, e + 1)
                    reach(eng, e_back, e - 1)
                    for c in range(K2):
                        ins = a.activation(oTe[par][:, c * CAP:(c + 1) * CAP], bank[5 + c][:, 0:CAP], ACT.Copy)
                    ins.then_inc(e_summed, 1)

                def body(e, k4, n):
                    par = k4 % 2
                    if n >= 1:
                        copy_sums(e - 1, 1 - par)
                    for half in range(2):
                        eng.wait_ge(e_hid, 2 * e + half + 1)
                        reach(eng, e_gated, 2 * e + half - 1)
                        a.activation(sge[half][:], bank[2 * half + 1][:, 0:HALF], ACT.Silu).then_inc(e_acted, 1)
                    if n < E - 1:
                        copy(e + 1, 1 - par)
                copy(0, 0)
                experts(eng, body)
                copy_sums(E - 1, 1)

            @block.vector
            def _(eng):
                def weigh(e, k4):
                    eng.wait_ge(e_back, e + 1)
                    reach(eng, added[k4 % 2], (e - k4 % 2) * 16)
                    for c in range(2):
                        ins = v.tensor_scalar(yse[k4 % 2][:, c, :], bank[7][0:HC, c * C:(c + 1) * C],
                                              xg[k4][:, c, bass.ds(e + C, 1)], None, ALU.mult)
                    ins.then_inc(e_scaled, 1)

                def body(e, k4, n):
                    par = k4 % 2
                    for half in range(2):
                        eng.wait_ge(e_acted, 2 * e + half + 1)
                        reach(eng, e_out, e - 1)
                        v.tensor_tensor(gTe[par][:, half * HALF:(half + 1) * HALF], bank[2 * half][:, 0:HALF],
                                        sge[half][:], ALU.mult).then_inc(e_gated, 1)
                        if half == 0 and n >= 1:
                            weigh(e - 1, (k4 - 1) % RING)
                experts(eng, body)
                weigh(E - 1, (E - 1) % RING)
        ffn.close()


_INPUTS = ["x", "ctx_2048", "itok_Bx1_68_817", "w_qkv", "b_qkv", "w_lepe", "b_lepe", "xb", "wg", "sw",
           "ew", "cos_t", "sin_t"]


def rope_tables():
    position = np.arange(N, dtype=np.float32)[:, None]
    rate = np.exp(np.arange(0, D, 2, dtype=np.float32) * np.float32(-np.log(10000.0) / D))
    angle = position * rate.astype(np.float32)
    return np.cos(angle), np.sin(angle)


def kernel(**inputs):
    import concourse.bacc as bacc
    from concourse.bass_utils import run_bass_kernel_spmd

    g = {k: np.asarray(v) for k, v in inputs.items()}
    cos_t, sin_t = rope_tables()
    def packed(w1, w2):
        n = w1.shape[0]
        first = w1.transpose(0, 2, 1).reshape(n, K2, P, 2 * FF).transpose(0, 2, 1, 3).reshape(n, P, -1)
        second = w2.transpose(0, 2, 1).reshape(n, FT, P, C).transpose(0, 2, 1, 3).reshape(n, P, -1)
        return np.concatenate([first, second], axis=2)

    arrays = {
        "x": g["x"], "ctx_2048": g["ctx_2048"], "itok_Bx1_68_817": g["itok_Bx1_68_817"],
        "w_qkv": g["L0_attn_w_qkv"].T, "b_qkv": g["L0_attn_b_qkv"],
        "w_lepe": g["L0_attn_w_lepe"].reshape(C, 3), "b_lepe": g["L0_attn_b_lepe"].reshape(K2, P).T,
        "xb": g["L0_xattn_b"].reshape(T, P).T,
        "wg": g["L0_ffn_wg"].T, "sw": packed(g["L0_ffn_shared_w1"][None], g["L0_ffn_shared_w2"][None])[0],
        "ew": packed(g["L0_ffn_expert_w1"], g["L0_ffn_expert_w2"]),
        "cos_t": cos_t, "sin_t": sin_t,
    }
    nc = bacc.Bacc("TRN2", target_bir_lowering=False, num_devices=1)
    args, sent = [], {}
    for name in _INPUTS:
        sent[f"in_{name}"] = np.ascontiguousarray(arrays[name])
        args.append(nc.dram_tensor(f"in_{name}", sent[f"in_{name}"].shape, mybir.dt.from_np(sent[f"in_{name}"].dtype),
                                   kind="ExternalInput").ap())
    args.append(nc.dram_tensor("out", (ROWS, C), F32, kind="ExternalOutput").ap())
    decoder_layer(nc, *args)
    result = run_bass_kernel_spmd(nc, [sent], core_ids=[0])
    return result.results[0]["out"][:NTOK].reshape(B, N, C)
```
